# Optimizing a Trainium2 kernel written in Bass

```python
import numpy as np
import jax
import jax.numpy as jnp

def _softmax(x, axis=-1):
    return jax.nn.softmax(x, axis=axis)

def _gelu(x):
    return jax.nn.gelu(x, approximate=True)

def _silu(x):
    return jax.nn.silu(x)

def _sigmoid(x):
    return jax.nn.sigmoid(x)

def _layernorm(x, axis=-1, eps=1e-05):
    m = jnp.mean(x, axis=axis, keepdims=True)
    v = jnp.var(x, axis=axis, keepdims=True)
    return (x - m) / jnp.sqrt(v + eps)

def _scatter_add(tgt, idx, src, axis=0):
    return tgt.at[idx].add(src)

def _segment_sum(src, seg, n):
    return jax.ops.segment_sum(src, seg, n)
kernel_name = 'mk_early_fusion_d2_tok_img1024_r4_c97f48'

def setup_inputs(seed: int=0):
    np.random.seed(seed)
    _w = jnp.asarray

    def _rec_inputs():
        import jax
        import jax.numpy as jnp
        _rk = jax.random.key(seed)
        x = 7.22013e-05 + 1.00017 * jax.random.normal(jax.random.fold_in(_rk, 1), (4, 1, 512, 256), jnp.float32)
        txt = 1.55315e-05 + 0.0209517 * jax.random.normal(jax.random.fold_in(_rk, 2), (4, 77, 256), jnp.float32)
        return (x, txt)
    x, txt = _rec_inputs()

    def _L0_tok_setup():
        import jax, jax.numpy as jnp
        import numpy as np
        import math
        EMBED_DIM = 256
        NUM_HEADS = 16
        HEAD_DIM = EMBED_DIM // NUM_HEADS
        INPUT_DIM = 256
        key = jax.random.key(seed)
        k_x, k_wqkv, k_wout = jax.random.split(key, 3)
        x = jax.random.normal(k_x, (4, 1, 512, INPUT_DIM), dtype=jnp.float32)

        def xavier(k, shape):
            fan_out, fan_in = shape
            bound = math.sqrt(6.0 / (fan_in + fan_out))
            return jax.random.uniform(k, shape, jnp.float32, -bound, bound)
        w_qkv = xavier(k_wqkv, (3 * EMBED_DIM, INPUT_DIM))
        b_qkv = jnp.zeros((3 * EMBED_DIM,), jnp.float32)
        w_out = xavier(k_wout, (EMBED_DIM, EMBED_DIM))
        b_out = jnp.zeros((EMBED_DIM,), jnp.float32)
        return {'x': x, 'w_qkv': w_qkv, 'b_qkv': b_qkv, 'w_out': w_out, 'b_out': b_out}
    _L0_tok_all = _L0_tok_setup()
    _L0_tok_in = {k: v for k, v in _L0_tok_all.items() if k in ('w_qkv', 'b_qkv', 'w_out', 'b_out')}
    del _L0_tok_all

    def _L0_attn_setup():
        import jax, jax.numpy as jnp
        import numpy as np
        import math
        D_MODEL = 256
        D_STATE = 16
        DT_RANK = 64
        BATCH = 4
        SEQLEN = 512
        key = jax.random.key(seed)
        ks = jax.random.split(key, 4)
        u = jax.random.normal(ks[0], (BATCH, SEQLEN, D_MODEL), dtype=jnp.float32)
        A = jnp.tile(jnp.arange(1, D_STATE + 1, dtype=jnp.float32)[None, :], (D_MODEL, 1))
        A_log = jnp.log(A)
        D_skip = jnp.ones((D_MODEL,), dtype=jnp.float32)
        dt_init_std = DT_RANK ** (-0.5)
        dt_proj_w = jax.random.uniform(ks[1], (D_MODEL, DT_RANK), dtype=jnp.float32, minval=-dt_init_std, maxval=dt_init_std)
        dt_proj_b = jnp.zeros((D_MODEL,), dtype=jnp.float32)
        x_proj_w = jax.random.normal(ks[2], (DT_RANK + 2 * D_STATE, D_MODEL), dtype=jnp.float32) * D_MODEL ** (-0.5)
        return {'u': u, 'A_log': A_log, 'D_skip': D_skip, 'dt_proj_w': dt_proj_w, 'dt_proj_b': dt_proj_b, 'x_proj_w': x_proj_w}
    _L0_attn_all = _L0_attn_setup()
    _L0_attn_in = {k: v for k, v in _L0_attn_all.items() if k in ('A_log', 'D_skip', 'dt_proj_w', 'dt_proj_b', 'x_proj_w')}
    del _L0_attn_all

    def _L0_ffn_setup():
        import jax, jax.numpy as jnp
        import numpy as np
        B, S, D, E, F = (2, 512, 256, 14, 512)
        key = jax.random.key(seed)
        k = jax.random.split(key, 4)
        h = jax.random.normal(k[0], (B, S, D), dtype=jnp.float32)
        router_w = jax.random.normal(k[1], (D, E), dtype=jnp.float32) * 0.02
        w1 = jax.random.uniform(k[2], (E, D, F), dtype=jnp.float32, minval=-1.0, maxval=1.0) * float(np.sqrt(6.0 / D))
        w2 = jax.random.uniform(k[3], (E, F, D), dtype=jnp.float32, minval=-1.0, maxval=1.0) * float(np.sqrt(6.0 / F))
        b1 = jnp.zeros((E, F), dtype=jnp.float32)
        b2 = jnp.zeros((E, D), dtype=jnp.float32)
        return {'h': h, 'router_w': router_w, 'w1': w1, 'b1': b1, 'w2': w2, 'b2': b2}
    _L0_ffn_all = _L0_ffn_setup()
    _L0_ffn_in = {k: v for k, v in _L0_ffn_all.items() if k in ('router_w', 'w1', 'b1', 'w2', 'b2')}
    del _L0_ffn_all

    def _L1_attn_setup():
        import jax, jax.numpy as jnp
        import numpy as np
        D = 256
        key = jax.random.key(seed)
        ks = jax.random.split(key, 7)
        s = 1.0 / np.sqrt(D)
        X = jax.random.normal(ks[0], (4, 512, D), dtype=jnp.float32)
        Wq = jax.random.uniform(ks[1], (D, D), jnp.float32, -s, s)
        Wk = jax.random.uniform(ks[2], (D, D), jnp.float32, -s, s)
        Wv = jax.random.uniform(ks[3], (D, D), jnp.float32, -s, s)
        bq = jax.random.uniform(ks[4], (D,), jnp.float32, -s, s)
        bk = jax.random.uniform(ks[5], (D,), jnp.float32, -s, s)
        bv = jax.random.uniform(ks[6], (D,), jnp.float32, -s, s)
        return {'X': X, 'Wq': Wq, 'bq': bq, 'Wk': Wk, 'bk': bk, 'Wv': Wv, 'bv': bv}
    _L1_attn_all = _L1_attn_setup()
    _L1_attn_in = {k: v for k, v in _L1_attn_all.items() if k in ('Wq', 'bq', 'Wk', 'bk', 'Wv', 'bv')}
    del _L1_attn_all

    def _L1_ffn_setup():
        import jax, jax.numpy as jnp
        import numpy as np
        E = 128
        D = 256
        C = 64
        key = jax.random.key(seed)
        kx, kg, ke = jax.random.split(key, 3)
        x = jax.random.normal(kx, (4, 512, D), dtype=jnp.float32)
        wg = jax.random.normal(kg, (D, E), dtype=jnp.float32) * 0.02
        we = jax.random.normal(ke, (E, D, D), dtype=jnp.float32) * 0.02
        return {'x': x, 'wg': wg, 'we': we}
    _L1_ffn_all = _L1_ffn_setup()
    _L1_ffn_in = {k: v for k, v in _L1_ffn_all.items() if k in ('wg', 'we')}
    del _L1_ffn_all
    return {'x': x, 'txt': txt, 'L0_tok_w_qkv': _L0_tok_in['w_qkv'], 'L0_tok_b_qkv': _L0_tok_in['b_qkv'], 'L0_tok_w_out': _L0_tok_in['w_out'], 'L0_tok_b_out': _L0_tok_in['b_out'], 'L0_attn_A_log': _L0_attn_in['A_log'], 'L0_attn_D_skip': _L0_attn_in['D_skip'], 'L0_attn_dt_proj_w': _L0_attn_in['dt_proj_w'], 'L0_attn_dt_proj_b': _L0_attn_in['dt_proj_b'], 'L0_attn_x_proj_w': _L0_attn_in['x_proj_w'], 'L0_ffn_router_w': _L0_ffn_in['router_w'], 'L0_ffn_w1': _L0_ffn_in['w1'], 'L0_ffn_b1': _L0_ffn_in['b1'], 'L0_ffn_w2': _L0_ffn_in['w2'], 'L0_ffn_b2': _L0_ffn_in['b2'], 'L1_attn_Wq': _L1_attn_in['Wq'], 'L1_attn_bq': _L1_attn_in['bq'], 'L1_attn_Wk': _L1_attn_in['Wk'], 'L1_attn_bk': _L1_attn_in['bk'], 'L1_attn_Wv': _L1_attn_in['Wv'], 'L1_attn_bv': _L1_attn_in['bv'], 'L1_ffn_wg': _L1_ffn_in['wg'], 'L1_ffn_we': _L1_ffn_in['we']}

def reference(x, txt, L0_tok_w_qkv, L0_tok_b_qkv, L0_tok_w_out, L0_tok_b_out, L0_attn_A_log, L0_attn_D_skip, L0_attn_dt_proj_w, L0_attn_dt_proj_b, L0_attn_x_proj_w, L0_ffn_router_w, L0_ffn_w1, L0_ffn_b1, L0_ffn_w2, L0_ffn_b2, L1_attn_Wq, L1_attn_bq, L1_attn_Wk, L1_attn_bk, L1_attn_Wv, L1_attn_bv, L1_ffn_wg, L1_ffn_we):
    import jax
    import jax.numpy as jnp

    def _L0_tok_ref(x, w_qkv, b_qkv, w_out, b_out):
        import jax, jax.numpy as jnp
        import numpy as np
        import math
        EMBED_DIM = 256
        NUM_HEADS = 16
        HEAD_DIM = EMBED_DIM // NUM_HEADS
        INPUT_DIM = 256
        B, y, S, _ = x.shape
        qkv = jnp.einsum('bysd,ed->byse', x, w_qkv) + b_qkv
        qkv = qkv.reshape(B, S, NUM_HEADS, 3 * HEAD_DIM).transpose(0, 2, 1, 3)
        q, k, v = jnp.split(qkv, 3, axis=-1)
        logits = jnp.einsum('bhqd,bhkd->bhqk', q, k) / math.sqrt(HEAD_DIM)
        attn = jax.nn.softmax(logits, axis=-1)
        vals = jnp.einsum('bhqk,bhkd->bhqd', attn, v)
        vals = vals.transpose(0, 2, 1, 3).reshape(B, S, EMBED_DIM)
        return jnp.einsum('bse,oe->bso', vals, w_out) + b_out

    def _L0_attn_ref(u, A_log, D_skip, dt_proj_w, dt_proj_b, x_proj_w):
        import jax, jax.numpy as jnp
        import numpy as np
        import math
        D_MODEL = 256
        D_STATE = 16
        DT_RANK = 64
        BATCH = 4
        SEQLEN = 512
        xp = jnp.einsum('bld,kd->blk', u, x_proj_w)
        dlow = xp[..., :DT_RANK]
        Bm = xp[..., DT_RANK:DT_RANK + D_STATE]
        Cm = xp[..., DT_RANK + D_STATE:]
        delta = jax.nn.softplus(jnp.einsum('blr,dr->bld', dlow, dt_proj_w) + dt_proj_b)
        A = -jnp.exp(A_log)

        def step(h, xs):
            dt, b_t, c_t, u_t = xs
            dA = jnp.exp(dt[..., None] * A)
            dB = dt[..., None] * b_t[:, None, :]
            h = dA * h + dB * u_t[..., None]
            y_t = jnp.sum(h * c_t[:, None, :], axis=-1)
            return (h, y_t)
        h0 = jnp.zeros((u.shape[0], D_MODEL, D_STATE), dtype=u.dtype)
        xs = (jnp.moveaxis(delta, 1, 0), jnp.moveaxis(Bm, 1, 0), jnp.moveaxis(Cm, 1, 0), jnp.moveaxis(u, 1, 0))
        _, ys = jax.lax.scan(step, h0, xs)
        y = jnp.moveaxis(ys, 0, 1)
        return y + u * D_skip[None, None, :]

    def _L0_ffn_ref(h, router_w, w1, b1, w2, b2):
        import jax, jax.numpy as jnp
        import numpy as np
        B, S, D, E, F = (2, 512, 256, 14, 512)
        Bb, Ss, Dd = h.shape
        x = h.reshape(-1, Dd)
        logits = x @ router_w
        assignments = jnp.argmax(logits, axis=-1)
        probs = jax.nn.softmax(logits, axis=-1)
        weights = jnp.take_along_axis(probs, assignments[:, None], axis=1)[:, 0]
        hid = jnp.einsum('nd,edf->nef', x, w1) + b1
        hid = jax.nn.gelu(hid, approximate=False)
        all_out = jnp.einsum('nef,efd->ned', hid, w2) + b2
        sel = jnp.take_along_axis(all_out, assignments[:, None, None], axis=1)[:, 0, :]
        moe_out = (sel * weights[:, None]).reshape(Bb, Ss, Dd)
        return moe_out

    def _L1_attn_ref(X, Wq, bq, Wk, bk, Wv, bv):
        import jax, jax.numpy as jnp
        import numpy as np
        D = 256
        N, S, Dm = X.shape
        scale = jnp.asarray(Dm ** 0.5, X.dtype)
        Q = jnp.einsum('nsd,ed->nse', X, Wq) + bq
        K = jnp.einsum('nsd,ed->nse', X, Wk) + bk
        V = jnp.einsum('nsd,ed->nse', X, Wv) + bv
        scores = jnp.einsum('nqd,nkd->nqk', Q, K) / scale
        causal = jnp.triu(jnp.ones((S, S), dtype=bool), k=1)
        scores = jnp.where(causal, -jnp.inf, scores)
        weights = jax.nn.softmax(scores, axis=-1)
        return jnp.einsum('nqk,nkd->nqd', weights, V)

    def _L1_ffn_ref(x, wg, we):
        import jax, jax.numpy as jnp
        import numpy as np
        E = 128
        D = 256
        C = 64
        B, S, d = x.shape
        xt = x.reshape(-1, d)
        T = xt.shape[0]
        logits = xt @ wg
        gates = jax.nn.softmax(logits, axis=-1)
        e1 = jnp.argmax(gates, axis=-1)
        mask1 = jax.nn.one_hot(e1, E, dtype=logits.dtype)
        logits2 = jnp.where(mask1 > 0, -jnp.inf, logits)
        e2 = jnp.argmax(logits2, axis=-1)
        mask2 = jax.nn.one_hot(e2, E, dtype=logits.dtype)
        g1 = jnp.take_along_axis(gates, e1[:, None], 1)[:, 0]
        g2 = jnp.take_along_axis(gates, e2[:, None], 1)[:, 0]
        denom = jnp.maximum(g1 + g2, jnp.finfo(gates.dtype).eps)
        g1, g2 = (g1 / denom, g2 / denom)
        loc1 = jnp.take_along_axis(jnp.cumsum(mask1, axis=0), e1[:, None], 1)[:, 0].astype(jnp.int32) - 1
        counts1 = mask1.sum(axis=0)
        loc2 = (jnp.take_along_axis(jnp.cumsum(mask2, axis=0), e2[:, None], 1)[:, 0] + counts1[e2]).astype(jnp.int32) - 1
        v1 = (loc1 < C).astype(xt.dtype)
        v2 = (loc2 < C).astype(xt.dtype)
        idx1 = e1.astype(jnp.int32) * C + jnp.minimum(loc1, C - 1)
        idx2 = e2.astype(jnp.int32) * C + jnp.minimum(loc2, C - 1)
        buf = jnp.zeros((E * C, d), dtype=xt.dtype)
        buf = buf.at[idx1].add(xt * v1[:, None])
        buf = buf.at[idx2].add(xt * v2[:, None])
        yb = jnp.einsum('ecd,edf->ecf', buf.reshape(E, C, d), we).reshape(E * C, d)
        y = (g1 * v1)[:, None] * yb[idx1] + (g2 * v2)[:, None] * yb[idx2]
        return y.reshape(B, S, d)
    h = _L0_tok_ref(x, L0_tok_w_qkv, L0_tok_b_qkv, L0_tok_w_out, L0_tok_b_out)
    h = jnp.concatenate([h, txt], axis=1)
    h = h + _L0_attn_ref(_layernorm(h, axis=-1), L0_attn_A_log, L0_attn_D_skip, L0_attn_dt_proj_w, L0_attn_dt_proj_b, L0_attn_x_proj_w)
    h = h + _L0_ffn_ref(_layernorm(h, axis=-1), L0_ffn_router_w, L0_ffn_w1, L0_ffn_b1, L0_ffn_w2, L0_ffn_b2)
    h = h + _L1_attn_ref(_layernorm(h, axis=-1), L1_attn_Wq, L1_attn_bq, L1_attn_Wk, L1_attn_bk, L1_attn_Wv, L1_attn_bv)
    h = h + _L1_ffn_ref(_layernorm(h, axis=-1), L1_ffn_wg, L1_ffn_we)
    return h

_drawn_inputs = setup_inputs


def setup_inputs(seed=0):
    import zlib

    import numpy as np

    out = dict(_drawn_inputs(seed))
    spreads = {'L0_tok_b_qkv': (0.0, 0.1),
     'L0_tok_b_out': (0.0, 0.1),
     'L0_attn_D_skip': (1.0, 0.2),
     'L0_attn_dt_proj_b': (0.0, 0.1),
     'L0_ffn_b1': (0.0, 0.8),
     'L0_ffn_b2': (0.0, 0.8)}
    factors = {'L1_attn_Wq': 8.0,
     'L1_attn_bq': 26.742,
     'L1_attn_Wk': 8.0,
     'L1_attn_bk': 64.0,
     'L1_attn_bv': 7.518,
     'L1_ffn_we': 2.726}
    for name, (base, spread) in spreads.items():
        noise = np.random.default_rng([zlib.crc32(name.encode()), seed]).standard_normal(out[name].shape)
        drawn = base * np.exp(spread * noise) if base else spread * noise
        out[name] = jnp.asarray(drawn.astype(out[name].dtype))
    for name, factor in factors.items():
        out[name] = (out[name] * factor).astype(out[name].dtype)
    return out
```

```python
import concourse.bass as bass
from concourse import mybir
from contextlib import ExitStack

STAGE = 5


def fusion_kernel(nc, A, out):
    F32, BF16, U32 = mybir.dt.float32, mybir.dt.bfloat16, mybir.dt.uint32
    ALU, ACT, AX = mybir.AluOpType, mybir.ActivationFunctionType, mybir.AxisListType

    P = 128
    NB, S, D = 4, 512, 256
    TXT = 77
    L = S + TXT
    LP = L + 1
    HC = LP // 2
    KC = D // P
    QT = S // P
    NT = QT + 1
    H, HD = 16, D // 16
    PART = 6 * HD
    KR = PART + 3
    NS = 16
    RANK = 64
    EPS = 1e-5
    LT = NT * P
    NE2, CAP = 128, 64
    NP2 = NE2 // 2
    RING, LOAD = 32, 4
    FEPS = 1.1920928955078125e-07
    YG = 4
    NE1, FF = 14, 512
    FC = FF // P
    MT = (NB * L + NE1 * (P - 1)) // P
    QPARTS = [0, 0, 1, 1, 0, 2]
    KPARTS = [0, 1, 0, 1, 2, 0]

    ctx = ExitStack()
    with ctx:
        def sb(name, shape, dt=F32):
            return ctx.enter_context(nc.sbuf_tensor(name, shape, dt))

        def sem(name):
            return ctx.enter_context(nc.semaphore(name))

        def dram(name, shape, dt=F32):
            return nc.dram_tensor(name, shape, dt).ap()

        ps = ctx.enter_context(nc.psum_tensor("ps", [P, 8, 512], F32))

        Hs = sb("Hs", [P, NB * NT, D])
        ident = sb("ident", [P, P])
        zeros = sb("zeros", [P, D])
        G = NB * NT
        lst = sb("lst", [P, G, 6])
        lmean = sb("lmean", [P, G])
        lrstd = sb("lrstd", [P, G])
        ltmp = sb("ltmp", [P, G])
        lbias = sb("lbias", [P, G])
        xab = sb("xab", [P, 2, D])
        xaT = sb("xaT", [P, 2, KC, P])
        m8b = sb("m8b", [P, 2, 8])
        i8b = sb("i8b", [P, 2, 8], U32)
        best = sb("best", [P, G, 2])
        besti = sb("besti", [P, G, 2])
        early = ExitStack()

        def eb(name, shape, dt=F32):
            return early.enter_context(nc.sbuf_tensor(name, shape, dt))
        xT = eb("xT", [P, KC, S])
        wqkv = eb("wqkv", [P, KC, 3 * D])
        wo = eb("wo", [P, KC, D])
        bqk = eb("bqk", [P, 4])
        bv = eb("bv", [P, D])
        bo = eb("bo", [P, D])
        Qst = eb("Qst", [KR, H, S], BF16)
        Kst = eb("Kst", [KR, H, S], BF16)
        Vaug = eb("Vaug", [P, QT, H, HD + 1])
        mx = eb("mx", [P, P // QT, QT])
        mneg = eb("mneg", [H * QT, P])
        mparts = eb("mparts", [H * QT, 3, P], BF16)
        rsum = eb("rsum", [P, 2, QT, 1])
        vals = eb("vals", [P, QT, D])
        valsT = eb("valsT", [P, KC, S])
        xpw = eb("xpw", [P, KC, RANK])
        xpbc = eb("xpbc", [P, KC, 96])
        dtw = eb("dtw", [RANK, D])
        dtb = eb("dtb", [P, KC])
        dsk = eb("dsk", [P, KC])
        alog = eb("alog", [P, KC * NS])
        acol = eb("acol", [P, KC * NS])
        sel = eb("sel", [96, 2 * NS, P], BF16)
        tick = eb("tick", [P, 1])
        st6 = eb("st6", [P, NT, 6])
        mv = eb("mv", [P, NT, 2])
        rstd = eb("rstd", [P, NT])
        xn = eb("xn", [P, NT, D])
        uT = eb("uT", [P, KC, LP])
        dlow = eb("dlow", [RANK, LP])
        bc32 = eb("bc32", [96, LP])
        bcp = eb("bcp", [96, 2, LP], BF16)
        bcs = eb("bcs", [96, LP], BF16)
        xb = eb("xb", [P, KC, LP])
        sp = eb("sp", [P, KC, LP])
        delta = eb("delta", [P, KC, LP])
        dtu = eb("dtu", [P, KC, LP])
        Cb = eb("Cb", [P, 2, LP])

        turn1, turn2 = ExitStack(), ExitStack()
        qk32 = turn1.enter_context(nc.sbuf_tensor("qk32", [P, 4, S], F32))
        parts = turn1.enter_context(nc.sbuf_tensor("parts", [P, 3, 4, S], BF16))
        PT = turn1.enter_context(nc.sbuf_tensor("PT", [P, 2, QT, S], F32))
        turn1.close()
        dA = turn2.enter_context(nc.sbuf_tensor("dA", [P, 2, KC, LP], F32))
        dBu = turn2.enter_context(nc.sbuf_tensor("dBu", [P, 2, KC, LP], F32))
        hst = turn2.enter_context(nc.sbuf_tensor("hst", [P, 2, KC, LP], F32))
        hC = turn2.enter_context(nc.sbuf_tensor("hC", [P, 2, KC, LP], F32))
        turn2.close()
        early.close()
        late = ExitStack()

        def lb(name, shape, dt=F32):
            return late.enter_context(nc.sbuf_tensor(name, shape, dt))
        W1 = lb("W1", [P, NE1, KC, FF])
        W2 = lb("W2", [P, NE1, FC, D])
        b12 = lb("b12", [NE1, FF + D])
        b12p = lb("b12p", [NE1, 3, FF + D], BF16)
        brow = lb("brow", [3, NE1, FF + D], BF16)
        ones3 = lb("ones3", [3, P], BF16)
        rw = lb("rw", [P, KC, NE1])
        tri = lb("tri", [P, P], BF16)
        onesm = lb("onesm", [P, P], BF16)
        real = lb("real", [P, G])
        iota1 = lb("iota1", [P, NE1])
        iota128 = lb("iota128", [P, G])
        ramp = lb("ramp", [P, MT])
        keep = lb("keep", [P, NE1 * G])
        lg = lb("lg", [P, G, NE1])
        lgb = lb("lgb", [P, 2, NE1])
        nottoken = lb("nottoken", [P, G])
        hot = lb("hot", [P, G, NE1], BF16)
        cnt = lb("cnt", [P, NE1, G])
        cum = lb("cum", [P, NE1, G])
        big = lb("big", [P, NE1, MT])
        ntile = lb("ntile", [P, NE1])
        tend = lb("tend", [P, NE1])
        toff = lb("toff", [P, NE1])
        pos = lb("pos", [P, G, NE1])
        slotf = lb("slotf", [P, G])
        slots = lb("slots", [P, G], U32)
        slotg = lb("slotg", [P, G], U32)
        te = lb("te", [P, MT])
        tei = lb("tei", [P, MT], U32)
        gate = lb("gate", [P, G])
        turn3 = ExitStack()
        xa = turn3.enter_context(nc.sbuf_tensor("xa", [P, G, D], F32))
        turn3.close()
        xg = lb("xg", [P, 2, D])
        xgT = lb("xgT", [P, 2, KC, P])
        hid = lb("hid", [P, 2, FF])
        hidT = lb("hidT", [P, 2, FC, P])
        yo = lb("yo", [P, 2, D])
        yg = lb("yg", [P, YG, D])
        late.close()
        last = ExitStack()

        def tb(name, shape, dt=F32):
            return last.enter_context(nc.sbuf_tensor(name, shape, dt))
        ring = tb("ring", [P, RING, KC, D])
        w4 = tb("w4", [P, KC, 3 * D])
        bqk4 = tb("bqk4", [P, 4])
        bv4 = tb("bv4", [P, D])
        mask4 = tb("mask4", [P, P])
        wg = tb("wg", [P, KC, NE2])
        xn4 = tb("xn4", [P, NT, D])
        xT4 = tb("xT4", [P, KC, LT])
        QK4 = tb("QK4", [P, 4, LT])
        V4 = tb("V4", [P, NT, D])
        P4 = tb("P4", [P, 2, LT])
        PT4 = tb("PT4", [P, 2, NT, P])
        nm4 = tb("nm4", [P, NT])
        rs4 = tb("rs4", [P, NT])
        tri5 = tb("tri5", [P, 2, P], BF16)
        real5 = tb("real5", [P, G])
        nottoken5 = tb("nottoken5", [P, G])
        iota5 = tb("iota5", [P, NE2])
        lgb5 = tb("lgb5", [P, 2, NE2])
        lg5 = tb("lg5", [P, G, NE2])
        hotb = tb("hotb", [P, 2, 2, NE2], BF16)
        hot2 = tb("hot2", [P, G, NE2], BF16)
        hot2f = tb("hot2f", [P, G, NE2])
        junk = tb("junk", [P, NE2])
        locb = tb("locb", [P, 2, 2])
        loc = tb("loc", [P, G, 2])
        c1 = tb("c1", [P, NE2])
        w5 = tb("w5", [P, G, 2])
        v5 = tb("v5", [P, G, 2])
        den = tb("den", [P, G])
        rowf = tb("rowf", [P, G, 2])
        to5 = tb("to5", [P, G, 2], U32)
        from5 = tb("from5", [P, G, 2], U32)
        turn4 = ExitStack()
        xa5 = turn4.enter_context(nc.sbuf_tensor("xa5", [P, G, D], F32))
        turn4.close()
        xg5 = tb("xg5", [P, 2, D])
        xgT5 = tb("xgT5", [P, 2, KC, P])
        yo5 = tb("yo5", [P, 2, D])
        yg5 = tb("yg5", [P, 2 * YG, D])
        last.close()

        qk_dram = dram("qk_dram", [NB, 3, 2, D, S], BF16)
        xs_dram = dram("xs_dram", [MT * P, D])
        ys_dram = dram("ys_dram", [MT * P, D])
        b_dram = dram("b_dram", [3, NE1, FF + D], BF16)
        xs5_dram = dram("xs5_dram", [NE2 * CAP, D])
        ys5_dram = dram("ys5_dram", [NE2 * CAP, D])
        m_dram = dram("m_dram", [NB, 3, H * QT * P], BF16)

        consts_in = sem("consts_in")
        txt_in = sem("txt_in")
        x_in = sem("x_in")
        parts_out = sem("parts_out")
        stacks_in = sem("stacks_in")
        mrow_out = sem("mrow_out")
        mrow_in = sem("mrow_in")
        out_done = sem("out_done")
        pool_init = sem("pool_init")
        pe_qk = sem("pe_qk")
        pe_v = sem("pe_v")
        pe_s = sem("pe_s")
        pe_mT = sem("pe_mT")
        pe_st = sem("pe_st")
        pe_pv = sem("pe_pv")
        pe_vT = sem("pe_vT")
        pe_o = sem("pe_o")
        dve_init = sem("dve_init")
        dve_qk32 = sem("dve_qk32")
        dve_res = sem("dve_res")
        dve_p3 = sem("dve_p3")
        dve_v = sem("dve_v")
        dve_max = sem("dve_max")
        dve_mneg = sem("dve_mneg")
        dve_mparts = sem("dve_mparts")
        dve_rsum = sem("dve_rsum")
        dve_vals = sem("dve_vals")
        dve_vT = sem("dve_vT")
        dve_h1 = sem("dve_h1")
        act_acol = sem("act_acol")
        act_p1 = sem("act_p1")
        act_p2 = sem("act_p2")
        act_exp = sem("act_exp")
        dve_stats = sem("dve_stats")
        act_std = sem("act_std")
        dve_rstd = sem("dve_rstd")
        dve_xn = sem("dve_xn")
        pe_uT = sem("pe_uT")
        act_uT = sem("act_uT")
        pe_xp = sem("pe_xp")
        act_dlow = sem("act_dlow")
        dve_bcs = sem("dve_bcs")
        dve_bcchain = sem("dve_bcchain")
        pe_dt = sem("pe_dt")
        dve_xb = sem("dve_xb")
        dve_sp = sem("dve_sp")
        act_sp = sem("act_sp")
        dve_delta = sem("dve_delta")
        dve_dtu = sem("dve_dtu")
        pe_bc = sem("pe_bc")
        act_dA = sem("act_dA")
        act_C = sem("act_C")
        dve_dBu = sem("dve_dBu")
        dve_scan = sem("dve_scan")
        pool_hC = sem("pool_hC")
        pe_y = sem("pe_y")
        dve_yT = sem("dve_yT")
        pe_yT = sem("pe_yT")
        dve_h2 = sem("dve_h2")
        late_in = sem("late_in")
        w_in = sem("w_in")
        b12_in = sem("b12_in")
        b_out = sem("b_out")
        brow_in = sem("brow_in")
        ln_chain = sem("ln_chain")
        ln_stats = sem("ln_stats")
        ln_std = sem("ln_std")
        ln_done = sem("ln_done")
        dve_bparts = sem("dve_bparts")
        zero_out = sem("zero_out")
        pe_xaT = sem("pe_xaT")
        act_xaT = sem("act_xaT")
        pe_lg = sem("pe_lg")
        dve_lg = sem("dve_lg")
        c3 = sem("c3")
        dve_hot = sem("dve_hot")
        pe_rank = sem("pe_rank")
        dve_slots = sem("dve_slots")
        dve_te = sem("dve_te")
        dve_ex = sem("dve_ex")
        act_ex = sem("act_ex")
        dve_gate = sem("dve_gate")
        rows_out = sem("rows_out")
        tile_in0 = sem("tile_in0")
        tile_in1 = sem("tile_in1")
        pe_xg = sem("pe_xg")
        act_xg = sem("act_xg")
        pe_up = sem("pe_up")
        act_gelu = sem("act_gelu")
        pe_hidT = sem("pe_hidT")
        dve_hidT = sem("dve_hidT")
        pe_down = sem("pe_down")
        dve_yo = sem("dve_yo")
        yo_out = [sem("yo_out0"), sem("yo_out1")]
        yg_in = [sem(f"yg_in{k}") for k in range(YG)]
        best_chain = sem("best_chain")
        act_xab = sem("act_xab")
        pool_xa = sem("pool_xa")
        dve_h3 = sem("dve_h3")
        last_in = sem("last_in")
        act_xn4 = sem("act_xn4")
        pe_xT4 = sem("pe_xT4")
        act_xT4 = sem("act_xT4")
        pe_qk4 = sem("pe_qk4")
        pe_v4 = sem("pe_v4")
        dve_qk4 = sem("dve_qk4")
        dve_v4 = sem("dve_v4")
        pe_s4 = sem("pe_s4")
        dve_mask4 = sem("dve_mask4")
        dve_nm4 = sem("dve_nm4")
        act_p4 = sem("act_p4")
        pe_pt4 = sem("pe_pt4")
        dve_pt4 = sem("dve_pt4")
        pe_pv4 = sem("pe_pv4")
        dve_rs4 = sem("dve_rs4")
        dve_h4 = sem("dve_h4")
        zero5_out = sem("zero5_out")
        ring_in = [sem(f"ring_in{k}") for k in range(RING // LOAD)]
        dve_hot5 = sem("dve_hot5")
        pe_rank5 = sem("pe_rank5")
        dve_rank5 = sem("dve_rank5")
        pe_count5 = sem("pe_count5")
        c5 = sem("c5")
        dve_ex5 = sem("dve_ex5")
        act_ex5 = sem("act_ex5")
        dve_to5 = sem("dve_to5")
        rows5_out = sem("rows5_out")
        tile5_in = [sem("tile5_in0"), sem("tile5_in1")]
        pe_xg5 = sem("pe_xg5")
        act_xg5 = sem("act_xg5")
        pe_y5 = sem("pe_y5")
        dve_y5 = sem("dve_y5")
        y5_out = [sem("y5_out0"), sem("y5_out1")]
        yg5_in = [sem(f"yg5_in{k}") for k in range(2 * YG)]
        dve_h5 = sem("dve_h5")
        N_CONSTS = 14
        N_LAST = 9
        N_LATE = 10

        def bias_rows(name):
            return A[name].rearrange("(o d) -> o d", o=1).to_broadcast([P, D])

        def two_banks(lo, rows=P):
            return ps[0:rows, lo:lo + 2, 0:HC]

        def halves(ap):
            return ap.rearrange("p (c t) -> p c t", c=2)

        A = {n: a.bitcast(BF16) if n in ("sel", "ones3", "tri", "onesm", "tri5", "ones3p") else a for n, a in A.items()}
        block = ctx.enter_context(nc.Block())

        @block.sync
        def _(q):
            q.dma_start(wqkv[:, :, :], A["wqkvT"]).then_inc(consts_in, 16)
            q.dma_start(bqk[:, :], A["bqk"]).then_inc(consts_in, 16)
            q.dma_start(bv[:, :], bias_rows("bv")).then_inc(consts_in, 16)
            q.dma_start(bo[:, :], bias_rows("bo")).then_inc(consts_in, 16)
            q.dma_start(wo[:, :, :], A["woT"]).then_inc(consts_in, 16)
            q.dma_start(ident[:, :], A["ident"]).then_inc(consts_in, 16)
            q.dma_start(xpw[:, :, :], A["xpwT"]).then_inc(consts_in, 16)
            q.dma_start(xpbc[:, :, :], A["xpbcT"]).then_inc(consts_in, 16)
            q.dma_start(dtw[:, :], A["dtwT"]).then_inc(consts_in, 16)
            q.dma_start(dtb[:, :], A["dtb"]).then_inc(consts_in, 16)
            q.dma_start(dsk[:, :], A["dsk"]).then_inc(consts_in, 16)
            q.dma_start(alog[:, :], A["alog"]).then_inc(consts_in, 16)
            q.dma_start(sel[:, :, :], A["sel"]).then_inc(consts_in, 16)
            q.dma_start(Kst[PART:KR, :, :], A["ones3"]).then_inc(consts_in, 16)
            q.wait_ge(pool_init, 2)
            if STAGE >= 3:
                q.dma_start(xs_dram.rearrange("(j p) d -> p j d", p=P),
                            zeros[:, :].rearrange("p (o d) -> p o d", o=1).to_broadcast([P, MT, D])).then_inc(zero_out, 16)
                q.dma_start(xs5_dram.rearrange("(j p) d -> p j d", p=P),
                            zeros[:, :].rearrange("p (o d) -> p o d", o=1).to_broadcast([P, NP2, D])).then_inc(zero5_out, 16)
            for b in range(NB):
                q.dma_start(Hs[0:TXT, b * NT + QT, :], A["txt"][b]).then_inc(txt_in, 16)
            with q.Fori(0, NB) as b:
                q.wait_ge(pe_v, b + 1)
                q.dma_start(xT[:, :, :], A["xT"][b]).then_inc(x_in, 16)
                q.wait_ge(dve_p3, 4 * (b + 1))
                for part in range(3):
                    q.dma_start(qk_dram[b, part].rearrange("a (m p) s -> p (a m) s", p=P),
                                parts[:, part, :, :]).then_inc(parts_out, 16)
                q.wait_ge(parts_out, 48 * (b + 1))
                for stack, a, order in ((Qst, 0, QPARTS), (Kst, 1, KPARTS)):
                    for g, part in enumerate(order):
                        q.dma_start(stack[HD * g:HD * (g + 1), :, :],
                                    qk_dram[b, part, a].rearrange("(h d) s -> d h s", d=HD)).then_inc(stacks_in, 16)
                q.wait_ge(dve_mparts, b + 1)
                q.dma_start(m_dram[b].rearrange("a (r s) -> r a s", s=P), mparts[:, :, :]).then_inc(mrow_out, 16)
                q.wait_ge(mrow_out, 16 * (b + 1))
                q.dma_start(Qst[PART:KR, :, :].rearrange("p h s -> p (h s)"), m_dram[b]).then_inc(mrow_in, 16)
            q.wait_ge(dve_h2, NB + 1)
            if STAGE >= 3:
                q.dma_start(b12[:, :], A["b12"]).then_inc(b12_in, 16)
                for dst, name in ((rw[:, :, :], "rw"), (tri[:, :], "tri"), (onesm[:, :], "onesm"), (real[:, :], "real"),
                                  (iota1[:, :], "iota1"), (iota128[:, :], "iota128"), (ramp[:, :], "ramp"),
                                  (keep[:, :], "keep1"), (nottoken[:, :], "nottoken"), (ones3[:, :], "ones3p")):
                    q.dma_start(dst, A[name]).then_inc(late_in, 16)
                q.wait_ge(dve_bparts, 3)
                q.dma_start(b_dram.rearrange("k e f -> e k f"), b12p[:, :, :]).then_inc(b_out, 16)
                q.wait_ge(b_out, 16)
                q.dma_start(brow[:, :, :], b_dram).then_inc(brow_in, 16)
                for e in range(0, NE1, 2):
                    q.dma_start(W1[:, e:e + 2, :, :], A["w1"][:, e:e + 2]).then_inc(w_in, 16)
                    q.dma_start(W2[:, e:e + 2, :, :], A["w2"][:, e:e + 2]).then_inc(w_in, 16)
                q.wait_ge(rows_out, 16 * G)
                q.wait_ge(zero_out, 16)

                def tile_load(j, u, tile_in):
                    q.wait_ge(pe_xg, j - 1)
                    q.dma_start(xg[:, u, :], xs_dram[bass.ds(j * P, P), :]).then_inc(tile_in, 16)

                def tile_store(j, u):
                    q.wait_ge(dve_yo, j + 1)
                    q.dma_start(ys_dram[bass.ds(j * P, P), :], yo[:, u, :]).then_inc(yo_out[u], 16)
                q.dma_start(xg[:, 0, :], xs_dram[0:P, :]).then_inc(tile_in0, 16)
                q.dma_start(xg[:, 1, :], xs_dram[P:2 * P, :]).then_inc(tile_in1, 16)
                with q.Fori(1, MT // 2) as i:
                    tile_load(2 * i, 0, tile_in0)
                    tile_store(2 * i - 2, 0)
                    tile_load(2 * i + 1, 1, tile_in1)
                    tile_store(2 * i - 1, 1)
                tile_store(MT - 2, 0)
                tile_store(MT - 1, 1)
                q.wait_ge(dve_h3, G)
            if STAGE >= 4:
                for dst, name in ((w4[:, :, :], "w4T"), (bqk4[:, :], "bqk4"), (mask4[:, :], "mask4"), (wg[:, :, :], "wg"),
                                  (tri5[:, :, :], "tri5"), (real5[:, :], "real"), (nottoken5[:, :], "nottoken"),
                                  (iota5[:, :], "iota5")):
                    q.dma_start(dst, A[name]).then_inc(last_in, 16)
                q.dma_start(bv4[:, :], bias_rows("bv4")).then_inc(last_in, 16)
                if STAGE >= 5:
                    for k in range(RING // LOAD):
                        q.dma_start(ring[:, LOAD * k:LOAD * (k + 1), :, :], A["we"][:, LOAD * k:LOAD * (k + 1)]).then_inc(ring_in[k], 16)
                q.wait_ge(dve_h4, G + 1)
            if STAGE >= 5:
                q.wait_ge(zero5_out, 16)
                q.wait_ge(rows5_out, 32 * G)

                def pair_load(j, u, first):
                    if not first:
                        q.wait_ge(pe_xg5, j - 1)
                    q.dma_start(xg5[:, u, :], xs5_dram[bass.ds(j * P, P), :]).then_inc(tile5_in[u], 16)

                def pair_store(j, u):
                    q.wait_ge(dve_y5, 2 * j + 2)
                    q.dma_start(ys5_dram[bass.ds(j * P, P), :], yo5[:, u, :]).then_inc(y5_out[u], 16)

                def turn_of_ring(lap, last_lap):
                    for k in range(RING // LOAD):
                        for m in range(LOAD // 2):
                            j = lap * (RING // 2) + k * (LOAD // 2) + m
                            u = m % 2
                            if not (last_lap and k == RING // LOAD - 1):
                                pair_load(j + 2, u, False)
                            pair_store(j, u)
                        if not last_lap:
                            q.dma_start(ring[:, LOAD * k:LOAD * (k + 1), :, :],
                                        A["we"][:, bass.ds((lap + 1) * RING + LOAD * k, LOAD)]).then_inc(ring_in[k], 16)
                pair_load(0, 0, True)
                pair_load(1, 1, True)
                with q.Fori(0, NE2 // RING - 1) as lap:
                    turn_of_ring(lap, False)
                turn_of_ring(NE2 // RING - 1, True)
                q.wait_ge(dve_h5, 2 * G)
            for b in range(NB):
                q.dma_start(out[b, 0:S].rearrange("(i p) d -> p i d", p=P), Hs[:, b * NT:b * NT + QT, :]).then_inc(out_done, 16)
                q.dma_start(out[b, S:L], Hs[0:TXT, b * NT + QT, :]).then_inc(out_done, 16)
            q.wait_ge(out_done, 32 * NB)

        @block.tensor
        def _(pe):
            def attention(b):
                pe.wait_ge(x_in, 16 * (b + 1))
                pe.wait_ge(dve_h2, b + 1)
                for t in range(4):
                    for c in range(KC):
                        m = nc.tensor.matmul(ps[:, t, :], wqkv[:, c, P * t:P * (t + 1)], xT[:, c, :],
                                             start=(c == 0), stop=(c == KC - 1))
                    m.then_inc(pe_qk, 1)
                for i in range(QT):
                    for c in range(KC):
                        m = nc.tensor.matmul(ps[:, 4 + i // 2, D * (i % 2):D * (i % 2 + 1)],
                                             xT[:, c, P * i:P * (i + 1)], wqkv[:, c, 2 * D:3 * D],
                                             start=(c == 0), stop=(c == KC - 1))
                m.then_inc(pe_v, 1)
                pe.wait_ge(stacks_in, 192 * (b + 1))
                pe.wait_ge(dve_v, b + 1)

                def scores(h, group, first):
                    if not first:
                        pe.wait_ge(dve_max, H * b + h - 1)
                    for i in range(QT):
                        m = nc.tensor.matmul(ps[:, 4 * group + i, :], Qst[0:PART, h, P * i:P * (i + 1)],
                                             Kst[0:PART, h, :], start=True, stop=True)
                    m.then_inc(pe_s, 1)
                scores(0, 0, True)
                scores(1, 1, True)
                with pe.Fori(1, H // 2) as i:
                    scores(2 * i, 0, False)
                    scores(2 * i + 1, 1, False)
                pe.wait_ge(dve_max, H * (b + 1))
                nc.tensor.transpose(ps[:, 0, 0:P], mx[:, :, :].rearrange("p h i -> p (h i)"),
                                    ident[:, :]).then_inc(pe_mT, 1)
                pe.wait_ge(dve_mneg, b + 1)
                pe.wait_ge(mrow_in, 16 * (b + 1))

                def tscores(h, first):
                    for half in range(2):
                        if not first:
                            pe.wait_ge(act_exp, 2 * (H * b + h) - 1 + half)
                        for j in range(2):
                            i = 2 * half + j
                            m = nc.tensor.matmul(ps[:, i, :], Kst[:, h, P * i:P * (i + 1)],
                                                 Qst[:, h, :], start=True, stop=True)
                        m.then_inc(pe_st, 1)

                def weighted(h, group, first):
                    pe.wait_ge(act_exp, 2 * (H * b + h + 1))
                    if not first:
                        pe.wait_ge(dve_vals, H * b + h - 1)
                    for i in range(QT):
                        for j in range(QT):
                            m = nc.tensor.matmul(ps[:, 4 + group, (HD + 1) * i:(HD + 1) * (i + 1)],
                                                 PT[:, group, j, P * i:P * (i + 1)], Vaug[:, j, h, :],
                                                 start=(j == 0), stop=(j == QT - 1))
                    m.then_inc(pe_pv, 1)
                tscores(0, True)
                tscores(1, False)
                weighted(0, 0, True)
                tscores(2, False)
                weighted(1, 1, True)
                with pe.Fori(1, H // 2 - 1) as i:
                    tscores(2 * i + 1, False)
                    weighted(2 * i, 0, False)
                    tscores(2 * i + 2, False)
                    weighted(2 * i + 1, 1, False)
                tscores(H - 1, False)
                weighted(H - 2, 0, False)
                weighted(H - 1, 1, False)
                pe.wait_ge(dve_vals, H * (b + 1))
                for c in range(KC):
                    for i in range(QT):
                        m = nc.tensor.transpose(ps[:, c, P * i:P * (i + 1)], vals[:, i, P * c:P * (c + 1)], ident[:, :])
                m.then_inc(pe_vT, 1)
                pe.wait_ge(dve_vT, b + 1)
                for i in range(QT):
                    for c in range(KC):
                        m = nc.tensor.matmul(ps[:, 2 + i // 2, D * (i % 2):D * (i % 2 + 1)],
                                             valsT[:, c, P * i:P * (i + 1)], wo[:, c, :],
                                             start=(c == 0), stop=(c == KC - 1))
                m.then_inc(pe_o, 1)

            def scan(b):
                pe.wait_ge(dve_xn, b + 1)
                for c in range(KC):
                    for i in range(NT):
                        dst = ps[:, 4 + c, P * i:P * (i + 1)] if i < QT else ps[:, 6, P * c:P * (c + 1)]
                        m = nc.tensor.transpose(dst, xn[:, i, P * c:P * (c + 1)], ident[:, :])
                m.then_inc(pe_uT, 1)
                pe.wait_ge(act_uT, b + 1)
                for half in range(2):
                    for c in range(KC):
                        nc.tensor.matmul(ps[0:RANK, half, 0:HC], xpw[:, c, :], uT[:, c, HC * half:HC * (half + 1)],
                                         start=(c == 0), stop=(c == KC - 1))
                for half in range(2):
                    for c in range(KC):
                        m = nc.tensor.matmul(ps[0:96, 2 + half, 0:HC], xpbc[:, c, :], uT[:, c, HC * half:HC * (half + 1)],
                                             start=(c == 0), stop=(c == KC - 1))
                m.then_inc(pe_xp, 1)
                pe.wait_ge(act_dlow, b + 1)
                for c in range(KC):
                    for half in range(2):
                        m = nc.tensor.matmul(ps[:, 4 + 2 * c + half, 0:HC], dtw[:, P * c:P * (c + 1)],
                                             dlow[:, HC * half:HC * (half + 1)], start=True, stop=True)
                m.then_inc(pe_dt, 1)

                def spread(n, first):
                    if not first:
                        pe.wait_ge(dve_dBu, NS * b + n)
                        pe.wait_ge(act_C, NS * b + n)
                    for which in range(2):
                        for half in range(2):
                            m = nc.tensor.matmul(ps[:, 2 * which + half, 0:HC], sel[:, NS * which + n, :],
                                                 bcs[:, HC * half:HC * (half + 1)], start=True, stop=True)
                    m.then_inc(pe_bc, 1)

                def add_state(n, u, start, stop):
                    for c in range(KC):
                        pe.wait_ge(pool_hC, 2 * (NS * b + n) + 1 + c)
                        for half in range(2):
                            m = nc.tensor.matmul(ps[:, 4 + 2 * c + half, 0:HC], ident[:, :],
                                                 hC[:, u, c, HC * half:HC * (half + 1)], start=start, stop=stop,
                                                 skip_group_check=True)
                    m.then_inc(pe_y, 1)
                pe.wait_ge(dve_bcs, b + 1)
                spread(0, True)
                pe.wait_ge(dve_xb, b + 1)
                spread(1, False)
                add_state(0, 0, True, False)
                spread(2, False)
                add_state(1, 1, False, False)
                with pe.Fori(1, NS // 2 - 1) as i:
                    spread(2 * i + 1, False)
                    add_state(2 * i, 0, False, False)
                    spread(2 * i + 2, False)
                    add_state(2 * i + 1, 1, False, False)
                spread(NS - 1, False)
                add_state(NS - 2, 0, False, False)
                add_state(NS - 1, 1, False, True)
                pe.wait_ge(dve_yT, b + 1)
                pe.wait_ge(dve_dBu, NS * (b + 1))
                pe.wait_ge(act_C, NS * (b + 1))
                for i in range(NT):
                    rows = P if i < QT else TXT
                    for c in range(KC):
                        m = nc.tensor.transpose(ps[0:rows, i // 2, D * (i % 2) + P * c:D * (i % 2) + P * (c + 1)],
                                                xb[:, c, P * i:P * i + rows], ident[:, :])
                m.then_inc(pe_yT, 1)

            def route(r, weights, n_experts, rank=None):
                def turn(t, u, first):
                    pe.wait_ge(act_xab, r * G + t + 1)
                    if not first:
                        pe.wait_ge(act_xaT, r * G + t - 1)
                    for c in range(KC):
                        m = nc.tensor.transpose(ps[:, u, P * c:P * (c + 1)], xab[:, u, P * c:P * (c + 1)], ident[:, :])
                    m.then_inc(pe_xaT, 1)

                def logits(t, u, first):
                    pe.wait_ge(act_xaT, r * G + t + 1)
                    if not first:
                        pe.wait_ge(dve_lg, r * G + t - 1)
                    for c in range(KC):
                        m = nc.tensor.matmul(ps[:, 2 + u, 0:n_experts], xaT[:, u, c, :], weights[:, c, :],
                                             start=(c == 0), stop=(c == KC - 1))
                    m.then_inc(pe_lg, 1)
                    if rank:
                        rank(t, u, isinstance(t, int) and t == 0)
                turn(0, 0, True)
                turn(1, 1, True)
                logits(0, 0, True)
                turn(2, 0, False)
                logits(1, 1, True)
                with pe.Fori(1, G // 2 - 1) as i:
                    turn(2 * i + 1, 1, False)
                    logits(2 * i, 0, False)
                    turn(2 * i + 2, 0, False)
                    logits(2 * i + 1, 1, False)
                turn(G - 1, 1, False)
                logits(G - 2, 0, False)
                logits(G - 1, 1, False)

            def one_expert():
                pe.wait_ge(late_in, 16 * N_LATE)
                route(0, rw, NE1)
                pe.wait_ge(dve_hot, 1)
                nc.tensor.matmul(ps[:, 4, 0:G * NE1], tri[:, :], hot[:, :, :].rearrange("p g e -> p (g e)"), start=True, stop=True)
                nc.tensor.matmul(ps[:, 5, 0:G * NE1], onesm[:, :], hot[:, :, :].rearrange("p g e -> p (g e)"),
                                 start=True, stop=True).then_inc(pe_rank, 1)
                pe.wait_ge(dve_te, 1)
                pe.wait_ge(w_in, 16 * NE1)
                pe.wait_ge(brow_in, 16)

                def turn(j, u, tile_in, first):
                    pe.wait_ge(tile_in, 16 * (j // 2 + 1) if isinstance(j, int) else 8 * (j - u) + 16)
                    if not first:
                        pe.wait_ge(act_xg, j - 1)
                    for c in range(KC):
                        m = nc.tensor.transpose(ps[:, u, P * c:P * (c + 1)], xg[:, u, P * c:P * (c + 1)], ident[:, :])
                    m.then_inc(pe_xg, 1)

                def up(j, u, first):
                    e = pe.value_load(tei[0:1, bass.ds(j, 1)], min_val=0, max_val=NE1 - 1)
                    pe.wait_ge(act_xg, j + 1)
                    if not first:
                        pe.wait_ge(act_gelu, j - 1)
                    for c in range(KC):
                        nc.tensor.matmul(ps[:, 2 + u, :], xgT[:, u, c, :], W1[:, e, c, :], start=(c == 0), stop=False)
                    nc.tensor.matmul(ps[:, 2 + u, :], ones3[:, :], brow[:, e, 0:FF], start=False, stop=True).then_inc(pe_up, 1)

                def down(j, u, first):
                    e = pe.value_load(tei[0:1, bass.ds(j, 1)], min_val=0, max_val=NE1 - 1)
                    pe.wait_ge(act_gelu, j + 1)
                    if not first:
                        pe.wait_ge(dve_hidT, j - 1)
                    for f in range(FC):
                        m = nc.tensor.transpose(ps[:, 4 + u, P * f:P * (f + 1)], hid[:, u, P * f:P * (f + 1)], ident[:, :])
                    m.then_inc(pe_hidT, 1)
                    pe.wait_ge(dve_hidT, j + 1)
                    if not first:
                        pe.wait_ge(dve_yo, j - 1)
                    for f in range(FC):
                        nc.tensor.matmul(ps[:, 6 + u, 0:D], hidT[:, u, f, :], W2[:, e, f, :], start=(f == 0), stop=False)
                    nc.tensor.matmul(ps[:, 6 + u, 0:D], ones3[:, :], brow[:, e, FF:FF + D], start=False, stop=True).then_inc(pe_down, 1)
                turn(0, 0, tile_in0, True)
                up(0, 0, True)
                turn(1, 1, tile_in1, True)
                up(1, 1, True)
                down(0, 0, True)
                turn(2, 0, tile_in0, False)
                up(2, 0, False)
                down(1, 1, True)
                with pe.Fori(1, MT // 2 - 1) as i:
                    turn(2 * i + 1, 1, tile_in1, False)
                    up(2 * i + 1, 1, False)
                    down(2 * i, 0, False)
                    turn(2 * i + 2, 0, tile_in0, False)
                    up(2 * i + 2, 0, False)
                    down(2 * i + 1, 1, False)
                turn(MT - 1, 1, tile_in1, False)
                up(MT - 1, 1, False)
                down(MT - 2, 0, False)
                down(MT - 1, 1, False)

            def causal_batch(b):
                for i in range(NT):
                    pe.wait_ge(act_xn4, NT * b + i + 1)
                    if i == 0:
                        pe.wait_ge(dve_h4, NT * b + 1)
                    for c in range(KC):
                        dst = ps[:, c, P * i:P * (i + 1)] if i < QT else ps[:, 2, P * c:P * (c + 1)]
                        m = nc.tensor.transpose(dst, xn4[:, i, P * c:P * (c + 1)], ident[:, :])
                m.then_inc(pe_xT4, 1)
                pe.wait_ge(act_xT4, b + 1)
                for t in range(4):
                    for lo, n, dst in ((0, S, ps[:, t, :]), (S, P, ps[:, 4, P * t:P * (t + 1)])):
                        for c in range(KC):
                            m = nc.tensor.matmul(dst, w4[:, c, P * t:P * (t + 1)], xT4[:, c, lo:lo + n],
                                                 start=(c == 0), stop=(c == KC - 1))
                m.then_inc(pe_qk4, 1)
                for i in range(NT):
                    for c in range(KC):
                        m = nc.tensor.matmul(ps[:, 5 + i // 2, D * (i % 2):D * (i % 2 + 1)], xT4[:, c, P * i:P * (i + 1)],
                                             w4[:, c, 2 * D:3 * D], start=(c == 0), stop=(c == KC - 1))
                m.then_inc(pe_v4, 1)

                def scores(i):
                    if i >= 2:
                        pe.wait_ge(act_p4, NT * b + i - 1)
                    for lo, hi in ((0, min(P * (i + 1), S)), (S, P * (i + 1))):
                        for c in range(KC):
                            if hi > lo:
                                m = nc.tensor.matmul(ps[:, 2 * (i % 2) + lo // S, 0:hi - lo], QK4[:, c, P * i:P * (i + 1)],
                                                     QK4[:, 2 + c, lo:hi], start=(c == 0), stop=(c == KC - 1))
                    m.then_inc(pe_s4, 1)

                def weighted(i):
                    pe.wait_ge(act_p4, NT * b + i + 1)
                    if i >= 1:
                        pe.wait_ge(dve_pt4, NT * b + i)
                    for j in range(i + 1):
                        m = nc.tensor.transpose(ps[:, 4 + j // QT, P * (j % QT):P * (j % QT + 1)],
                                                P4[:, i % 2, P * j:P * (j + 1)], ident[:, :])
                    m.then_inc(pe_pt4, 1)
                    pe.wait_ge(dve_pt4, NT * b + i + 1)
                    if i >= 2:
                        pe.wait_ge(dve_h4, NT * b + i)
                    for j in range(i + 1):
                        m = nc.tensor.matmul(ps[:, 6 + i % 2, 0:D], PT4[:, i % 2, j, :], V4[:, j, :],
                                             start=(j == 0), stop=(j == i))
                    m.then_inc(pe_pv4, 1)
                pe.wait_ge(dve_qk4, b + 1)
                pe.wait_ge(dve_v4, b + 1)
                scores(0)
                for i in range(1, NT):
                    scores(i)
                    weighted(i - 1)
                weighted(NT - 1)

            def causal():
                pe.wait_ge(last_in, 16 * N_LAST)
                with pe.Fori(0, NB) as b:
                    causal_batch(b)

            def rank(t, u, first):
                for k in range(2):
                    pe.wait_ge(dve_hot5, 2 * t + k + 1)
                    nc.tensor.matmul(ps[:, 4 + k, 0:NE2], tri5[:, 0, :], hotb[:, u, k, :], start=first, stop=False,
                                     skip_group_check=True).then_inc(pe_rank5, 1)
                for k in range(2):
                    pe.wait_ge(dve_rank5, 2 * t + k + 1)
                    nc.tensor.matmul(ps[:, 4 + k, 0:NE2], tri5[:, 1, :], hotb[:, u, k, :], start=False, stop=False,
                                     skip_group_check=True).then_inc(pe_count5, 1)

            def two_experts():
                route(1, wg, NE2, rank)

                def turn(j, u, first):
                    pe.wait_ge(tile5_in[u], 8 * (j - u) + 16)
                    if not first:
                        pe.wait_ge(act_xg5, j - 1)
                    for c in range(KC):
                        m = nc.tensor.transpose(ps[:, u, P * c:P * (c + 1)], xg5[:, u, P * c:P * (c + 1)], ident[:, :])
                    m.then_inc(pe_xg5, 1)

                def multiply(j, u, place, first):
                    pe.wait_ge(act_xg5, j + 1)
                    if not first:
                        pe.wait_ge(dve_y5, 2 * (j - 1))
                    for k in range(2):
                        for c in range(KC):
                            m = nc.tensor.matmul(ps[:, 2 + u, D * k:D * (k + 1)], xgT5[:, u, c, :], ring[:, place + k, c, :],
                                                 start=(c == 0), stop=(c == KC - 1))
                    m.then_inc(pe_y5, 1)

                def lap_of_ring(lap, first_lap, last_lap):
                    for k in range(RING // LOAD):
                        pe.wait_ge(ring_in[k], 16 * lap + 16)
                        for m in range(LOAD // 2):
                            j = lap * (RING // 2) + k * (LOAD // 2) + m
                            u = m % 2
                            if not (last_lap and k == RING // LOAD - 1 and m == LOAD // 2 - 1):
                                turn(j + 1, 1 - u, first_lap and k == 0 and m == 0)
                            multiply(j, u, LOAD * k + 2 * m, first_lap and k == 0)
                turn(0, 0, True)
                lap_of_ring(0, True, False)
                with pe.Fori(1, NE2 // RING - 1) as lap:
                    lap_of_ring(lap, False, False)
                lap_of_ring(NE2 // RING - 1, False, True)

            pe.wait_ge(consts_in, 16 * N_CONSTS)
            pe.nop().then_inc(pe_v, 1)
            with pe.Fori(0, NB) as b:
                attention(b)
                if STAGE >= 2:
                    scan(b)
            if STAGE >= 3:
                one_expert()
            if STAGE >= 4:
                causal()
            if STAGE >= 5:
                two_experts()

        @block.scalar
        def _(act):
            def attention(b):
                for t in range(4):
                    act.wait_ge(dve_qk32, 4 * b + t + 1)
                    nc.scalar.activation(parts[:, 0, t, :], qk32[:, t, :], ACT.Copy).then_inc(act_p1, 1)
                for t in range(4):
                    act.wait_ge(dve_res, 4 * b + t + 1)
                    nc.scalar.activation(parts[:, 1, t, :], qk32[:, t, :], ACT.Copy).then_inc(act_p2, 1)

                def exps(h, group, first):
                    if not first:
                        act.wait_ge(pe_pv, H * b + h - 1)
                    for half in range(2):
                        act.wait_ge(pe_st, 2 * (H * b + h) + half + 1)
                        nc.scalar.activation(PT[:, group, 2 * half:2 * half + 2, :], ps[:, 2 * half:2 * half + 2, :],
                                             ACT.Exp, scale=float(HD) ** -0.5).then_inc(act_exp, 1)
                exps(0, 0, True)
                exps(1, 1, True)
                with act.Fori(1, H // 2) as i:
                    exps(2 * i, 0, False)
                    exps(2 * i + 1, 1, False)

            def scan(b):
                act.wait_ge(dve_stats, b + 1)
                nc.scalar.activation(rstd[:, :], mv[:, :, 1], ACT.Sqrt).then_inc(act_std, 1)
                act.wait_ge(pe_uT, b + 1)
                for c in range(KC):
                    nc.scalar.activation(uT[:, c, 0:S], ps[:, 4 + c, :], ACT.Copy)
                nc.scalar.activation(uT[:, :, S:LP], ps[:, 6, 0:2 * P].rearrange("p (c t) -> p c t", c=KC)[:, :, 0:LP - S],
                                     ACT.Copy).then_inc(act_uT, 1)
                act.wait_ge(pe_xp, b + 1)
                nc.scalar.activation(halves(dlow[:, :]), two_banks(0, RANK), ACT.Copy).then_inc(act_dlow, 1)
                act.wait_ge(dve_sp, b + 1)
                nc.scalar.activation(sp[:, :, :], sp[:, :, :], ACT.Exp, scale=-1.0).then_inc(act_sp, 1)
                act.wait_ge(act_sp, 2 * b + 1)
                nc.scalar.activation(sp[:, :, :], sp[:, :, :], ACT.Ln, bias=1.0).then_inc(act_sp, 1)
                act.wait_ge(dve_delta, b + 1)

                def decay(n, u, first):
                    for c in range(KC):
                        if not first:
                            act.wait_ge(dve_scan, 2 * (NS * b + n - 2) + c + 1)
                        nc.scalar.activation(dA[:, u, c, :], delta[:, c, :], ACT.Exp,
                                             scale=acol[:, bass.ds(n + NS * c, 1)]).then_inc(act_dA, 1)
                    act.wait_ge(pe_bc, NS * b + n + 1)
                    if not first:
                        act.wait_ge(pool_hC, 2 * (NS * b + n - 1))
                    nc.scalar.activation(halves(Cb[:, u, :]), two_banks(2), ACT.Copy).then_inc(act_C, 1)
                decay(0, 0, True)
                decay(1, 1, True)
                with act.Fori(1, NS // 2) as i:
                    decay(2 * i, 0, False)
                    decay(2 * i + 1, 1, False)

            def normalise_rows(r, norm):
                def rows(t, u, first):
                    if not first:
                        act.wait_ge(pe_xaT, r * G + t - 1)
                        act.wait_ge(pool_xa, r * G + t - 1)
                    nc.scalar.activation(xab[:, u, :], Hs[:, t, :], ACT.Identity, bias=lbias[:, bass.ds(t, 1)],
                                         scale=lrstd[:, bass.ds(t, 1)]).then_inc(act_xab, 1)

                def turned(t, u, first):
                    act.wait_ge(pe_xaT, r * G + t + 1)
                    if not first:
                        act.wait_ge(pe_lg, r * G + t - 1)
                    nc.scalar.activation(xaT[:, u, :, :], ps[:, u, 0:D].rearrange("p (c t) -> p c t", c=KC), ACT.Copy).then_inc(act_xaT, 1)
                act.wait_ge(ln_stats, norm)
                nc.scalar.activation(lrstd[:, :], lrstd[:, :], ACT.Sqrt).then_inc(ln_std, 1)
                act.wait_ge(ln_done, norm)
                rows(0, 0, True)
                rows(1, 1, True)
                turned(0, 0, True)
                rows(2, 0, False)
                turned(1, 1, True)
                with act.Fori(1, G // 2 - 1) as i:
                    rows(2 * i + 1, 1, False)
                    turned(2 * i, 0, False)
                    rows(2 * i + 2, 0, False)
                    turned(2 * i + 1, 1, False)
                rows(G - 1, 1, False)
                turned(G - 2, 0, False)
                turned(G - 1, 1, False)

            def one_expert():
                act.wait_ge(late_in, 16 * N_LATE)
                normalise_rows(0, 1)
                act.wait_ge(dve_ex, 1)
                nc.scalar.activation(lg[:, :, :], lg[:, :, :], ACT.Exp).then_inc(act_ex, 1)

                def turned(j, u, first):
                    act.wait_ge(pe_xg, j + 1)
                    if not first:
                        act.wait_ge(pe_up, j - 1)
                    nc.scalar.activation(xgT[:, u, :, :], ps[:, u, 0:D].rearrange("p (c t) -> p c t", c=KC), ACT.Copy).then_inc(act_xg, 1)

                def gelu(j, u, first):
                    act.wait_ge(pe_up, j + 1)
                    if not first:
                        act.wait_ge(pe_hidT, j - 1)
                    nc.scalar.activation(hid[:, u, :], ps[:, 2 + u, :], ACT.Gelu).then_inc(act_gelu, 1)
                turned(0, 0, True)
                gelu(0, 0, True)
                turned(1, 1, True)
                gelu(1, 1, True)
                with act.Fori(1, MT // 2) as i:
                    turned(2 * i, 0, False)
                    gelu(2 * i, 0, False)
                    turned(2 * i + 1, 1, False)
                    gelu(2 * i + 1, 1, False)

            def causal():
                act.wait_ge(ln_stats, 2)
                nc.scalar.activation(lrstd[:, :], lrstd[:, :], ACT.Sqrt).then_inc(ln_std, 1)
                act.wait_ge(ln_done, 2)
                with act.Fori(0, NB) as b:
                    for i in range(NT):
                        nc.scalar.activation(xn4[:, i, :], Hs[:, NT * b + i, :], ACT.Identity, bias=lbias[:, bass.ds(NT * b + i, 1)],
                                             scale=lrstd[:, bass.ds(NT * b + i, 1)]).then_inc(act_xn4, 1)
                    act.wait_ge(pe_xT4, b + 1)
                    for c in range(KC):
                        nc.scalar.activation(xT4[:, c, 0:S], ps[:, c, :], ACT.Copy)
                    nc.scalar.activation(xT4[:, :, S:LT], ps[:, 2, 0:D].rearrange("p (c t) -> p c t", c=KC), ACT.Copy).then_inc(act_xT4, 1)
                    for i in range(NT):
                        act.wait_ge(dve_nm4, NT * b + i + 1)
                        if i >= 2:
                            act.wait_ge(pe_pt4, NT * b + i - 1)
                        n = P * (i + 1)
                        nc.scalar.activation(P4[:, i % 2, 0:n], ps[:, 2 * (i % 2):2 * (i % 2) + 2, :].rearrange("p b s -> p (b s)")[:, 0:n],
                                             ACT.Exp, bias=nm4[:, i:i + 1], scale=float(D) ** -0.5,
                                             accum_out=rs4[:, i:i + 1]).then_inc(act_p4, 1)

            def two_experts():
                normalise_rows(1, 3)
                act.wait_ge(dve_ex5, 1)
                nc.scalar.activation(lg5[:, :, :], lg5[:, :, :], ACT.Exp)
                nc.scalar.activation(w5[:, :, :], w5[:, :, :], ACT.Exp).then_inc(act_ex5, 1)

                def turned(j, u, first):
                    act.wait_ge(pe_xg5, j + 1)
                    if not first:
                        act.wait_ge(pe_y5, j - 1)
                    nc.scalar.activation(xgT5[:, u, :, :], ps[:, u, 0:D].rearrange("p (c t) -> p c t", c=KC), ACT.Copy).then_inc(act_xg5, 1)
                turned(0, 0, True)
                turned(1, 1, True)
                with act.Fori(1, NP2 // 2) as i:
                    turned(2 * i, 0, False)
                    turned(2 * i + 1, 1, False)

            act.wait_ge(consts_in, 16 * N_CONSTS)
            nc.scalar.activation(acol[:, :], alog[:, :], ACT.Exp).then_inc(act_acol, 1)
            act.wait_ge(dve_init, 1)
            with act.Fori(0, NB) as b:
                attention(b)
                if STAGE >= 2:
                    scan(b)
            if STAGE >= 3:
                one_expert()
            if STAGE >= 4:
                causal()
            if STAGE >= 5:
                two_experts()

        @block.gpsimd
        def _(pool):
            nc.gpsimd.memset(Hs[:, :, :].rearrange("p (b i) d -> p b i d", i=NT)[:, :, QT, :], 0.0).then_inc(pool_init, 1)
            nc.gpsimd.memset(zeros[:, :], 0.0).then_inc(pool_init, 1)
            nc.gpsimd.memset(mx[:, :, :], 0.0).then_inc(pool_init, 1)
            nc.gpsimd.memset(Vaug[:, :, :, HD:HD + 1], 1.0).then_inc(pool_init, 1)

            def output_gate(b, n, u, first):
                for c in range(KC):
                    if c == 0:
                        pool.wait_ge(act_C, NS * b + n + 1)
                        if not first:
                            pool.wait_ge(pe_y, NS * b + n - 1)
                    pool.wait_ge(dve_scan, 2 * (NS * b + n) + c + 1)
                    nc.gpsimd.tensor_tensor(hC[:, u, c, :], hst[:, u, c, :], Cb[:, u, :], ALU.mult).then_inc(pool_hC, 1)
            if STAGE >= 2:
                with pool.Fori(0, NB) as b:
                    output_gate(b, 0, 0, True)
                    output_gate(b, 1, 1, True)
                    with pool.Fori(1, NS // 2) as i:
                        output_gate(b, 2 * i, 0, False)
                        output_gate(b, 2 * i + 1, 1, False)

            def keep_rows(r, xa):
                def rows(t, u):
                    pool.wait_ge(act_xab, r * G + t + 1)
                    nc.gpsimd.tensor_copy(xa[:, t, :], xab[:, u, :]).then_inc(pool_xa, 1)
                with pool.Fori(0, G // 2) as i:
                    rows(2 * i, 0)
                    rows(2 * i + 1, 1)
            if STAGE >= 3:
                keep_rows(0, xa)
                pool.wait_ge(dve_slots, 1)
                pool.wait_ge(zero_out, 16)
                pool.wait_ge(pool_xa, G)
                for t in range(G):
                    nc.gpsimd.indirect_dma_start(xs_dram, bass.IndirectOffsetOnAxis(slots[:, t:t + 1], 0), xa[:, t, :], None,
                                                 bounds_check=MT * P - 1, oob_is_err=False).then_inc(rows_out, 16)
                pool.wait_ge(yo_out[0], 8 * MT)
                pool.wait_ge(yo_out[1], 8 * MT)
                for t in range(G):
                    if t >= YG:
                        pool.wait_ge(dve_h3, t - YG + 1)
                    nc.gpsimd.indirect_dma_start(yg[:, t % YG, :], None, ys_dram, bass.IndirectOffsetOnAxis(slotg[:, t:t + 1], 0),
                                                 bounds_check=MT * P - 1, oob_is_err=False).then_inc(yg_in[t % YG], 16)
            if STAGE >= 5:
                keep_rows(1, xa5)
                pool.wait_ge(dve_to5, 1)
                pool.wait_ge(zero5_out, 16)
                pool.wait_ge(pool_xa, 2 * G)
                for t in range(G):
                    for k in range(2):
                        nc.gpsimd.indirect_dma_start(xs5_dram, bass.IndirectOffsetOnAxis(to5[:, t, k:k + 1], 0), xa5[:, t, :], None,
                                                     bounds_check=NE2 * CAP - 1, oob_is_err=False).then_inc(rows5_out, 16)
                pool.wait_ge(y5_out[0], 8 * NP2)
                pool.wait_ge(y5_out[1], 8 * NP2)
                for n in range(2 * G):
                    if n >= 2 * YG:
                        pool.wait_ge(dve_h5, n - 2 * YG + 1)
                    nc.gpsimd.indirect_dma_start(yg5[:, n % (2 * YG), :], None, ys5_dram,
                                                 bass.IndirectOffsetOnAxis(from5[:, n // 2, n % 2:n % 2 + 1], 0),
                                                 bounds_check=NE2 * CAP - 1, oob_is_err=False).then_inc(yg5_in[n % (2 * YG)], 16)

        @block.vector
        def _(dve):
            def attention(b):
                for t in range(4):
                    dve.wait_ge(pe_qk, 4 * b + t + 1)
                    nc.vector.tensor_scalar(qk32[:, t, :], ps[:, t, :], bqk[:, t:t + 1], None, ALU.add).then_inc(dve_qk32, 1)
                for t in range(4):
                    dve.wait_ge(act_p1, 4 * b + t + 1)
                    nc.vector.tensor_tensor(qk32[:, t, :], qk32[:, t, :], parts[:, 0, t, :], ALU.subtract).then_inc(dve_res, 1)
                for t in range(4):
                    dve.wait_ge(act_p2, 4 * b + t + 1)
                    nc.vector.tensor_tensor(parts[:, 2, t, :], qk32[:, t, :], parts[:, 1, t, :], ALU.subtract).then_inc(dve_p3, 1)
                dve.wait_ge(pe_v, b + 2)
                for i in range(QT):
                    v = nc.vector.tensor_tensor(Vaug[:, i, :, 0:HD],
                                                ps[:, 4 + i // 2, D * (i % 2):D * (i % 2 + 1)].rearrange("p (h d) -> p h d", h=H),
                                                bv[:, :].rearrange("p (h d) -> p h d", h=H), ALU.add)
                v.then_inc(dve_v, 1)

                def maxima(h, group):
                    dve.wait_ge(pe_s, H * b + h + 1)
                    nc.vector.tensor_reduce(mx[:, h, :], ps[:, 4 * group:4 * group + 4, :], AX.X, ALU.max).then_inc(dve_max, 1)
                with dve.Fori(0, H // 2) as i:
                    maxima(2 * i, 0)
                    maxima(2 * i + 1, 1)
                dve.wait_ge(pe_mT, b + 1)
                nc.vector.tensor_scalar(mneg[:, :], ps[0:H * QT, 0, 0:P], -1.0, None, ALU.mult).then_inc(dve_mneg, 1)
                dve.wait_ge(dve_mneg, b + 1)
                nc.vector.tensor_copy(mparts[:, 0, :], mneg[:, :]).then_inc(dve_rsum, 1)
                dve.wait_ge(dve_rsum, (H + 4) * b + 1)
                nc.vector.tensor_tensor(mneg[:, :], mneg[:, :], mparts[:, 0, :], ALU.subtract).then_inc(dve_rsum, 1)
                dve.wait_ge(dve_rsum, (H + 4) * b + 2)
                nc.vector.tensor_copy(mparts[:, 1, :], mneg[:, :]).then_inc(dve_rsum, 1)
                dve.wait_ge(dve_rsum, (H + 4) * b + 3)
                nc.vector.tensor_tensor(mparts[:, 2, :], mneg[:, :], mparts[:, 1, :], ALU.subtract).then_inc(dve_mparts, 1)

                def normalise(h, group):
                    dve.wait_ge(pe_pv, H * b + h + 1)
                    acc = ps[:, 4 + group, 0:(HD + 1) * QT].rearrange("p (i d) -> p i d", i=QT)
                    nc.vector.reciprocal(rsum[:, group, :, :], acc[:, :, HD:HD + 1]).then_inc(dve_rsum, 1)
                    dve.wait_ge(dve_rsum, (H + 4) * b + 4 + h)
                    nc.vector.tensor_tensor(vals[:, :, bass.ds(h * HD, HD)], acc[:, :, 0:HD],
                                            rsum[:, group, :, :].to_broadcast([P, QT, HD]), ALU.mult).then_inc(dve_vals, 1)
                with dve.Fori(0, H // 2) as i:
                    normalise(2 * i, 0)
                    normalise(2 * i + 1, 1)
                dve.wait_ge(pe_vT, b + 1)
                v = nc.vector.tensor_copy(valsT[:, :, :], ps[:, 0:KC, :])
                v.then_inc(dve_vT, 1)
                dve.nop().then_inc(dve_rsum, 1)
                dve.wait_ge(pe_o, b + 1)
                for i in range(QT):
                    v = nc.vector.tensor_tensor(Hs[:, b * NT + i, :], ps[:, 2 + i // 2, D * (i % 2):D * (i % 2 + 1)],
                                                bo[:, :], ALU.add)
                v.then_inc(dve_h1, 1)

            def scan(b):
                dve.wait_ge(dve_h1, b + 1)
                nc.vector.memset(tick[:, :], 0.0)
                for i in range(NT):
                    v = nc.vector.bn_stats(st6[:, i, :], Hs[:, b * NT + i, :])
                v.then_inc(dve_bcchain, 1)
                dve.wait_ge(dve_bcchain, 7 * b + 1)
                nc.vector.memset(tick[:, :], 0.0)
                for i in range(NT):
                    v = nc.vector.bn_aggr(mv[:, i, :], st6[:, i, :])
                v.then_inc(dve_bcchain, 1)
                dve.wait_ge(dve_bcchain, 7 * b + 2)
                nc.vector.tensor_scalar(mv[:, :, 1], mv[:, :, 1], EPS, None, ALU.add).then_inc(dve_stats, 1)
                dve.wait_ge(act_std, b + 1)
                nc.vector.reciprocal(rstd[:, :], rstd[:, :]).then_inc(dve_rstd, 1)
                dve.wait_ge(dve_rstd, b + 1)
                for i in range(NT):
                    v = nc.vector.tensor_scalar(xn[:, i, :], Hs[:, b * NT + i, :], mv[:, i, 0:1], rstd[:, i:i + 1],
                                                ALU.subtract, ALU.mult)
                v.then_inc(dve_xn, 1)
                dve.wait_ge(pe_xp, b + 1)
                base = 7 * b + 2
                nc.vector.tensor_copy(halves(bc32[:, :]), two_banks(2, 96)).then_inc(dve_bcchain, 1)
                dve.wait_ge(dve_bcchain, base + 1)
                nc.vector.tensor_copy(bcp[:, 0, :], bc32[:, :]).then_inc(dve_bcchain, 1)
                dve.wait_ge(dve_bcchain, base + 2)
                nc.vector.tensor_tensor(bc32[:, :], bc32[:, :], bcp[:, 0, :], ALU.subtract).then_inc(dve_bcchain, 1)
                dve.wait_ge(dve_bcchain, base + 3)
                nc.vector.tensor_copy(bcp[:, 1, :], bc32[:, :]).then_inc(dve_bcchain, 1)
                dve.wait_ge(dve_bcchain, base + 4)
                nc.vector.tensor_tensor(bc32[:, :], bc32[:, :], bcp[:, 1, :], ALU.subtract).then_inc(dve_bcchain, 1)
                dve.wait_ge(dve_bcchain, base + 5)
                nc.vector.tensor_copy(bcs[0:32, :], bcp[0:32, 0, :])
                nc.vector.tensor_copy(bcs[32:64, :], bcp[32:64, 1, :])
                nc.vector.tensor_copy(bcs[64:96, :], bc32[64:96, :]).then_inc(dve_bcs, 1)
                dve.wait_ge(pe_dt, b + 1)
                for c in range(KC):
                    v = nc.vector.tensor_scalar(halves(xb[:, c, :]), two_banks(4 + 2 * c), dtb[:, c:c + 1], None, ALU.add)
                v.then_inc(dve_xb, 1)
                dve.wait_ge(dve_xb, b + 1)
                nc.vector.scalar_tensor_tensor(out=sp[:, :, :], in0=xb[:, :, :], scalar=-1.0, in1=xb[:, :, :],
                                               op0=ALU.mult, op1=ALU.max).then_inc(dve_sp, 1)
                dve.wait_ge(act_sp, 2 * b + 2)
                nc.vector.scalar_tensor_tensor(out=delta[:, :, :], in0=xb[:, :, :], scalar=0.0, in1=sp[:, :, :],
                                               op0=ALU.max, op1=ALU.add).then_inc(dve_delta, 1)
                dve.wait_ge(dve_delta, b + 1)
                dve.wait_ge(act_uT, b + 1)
                nc.vector.tensor_tensor(dtu[:, :, :], delta[:, :, :], uT[:, :, :], ALU.mult).then_inc(dve_dtu, 1)
                dve.wait_ge(dve_dtu, b + 1)

                def recurrence(n, u, first):
                    dve.wait_ge(pe_bc, NS * b + n + 1)
                    for c in range(KC):
                        v = nc.vector.tensor_tensor(halves(dBu[:, u, c, :]), halves(dtu[:, c, :]), two_banks(0), ALU.mult)
                    v.then_inc(dve_dBu, 1)
                    dve.wait_ge(dve_dBu, NS * b + n + 1)
                    if not first:
                        dve.wait_ge(pool_hC, 2 * (NS * b + n - 1))
                    for c in range(KC):
                        dve.wait_ge(act_dA, 2 * (NS * b + n) + c + 1)
                        nc.vector.tensor_tensor_scan(hst[:, u, c, :], dA[:, u, c, :], dBu[:, u, c, :], 0.0,
                                                     ALU.mult, ALU.add).then_inc(dve_scan, 1)
                recurrence(0, 0, True)
                recurrence(1, 1, True)
                with dve.Fori(1, NS // 2) as i:
                    recurrence(2 * i, 0, False)
                    recurrence(2 * i + 1, 1, False)
                dve.wait_ge(pe_y, NS * (b + 1))
                for c in range(KC):
                    v = nc.vector.scalar_tensor_tensor(out=halves(xb[:, c, :]), in0=halves(uT[:, c, :]), scalar=dsk[:, c:c + 1],
                                                       in1=two_banks(4 + 2 * c), op0=ALU.mult, op1=ALU.add)
                v.then_inc(dve_yT, 1)
                dve.wait_ge(pe_yT, b + 1)
                for i in range(NT):
                    rows = P if i < QT else TXT
                    v = nc.vector.tensor_tensor(Hs[0:rows, b * NT + i, :], Hs[0:rows, b * NT + i, :],
                                                ps[0:rows, i // 2, D * (i % 2):D * (i % 2 + 1)], ALU.add)
                v.then_inc(dve_h2, 1)

            def layer_norm(r):
                with dve.Fori(0, G) as t:
                    v = nc.vector.bn_stats(lst[:, t, :], Hs[:, t, :])
                    v.then_inc(ln_chain, 1)
                n = [(r + 1) * G + 6 * r]
                dve.wait_ge(ln_chain, n[0])

                def link(ins):
                    n[0] += 1
                    ins.then_inc(ln_chain, 1)
                    dve.wait_ge(ln_chain, n[0])
                m0, m1, q0, q1 = (lst[:, :, k] for k in (1, 4, 2, 5))
                link(nc.vector.tensor_tensor(lmean[:, :], m0, m1, ALU.add))
                link(nc.vector.tensor_tensor(ltmp[:, :], m0, m1, ALU.subtract))
                link(nc.vector.scalar_tensor_tensor(out=ltmp[:, :], in0=ltmp[:, :], scalar=0.25, in1=ltmp[:, :],
                                                    op0=ALU.mult, op1=ALU.mult))
                link(nc.vector.tensor_tensor(lrstd[:, :], q0, q1, ALU.add))
                link(nc.vector.scalar_tensor_tensor(out=lrstd[:, :], in0=lrstd[:, :], scalar=1.0 / D, in1=ltmp[:, :],
                                                    op0=ALU.mult, op1=ALU.add))
                nc.vector.tensor_scalar(lrstd[:, :], lrstd[:, :], EPS, None, ALU.add).then_inc(ln_stats, 1)
                dve.wait_ge(ln_std, r + 1)
                link(nc.vector.reciprocal(lrstd[:, :], lrstd[:, :]))
                nc.vector.scalar_tensor_tensor(out=lbias[:, :], in0=lmean[:, :], scalar=-0.5, in1=lrstd[:, :],
                                               op0=ALU.mult, op1=ALU.mult).then_inc(ln_done, 1)

            def choose(r, n_experts, lgb, lg, then=None):
                def tile(t, u):
                    dve.wait_ge(pe_lg, r * G + t + 1)
                    nc.vector.tensor_copy(lgb[:, u, :], ps[:, 2 + u, 0:n_experts]).then_inc(dve_lg, 1)
                    dve.wait_ge(dve_lg, r * G + t + 1)
                    nc.vector.tensor_copy(lg[:, t, :], lgb[:, u, :])
                    nc.vector.max(m8b[:, u, :], lgb[:, u, :]).then_inc(best_chain, 1)
                    dve.wait_ge(best_chain, 3 * (r * G + t) + 1)
                    nc.vector.tensor_copy(best[:, t, :], m8b[:, u, 0:2])
                    nc.vector.max_index(i8b[:, u, :], m8b[:, u, :], lgb[:, u, :]).then_inc(best_chain, 1)
                    dve.wait_ge(best_chain, 3 * (r * G + t) + 2)
                    nc.vector.tensor_copy(besti[:, t, :], i8b[:, u, 0:2]).then_inc(best_chain, 1)
                    if then:
                        dve.wait_ge(best_chain, 3 * (r * G + t) + 3)
                        then(t, u)
                with dve.Fori(0, G // 2) as i:
                    tile(2 * i, 0)
                    tile(2 * i + 1, 1)
                dve.wait_ge(best_chain, 3 * (r + 1) * G)

            def one_expert():
                n = [0]

                def link(ins):
                    n[0] += 1
                    ins.then_inc(c3, 1)
                    dve.wait_ge(c3, n[0])
                dve.wait_ge(dve_h2, NB + 1)
                layer_norm(0)
                dve.wait_ge(b12_in, 16)
                nc.vector.tensor_copy(b12p[:, 0, :], b12[:, :]).then_inc(dve_bparts, 1)
                dve.wait_ge(dve_bparts, 1)
                link(nc.vector.tensor_tensor(b12[:, :], b12[:, :], b12p[:, 0, :], ALU.subtract))
                nc.vector.tensor_copy(b12p[:, 1, :], b12[:, :]).then_inc(dve_bparts, 1)
                dve.wait_ge(dve_bparts, 2)
                nc.vector.tensor_tensor(b12p[:, 2, :], b12[:, :], b12p[:, 1, :], ALU.subtract).then_inc(dve_bparts, 1)
                dve.wait_ge(late_in, 16 * N_LATE)
                choose(0, NE1, lgb, lg)
                flat = [P, G, NE1]
                link(nc.vector.tensor_tensor(hot[:, :, :], iota1[:, :].rearrange("p (o e) -> p o e", o=1).to_broadcast(flat),
                                             besti[:, :, 0:1].to_broadcast(flat), ALU.is_equal))
                nc.vector.tensor_tensor(hot[:, :, :], hot[:, :, :], real[:, :].rearrange("p (g o) -> p g o", o=1).to_broadcast(flat),
                                        ALU.mult).then_inc(dve_hot, 1)
                nc.vector.tensor_tensor(lg[:, :, :], lg[:, :, :], best[:, :, 0:1].to_broadcast(flat), ALU.subtract).then_inc(dve_ex, 1)
                dve.wait_ge(pe_rank, 1)
                link(nc.vector.tensor_copy(cnt[:, :, :], ps[:, 5, 0:G * NE1].rearrange("p (g e) -> p e g", e=NE1)))
                link(nc.vector.tensor_tensor_scan(cum[:, :, :].rearrange("p e g -> p (e g)"), keep[:, :],
                                                  cnt[:, :, :].rearrange("p e g -> p (e g)"), 0.0, ALU.mult, ALU.add))
                steps = [P, NE1, G]
                link(nc.vector.tensor_tensor(big[:, :, 0:G], cum[:, :, G - 1:G].to_broadcast(steps),
                                             iota128[:, :].rearrange("p (o g) -> p o g", o=1).to_broadcast(steps), ALU.is_gt))
                link(nc.vector.tensor_reduce(ntile[:, :], big[:, :, 0:G], AX.X, ALU.add))
                link(nc.vector.memset(toff[:, :], 1.0))
                link(nc.vector.tensor_tensor_scan(tend[:, :], toff[:, :], ntile[:, :], 0.0, ALU.mult, ALU.add))
                link(nc.vector.tensor_tensor(toff[:, :], tend[:, :], ntile[:, :], ALU.subtract))
                link(nc.vector.tensor_scalar(toff[:, :], toff[:, :], float(P), None, ALU.mult))
                link(nc.vector.tensor_tensor(cum[:, :, :], cum[:, :, :], cnt[:, :, :], ALU.subtract))
                link(nc.vector.tensor_tensor(cum[:, :, :], cum[:, :, :], toff[:, :].rearrange("p (e o) -> p e o", o=1).to_broadcast(steps), ALU.add))
                link(nc.vector.tensor_tensor(pos[:, :, :], cum[:, :, :].rearrange("p e g -> p g e"),
                                             ps[:, 4, 0:G * NE1].rearrange("p (g e) -> p g e", e=NE1), ALU.add))
                link(nc.vector.tensor_tensor(pos[:, :, :], pos[:, :, :], hot[:, :, :], ALU.mult))
                link(nc.vector.tensor_reduce(slotf[:, :], pos[:, :, :], AX.X, ALU.add))
                link(nc.vector.tensor_copy(slotg[:, :], slotf[:, :]))
                nc.vector.tensor_tensor(slots[:, :], slotf[:, :], nottoken[:, :], ALU.add).then_inc(dve_slots, 1)
                pairs = [P, MT, NE1]
                which = big[:, :, :].rearrange("p a b -> p (a b)").rearrange("p (m e) -> p m e", e=NE1)
                link(nc.vector.tensor_tensor(which, tend[:, :].rearrange("p (o e) -> p o e", o=1).to_broadcast(pairs),
                                             ramp[:, :].rearrange("p (m o) -> p m o", o=1).to_broadcast(pairs), ALU.is_le))
                link(nc.vector.tensor_reduce(te[:, :], which, AX.X, ALU.add))
                nc.vector.tensor_scalar(tei[:, :], te[:, :], float(NE1 - 1), None, ALU.min).then_inc(dve_te, 1)
                dve.wait_ge(act_ex, 1)
                link(nc.vector.tensor_reduce(gate[:, :], lg[:, :, :], AX.X, ALU.add))
                link(nc.vector.reciprocal(gate[:, :], gate[:, :]))
                link(nc.vector.tensor_tensor(gate[:, :], gate[:, :], real[:, :], ALU.mult))

                def step(j, u, first):
                    dve.wait_ge(pe_hidT, j + 1)
                    if not first:
                        dve.wait_ge(pe_down, j - 1)
                    nc.vector.tensor_copy(hidT[:, u, :, :], ps[:, 4 + u, :].rearrange("p (f t) -> p f t", f=FC)).then_inc(dve_hidT, 1)
                    dve.wait_ge(pe_down, j + 1)
                    if not first:
                        dve.wait_ge(yo_out[u], 8 * (j - u))
                    nc.vector.tensor_copy(yo[:, u, :], ps[:, 6 + u, 0:D]).then_inc(dve_yo, 1)
                step(0, 0, True)
                step(1, 1, True)
                with dve.Fori(1, MT // 2) as i:
                    step(2 * i, 0, False)
                    step(2 * i + 1, 1, False)
                for t in range(G):
                    dve.wait_ge(yg_in[t % YG], 16 * (t // YG + 1))
                    nc.vector.scalar_tensor_tensor(out=Hs[:, t, :], in0=yg[:, t % YG, :], scalar=gate[:, t:t + 1], in1=Hs[:, t, :],
                                                   op0=ALU.mult, op1=ALU.add).then_inc(dve_h3, 1)

            def causal():
                dve.wait_ge(dve_h3, G)
                layer_norm(1)
                dve.nop().then_inc(dve_h4, 1)
                dve.wait_ge(last_in, 16 * N_LAST)
                with dve.Fori(0, NB) as b:
                    dve.wait_ge(pe_qk4, b + 1)
                    for t in range(4):
                        nc.vector.tensor_scalar(QK4[:, t, 0:S], ps[:, t, :], bqk4[:, t:t + 1], None, ALU.add)
                        v = nc.vector.tensor_scalar(QK4[:, t, S:LT], ps[:, 4, P * t:P * (t + 1)], bqk4[:, t:t + 1], None, ALU.add)
                    v.then_inc(dve_qk4, 1)
                    dve.wait_ge(pe_v4, b + 1)
                    for i in range(NT):
                        v = nc.vector.tensor_tensor(V4[:, i, :], ps[:, 5 + i // 2, D * (i % 2):D * (i % 2 + 1)], bv4[:, :], ALU.add)
                    v.then_inc(dve_v4, 1)

                    def maxima(i):
                        dve.wait_ge(pe_s4, NT * b + i + 1)
                        row = ps[:, 2 * (i % 2):2 * (i % 2) + 2, :].rearrange("p b s -> p (b s)")
                        nc.vector.tensor_tensor(row[:, P * i:P * (i + 1)], row[:, P * i:P * (i + 1)], mask4[:, :],
                                                ALU.add).then_inc(dve_mask4, 1)
                        dve.wait_ge(dve_mask4, 2 * (NT * b + i) + 1)
                        nc.vector.tensor_reduce(nm4[:, i:i + 1], row[:, 0:P * (i + 1)], AX.X, ALU.max).then_inc(dve_mask4, 1)
                        dve.wait_ge(dve_mask4, 2 * (NT * b + i) + 2)
                        nc.vector.tensor_scalar(nm4[:, i:i + 1], nm4[:, i:i + 1], -float(D) ** -0.5, None, ALU.mult).then_inc(dve_nm4, 1)

                    def weighted(i):
                        dve.wait_ge(pe_pt4, NT * b + i + 1)
                        n = P * (i + 1)
                        nc.vector.tensor_copy(PT4[:, i % 2, 0:i + 1, :].rearrange("p j q -> p (j q)"),
                                              ps[:, 4:6, :].rearrange("p b s -> p (b s)")[:, 0:n]).then_inc(dve_pt4, 1)
                        dve.wait_ge(pe_pv4, NT * b + i + 1)
                        nc.vector.reciprocal(rs4[:, i:i + 1], rs4[:, i:i + 1]).then_inc(dve_rs4, 1)
                        dve.wait_ge(dve_rs4, NT * b + i + 1)
                        nc.vector.scalar_tensor_tensor(out=Hs[:, NT * b + i, :], in0=ps[:, 6 + i % 2, 0:D], scalar=rs4[:, i:i + 1],
                                                       in1=Hs[:, NT * b + i, :], op0=ALU.mult, op1=ALU.add).then_inc(dve_h4, 1)
                    maxima(0)
                    for i in range(1, NT):
                        maxima(i)
                        weighted(i - 1)
                    weighted(NT - 1)

            def two_experts():
                n = [0]

                def link(ins):
                    n[0] += 1
                    ins.then_inc(c5, 1)
                    dve.wait_ge(c5, n[0])
                dve.wait_ge(dve_h4, G + 1)
                layer_norm(2)

                def rank(t, u):
                    for k in range(2):
                        nc.vector.tensor_scalar(hotb[:, u, k, :], iota5[:, :], besti[:, t, k:k + 1], real5[:, bass.ds(t, 1)],
                                                ALU.is_equal, ALU.mult).then_inc(dve_hot5, 1)
                    for k in range(2):
                        dve.wait_ge(pe_rank5, 2 * t + k + 1)
                        nc.vector.tensor_tensor_reduce(out=junk[:, :], in0=hotb[:, u, k, :], in1=ps[:, 4 + k, 0:NE2], scale=1.0, scalar=0.0,
                                                       op0=ALU.mult, op1=ALU.add, accum_out=locb[:, u, k:k + 1]).then_inc(dve_rank5, 1)
                        dve.wait_ge(dve_rank5, 2 * t + k + 1)
                    nc.vector.tensor_copy(hot2[:, t, :], hotb[:, u, 1, :])
                    nc.vector.tensor_copy(loc[:, t, :], locb[:, u, :])
                    dve.wait_ge(pe_count5, 2 * t + 2)
                choose(1, NE2, lgb5, lg5, rank)
                flat = [P, G, NE2]
                link(nc.vector.tensor_copy(c1[:, :], ps[:, 4, 0:NE2]))
                link(nc.vector.tensor_tensor(lg5[:, :, :], lg5[:, :, :], best[:, :, 0:1].to_broadcast(flat), ALU.subtract))
                nc.vector.tensor_tensor(w5[:, :, :], best[:, :, :], best[:, :, 0:1].to_broadcast([P, G, 2]), ALU.subtract).then_inc(dve_ex5, 1)
                link(nc.vector.tensor_tensor(hot2f[:, :, :], hot2[:, :, :], c1[:, :].rearrange("p (o e) -> p o e", o=1).to_broadcast(flat), ALU.mult))
                link(nc.vector.tensor_reduce(den[:, :], hot2f[:, :, :], AX.X, ALU.add))
                link(nc.vector.tensor_tensor(loc[:, :, 1], loc[:, :, 1], den[:, :], ALU.add))
                link(nc.vector.tensor_scalar(v5[:, :, :], loc[:, :, :], float(CAP), None, ALU.is_lt))
                link(nc.vector.tensor_scalar(loc[:, :, :], loc[:, :, :], float(CAP - 1), None, ALU.min))
                link(nc.vector.scalar_tensor_tensor(out=rowf[:, :, :], in0=besti[:, :, :], scalar=float(CAP), in1=loc[:, :, :],
                                                    op0=ALU.mult, op1=ALU.add))
                link(nc.vector.tensor_copy(from5[:, :, :], rowf[:, :, :]))
                link(nc.vector.tensor_tensor(rowf[:, :, :], rowf[:, :, :],
                                             nottoken5[:, :].rearrange("p (g o) -> p g o", o=1).to_broadcast([P, G, 2]), ALU.add))
                link(nc.vector.scalar_tensor_tensor(out=rowf[:, :, :], in0=v5[:, :, :], scalar=-1e6, in1=rowf[:, :, :],
                                                    op0=ALU.mult, op1=ALU.add))
                nc.vector.tensor_scalar(to5[:, :, :], rowf[:, :, :], 1e6, None, ALU.add).then_inc(dve_to5, 1)
                dve.wait_ge(act_ex5, 1)
                link(nc.vector.tensor_reduce(den[:, :], lg5[:, :, :], AX.X, ALU.add))
                link(nc.vector.reciprocal(den[:, :], den[:, :]))
                link(nc.vector.tensor_tensor(w5[:, :, :], w5[:, :, :], den[:, :].rearrange("p (g o) -> p g o", o=1).to_broadcast([P, G, 2]), ALU.mult))
                link(nc.vector.tensor_reduce(den[:, :], w5[:, :, :], AX.X, ALU.add))
                link(nc.vector.tensor_scalar(den[:, :], den[:, :], FEPS, None, ALU.max))
                link(nc.vector.reciprocal(den[:, :], den[:, :]))
                link(nc.vector.tensor_tensor(w5[:, :, :], w5[:, :, :], den[:, :].rearrange("p (g o) -> p g o", o=1).to_broadcast([P, G, 2]), ALU.mult))
                link(nc.vector.tensor_tensor(w5[:, :, :], w5[:, :, :], v5[:, :, :], ALU.mult))

                def step(j, u, first):
                    dve.wait_ge(pe_y5, j + 1)
                    if not first:
                        dve.wait_ge(y5_out[u], 8 * (j - u))
                    for k in range(2):
                        nc.vector.tensor_copy(yo5[CAP * k:CAP * (k + 1), u, :], ps[CAP * k:CAP * (k + 1), 2 + u, D * k:D * (k + 1)]).then_inc(dve_y5, 1)
                step(0, 0, True)
                step(1, 1, True)
                with dve.Fori(1, NP2 // 2) as i:
                    step(2 * i, 0, False)
                    step(2 * i + 1, 1, False)
                for m in range(2 * G):
                    dve.wait_ge(yg5_in[m % (2 * YG)], 16 * (m // (2 * YG) + 1))
                    if m % 2:
                        dve.wait_ge(dve_h5, m)
                    nc.vector.scalar_tensor_tensor(out=Hs[:, m // 2, :], in0=yg5[:, m % (2 * YG), :], scalar=w5[:, m // 2, m % 2:m % 2 + 1],
                                                   in1=Hs[:, m // 2, :], op0=ALU.mult, op1=ALU.add).then_inc(dve_h5, 1)

            dve.wait_ge(act_acol, 1)
            nc.vector.tensor_scalar(acol[:, :], acol[:, :], -1.0, None, ALU.mult).then_inc(dve_init, 1)
            dve.wait_ge(consts_in, 16 * N_CONSTS)
            dve.wait_ge(txt_in, 16 * NB)
            dve.wait_ge(pool_init, 4)
            dve.nop().then_inc(dve_h2, 1)
            with dve.Fori(0, NB) as b:
                attention(b)
                if STAGE >= 2:
                    scan(b)
                else:
                    dve.wait_ge(dve_h1, b + 1)
                    dve.nop().then_inc(dve_h2, 1)
            if STAGE >= 3:
                one_expert()
            if STAGE >= 4:
                causal()
            if STAGE >= 5:
                two_experts()


def layouts(x, txt, L0_tok_w_qkv, L0_tok_b_qkv, L0_tok_w_out, L0_tok_b_out, L0_attn_A_log, L0_attn_D_skip,
            L0_attn_dt_proj_w, L0_attn_dt_proj_b, L0_attn_x_proj_w, L0_ffn_router_w, L0_ffn_w1, L0_ffn_b1, L0_ffn_w2,
            L0_ffn_b2, L1_attn_Wq, L1_attn_bq, L1_attn_Wk, L1_attn_bk, L1_attn_Wv, L1_attn_bv, L1_ffn_wg, L1_ffn_we):
    import numpy as np

    def c(a):
        return np.ascontiguousarray(np.asarray(a))

    def ones_bf16(a):
        return (np.asarray(a) * 0x3F80).astype(np.uint16)

    def chunked(a):
        return c(np.asarray(a).reshape(-1, 128, a.shape[1]).transpose(1, 0, 2))

    def columns(v):
        return c(np.asarray(v).reshape(-1, 128).T)

    w = np.asarray(L0_tok_w_qkv).reshape(16, 3, 16, 256)
    bq = np.asarray(L0_tok_b_qkv).reshape(16, 3, 16)
    xp = np.asarray(L0_attn_x_proj_w)
    sel = np.zeros((96, 32, 128))
    for n in range(32):
        sel[n::32, n] = 1
    token = (np.arange(20) % 5 * 128 + np.arange(128)[:, None] < 589) * 1.0

    def rows(v):
        return np.tile(np.asarray(v, np.float32), (128, 1))
    return {
        "xT": c(np.asarray(x)[:, 0].transpose(0, 2, 1).reshape(4, 2, 128, 512).transpose(0, 2, 1, 3)),
        "txt": c(txt),
        "wqkvT": chunked(w.transpose(1, 0, 2, 3).reshape(768, 256).T),
        "bqk": columns(bq[:, 0:2].transpose(1, 0, 2).reshape(512)),
        "bv": c(bq[:, 2].reshape(256)),
        "woT": chunked(np.asarray(L0_tok_w_out).T),
        "bo": c(L0_tok_b_out),
        "ident": np.eye(128, dtype=np.float32),
        "ones3": ones_bf16(np.ones((3, 16, 512))),
        "xpwT": chunked(xp[:64].T),
        "xpbcT": chunked(np.concatenate([xp[64:]] * 3).T),
        "dtwT": c(np.asarray(L0_attn_dt_proj_w).T),
        "dtb": columns(L0_attn_dt_proj_b),
        "dsk": columns(L0_attn_D_skip),
        "alog": c(np.asarray(L0_attn_A_log).reshape(2, 128, 16).transpose(1, 0, 2).reshape(128, 32)),
        "sel": ones_bf16(sel),
        "w1": c(np.asarray(L0_ffn_w1).reshape(14, 2, 128, 512).transpose(2, 0, 1, 3)),
        "w2": c(np.asarray(L0_ffn_w2).reshape(14, 4, 128, 256).transpose(2, 0, 1, 3)),
        "b12": c(np.concatenate([np.asarray(L0_ffn_b1), np.asarray(L0_ffn_b2)], 1)),
        "rw": chunked(np.asarray(L0_ffn_router_w)),
        "tri": ones_bf16(np.triu(np.ones((128, 128)), 1)),
        "onesm": ones_bf16(np.ones((128, 128))),
        "real": token.astype(np.float32),
        "nottoken": ((1 - token) * 1e6).astype(np.float32),
        "iota1": rows(np.arange(14)),
        "iota128": rows(np.arange(20) * 128),
        "ramp": rows(np.arange((4 * 589 + 14 * 127) // 128)),
        "keep1": rows(np.arange(14 * 20) % 20 != 0),
        "w4T": chunked(np.concatenate([np.asarray(L1_attn_Wq), np.asarray(L1_attn_Wk), np.asarray(L1_attn_Wv)]).T),
        "bqk4": columns(np.concatenate([np.asarray(L1_attn_bq), np.asarray(L1_attn_bk)])),
        "bv4": c(L1_attn_bv),
        "mask4": np.triu(np.full((128, 128), -3e38, np.float32), 1),
        "wg": chunked(np.asarray(L1_ffn_wg)),
        "we": c(np.asarray(L1_ffn_we).reshape(128, 2, 128, 256).transpose(2, 0, 1, 3)),
        "tri5": ones_bf16(np.stack([np.triu(np.ones((128, 128)), 1), np.tril(np.ones((128, 128)))], 1)),
        "iota5": rows(np.arange(128)),
        "ones3p": ones_bf16(np.ones((3, 128))),
    }


def kernel(**inputs):
    import numpy as _np
    import concourse.bacc as _bacc
    from concourse import mybir as _mybir
    from concourse.bass_utils import run_bass_kernel_spmd as _run

    nc = _bacc.Bacc("TRN2", target_bir_lowering=False, num_devices=1)
    arrays = layouts(**inputs)
    args = {n: nc.dram_tensor(f"in_{n}", a.shape, _mybir.dt.from_np(a.dtype), kind="ExternalInput").ap() for n, a in arrays.items()}
    out = nc.dram_tensor("out", (4, 589, 256), _mybir.dt.float32, kind="ExternalOutput").ap()
    fusion_kernel(nc, args, out)
    r = _run(nc, [{f"in_{n}": a for n, a in arrays.items()}], core_ids=[0])
    return r.results[0]["out"]
```

```python
import concourse.bass as bass
from concourse import mybir
from contextlib import ExitStack

STAGE = 5


def fusion_kernel(nc, A, out):
    F32, BF16, FP16, U32 = mybir.dt.float32, mybir.dt.bfloat16, mybir.dt.float16, mybir.dt.uint32
    ALU, ACT, AX = mybir.AluOpType, mybir.ActivationFunctionType, mybir.AxisListType

    P = 128
    NB, S, D = 4, 512, 256
    TXT = 77
    L = S + TXT
    LP = L + 1
    HC = LP // 2
    KC = D // P
    QT = S // P
    NT = QT + 1
    H, HD = 16, D // 16
    PART = 6 * HD
    KR = PART + 3
    VW = HD + 1
    NU = 2 * H
    NS = 16
    RANK = 64
    EPS = 1e-5
    LT = NT * P
    NE2, CAP = 128, 64
    NP2 = NE2 // 2
    RING, LOAD = 32, 4
    FEPS = 1.1920928955078125e-07
    YG = 4
    NE1, FF = 14, 512
    FC = FF // P
    MT = (NB * L + NE1 * (P - 1)) // P
    QPARTS = [0, 0, 1, 1, 0, 2]
    KPARTS = [0, 1, 0, 1, 2, 0]

    ctx = ExitStack()
    with ctx:
        def sb(name, shape, dt=F32):
            return ctx.enter_context(nc.sbuf_tensor(name, shape, dt))

        def sem(name):
            return ctx.enter_context(nc.semaphore(name))

        def dram(name, shape, dt=F32):
            return nc.dram_tensor(name, shape, dt).ap()

        ps = ctx.enter_context(nc.psum_tensor("ps", [P, 8, 512], F32))

        Hs = sb("Hs", [P, NB * NT, D])
        ident = sb("ident", [P, P])
        zeros = sb("zeros", [P, D])
        G = NB * NT
        lst = sb("lst", [P, G, 6])
        lmean = sb("lmean", [P, G])
        lrstd = sb("lrstd", [P, G])
        ltmp = sb("ltmp", [P, G])
        lbias = sb("lbias", [P, G])
        xab = sb("xab", [P, 2, D])
        xaT = sb("xaT", [P, 2, KC, P])
        m8b = sb("m8b", [P, 2, 8])
        i8b = sb("i8b", [P, 2, 8], U32)
        best = sb("best", [P, G, 2])
        besti = sb("besti", [P, G, 2])
        early = ExitStack()

        def eb(name, shape, dt=F32):
            return early.enter_context(nc.sbuf_tensor(name, shape, dt))
        xT = eb("xT", [P, KC, S])
        wqkv = eb("wqkv", [P, KC, 3 * D])
        wo = eb("wo", [P, KC, D])
        bqk = eb("bqk", [P, 4])
        bv = eb("bv", [P, D])
        bo = eb("bo", [P, D])
        Qst = eb("Qst", [KR, H, S], BF16)
        Kst = eb("Kst", [KR, H, S], BF16)
        v32 = eb("v32", [P, QT, D])
        Vst = eb("Vst", [P, QT, H, P], BF16)
        sel3 = eb("sel3", [P, 2 * VW])
        OT = eb("OT", [P, 2, S])
        qk32 = eb("qk32", [P, 4, S])
        parts = eb("parts", [P, 3, 4, S], BF16)
        mx = eb("mx", [P, P // QT, QT])
        mneg = eb("mneg", [H * QT, P])
        mparts = eb("mparts", [H * QT, 3, P], BF16)
        rsum = eb("rsum", [P, 2, QT, 2, 1])
        vals = eb("vals", [P, QT, D])
        valsT = eb("valsT", [P, KC, S])
        xpw = eb("xpw", [P, KC, RANK])
        xpbc = eb("xpbc", [P, KC, 96])
        dtw = eb("dtw", [RANK, D])
        dtb = eb("dtb", [P, KC])
        dsk = eb("dsk", [P, KC])
        alog = eb("alog", [P, KC * NS])
        acol = eb("acol", [P, KC * NS])
        sel = eb("sel", [96, 2 * NS, P], BF16)
        tick = eb("tick", [P, 1])
        st6 = eb("st6", [P, NT, 6])
        mv = eb("mv", [P, NT, 2])
        rstd = eb("rstd", [P, NT])
        xn = eb("xn", [P, NT, D])
        uT = eb("uT", [P, KC, LP])
        dlow = eb("dlow", [RANK, LP])
        bcs = eb("bcs", [96, LP], BF16)
        xb = eb("xb", [P, KC, LP])
        delta = eb("delta", [P, KC, LP])
        dtu = eb("dtu", [P, KC, LP])
        Cb = eb("Cb", [P, 2, LP])

        turn1, turn2 = ExitStack(), ExitStack()
        P32 = turn1.enter_context(nc.sbuf_tensor("P32", [P, 4, 2, S], F32))
        Phl = turn1.enter_context(nc.sbuf_tensor("Phl", [P, 4, 2, 2, S], FP16))
        turn1.close()
        dA = turn2.enter_context(nc.sbuf_tensor("dA", [P, 2, KC, LP], F32))
        dBu = turn2.enter_context(nc.sbuf_tensor("dBu", [P, 2, KC, LP], F32))
        hst = turn2.enter_context(nc.sbuf_tensor("hst", [P, 2, KC, LP], F32))
        hC = turn2.enter_context(nc.sbuf_tensor("hC", [P, 2, KC, LP], F32))
        turn2.close()
        turn2 = ExitStack()
        turn2.enter_context(nc.sbuf_tensor("skip_dA", [P, 4, KC, LP], F32))
        bc32 = turn2.enter_context(nc.sbuf_tensor("bc32", [96, LP], F32))
        bcp = turn2.enter_context(nc.sbuf_tensor("bcp", [96, 2, LP], BF16))
        sp = turn2.enter_context(nc.sbuf_tensor("sp", [P, KC, LP], F32))
        turn2.close()
        early.close()
        late = ExitStack()

        def lb(name, shape, dt=F32):
            return late.enter_context(nc.sbuf_tensor(name, shape, dt))
        W1 = lb("W1", [P, NE1, KC, FF])
        W2 = lb("W2", [P, NE1, FC, D])
        b12 = lb("b12", [NE1, FF + D])
        b12p = lb("b12p", [NE1, 3, FF + D], BF16)
        brow = lb("brow", [3, NE1, FF + D], BF16)
        ones3 = lb("ones3", [3, P], BF16)
        rw = lb("rw", [P, KC, NE1])
        tri = lb("tri", [P, P], BF16)
        onesm = lb("onesm", [P, P], BF16)
        real = lb("real", [P, G])
        iota1 = lb("iota1", [P, NE1])
        iota128 = lb("iota128", [P, G])
        ramp = lb("ramp", [P, MT])
        keep = lb("keep", [P, NE1 * G])
        lg = lb("lg", [P, G, NE1])
        lgb = lb("lgb", [P, 2, NE1])
        nottoken = lb("nottoken", [P, G])
        hot = lb("hot", [P, G, NE1], BF16)
        cnt = lb("cnt", [P, NE1, G])
        cum = lb("cum", [P, NE1, G])
        big = lb("big", [P, NE1, MT])
        ntile = lb("ntile", [P, NE1])
        tend = lb("tend", [P, NE1])
        toff = lb("toff", [P, NE1])
        pos = lb("pos", [P, G, NE1])
        slotf = lb("slotf", [P, G])
        slots = lb("slots", [P, G], U32)
        slotg = lb("slotg", [P, G], U32)
        te = lb("te", [P, MT])
        tei = lb("tei", [P, MT], U32)
        gate = lb("gate", [P, G])
        turn3 = ExitStack()
        xa = turn3.enter_context(nc.sbuf_tensor("xa", [P, G, D], F32))
        turn3.close()
        xg = lb("xg", [P, 2, D])
        xgT = lb("xgT", [P, 2, KC, P])
        hid = lb("hid", [P, 2, FF])
        hidT = lb("hidT", [P, 2, FC, P])
        yo = lb("yo", [P, 2, D])
        yg = lb("yg", [P, YG, D])
        late.close()
        last = ExitStack()

        def tb(name, shape, dt=F32):
            return last.enter_context(nc.sbuf_tensor(name, shape, dt))
        ring = tb("ring", [P, RING, KC, D])
        w4 = tb("w4", [P, KC, 3 * D])
        bqk4 = tb("bqk4", [P, 4])
        bv4 = tb("bv4", [P, D])
        mask4 = tb("mask4", [P, P])
        wg = tb("wg", [P, KC, NE2])
        xn4 = tb("xn4", [P, NT, D])
        xT4 = tb("xT4", [P, KC, LT])
        QK4 = tb("QK4", [P, 4, LT])
        V4 = tb("V4", [P, NT, D])
        P4 = tb("P4", [P, 2, LT])
        PT4 = tb("PT4", [P, 2, NT, P])
        nm4 = tb("nm4", [P, NT])
        rs4 = tb("rs4", [P, NT])
        tri5 = tb("tri5", [P, 2, P], BF16)
        real5 = tb("real5", [P, G])
        nottoken5 = tb("nottoken5", [P, G])
        iota5 = tb("iota5", [P, NE2])
        lgb5 = tb("lgb5", [P, 2, NE2])
        lg5 = tb("lg5", [P, G, NE2])
        hotb = tb("hotb", [P, 2, 2, NE2], BF16)
        hot2 = tb("hot2", [P, G, NE2], BF16)
        hot2f = tb("hot2f", [P, G, NE2])
        junk = tb("junk", [P, NE2])
        locb = tb("locb", [P, 2, 2])
        loc = tb("loc", [P, G, 2])
        c1 = tb("c1", [P, NE2])
        w5 = tb("w5", [P, G, 2])
        v5 = tb("v5", [P, G, 2])
        den = tb("den", [P, G])
        rowf = tb("rowf", [P, G, 2])
        to5 = tb("to5", [P, G, 2], U32)
        from5 = tb("from5", [P, G, 2], U32)
        turn4 = ExitStack()
        xa5 = turn4.enter_context(nc.sbuf_tensor("xa5", [P, G, D], F32))
        turn4.close()
        xg5 = tb("xg5", [P, 2, D])
        xgT5 = tb("xgT5", [P, 2, KC, P])
        yo5 = tb("yo5", [P, 2, D])
        yg5 = tb("yg5", [P, YG, D])
        last.close()

        qk_dram = dram("qk_dram", [NB, 3, 2, D, S], BF16)
        xs_dram = dram("xs_dram", [MT * P, D])
        ys_dram = dram("ys_dram", [MT * P, D])
        b_dram = dram("b_dram", [3, NE1, FF + D], BF16)
        xs5_dram = dram("xs5_dram", [NE2 * CAP, D])
        ys5_dram = dram("ys5_dram", [NE2 * CAP, D])
        m_dram = dram("m_dram", [NB, 3, H * QT * P], BF16)

        consts_in = sem("consts_in")
        txt_in = sem("txt_in")
        x_in = sem("x_in")
        parts_out = sem("parts_out")
        stacks_in = sem("stacks_in")
        mrow_out = sem("mrow_out")
        mrow_in = sem("mrow_in")
        out_done = sem("out_done")
        pool_init = sem("pool_init")
        pe_qk = sem("pe_qk")
        pe_v = sem("pe_v")
        pe_s = sem("pe_s")
        pe_mT = sem("pe_mT")
        pe_st = sem("pe_st")
        pe_pv = sem("pe_pv")
        pe_vT = sem("pe_vT")
        pe_o = sem("pe_o")
        dve_init = sem("dve_init")
        dve_v32 = sem("dve_v32")
        act_v1 = sem("act_v1")
        dve_vr = sem("dve_vr")
        act_v2 = sem("act_v2")
        dve_mchain = sem("dve_mchain")
        dve_hi = sem("dve_hi")
        dve_lo = sem("dve_lo")
        act_OT = sem("act_OT")
        pe_cmb = sem("pe_cmb")
        dve_qk32 = sem("dve_qk32")
        dve_res = sem("dve_res")
        dve_p3 = sem("dve_p3")
        dve_v = sem("dve_v")
        dve_max = sem("dve_max")
        dve_mneg = sem("dve_mneg")
        dve_mparts = sem("dve_mparts")
        dve_rsum = sem("dve_rsum")
        dve_vals = sem("dve_vals")
        dve_vT = sem("dve_vT")
        dve_h1 = sem("dve_h1")
        act_acol = sem("act_acol")
        act_p1 = sem("act_p1")
        act_p2 = sem("act_p2")
        act_exp = sem("act_exp")
        dve_stats = sem("dve_stats")
        act_std = sem("act_std")
        dve_rstd = sem("dve_rstd")
        dve_xn = sem("dve_xn")
        pe_uT = sem("pe_uT")
        act_uT = sem("act_uT")
        pe_xp = sem("pe_xp")
        act_dlow = sem("act_dlow")
        dve_bcs = sem("dve_bcs")
        dve_bcchain = sem("dve_bcchain")
        pe_dt = sem("pe_dt")
        dve_xb = sem("dve_xb")
        dve_sp = sem("dve_sp")
        act_sp = sem("act_sp")
        dve_delta = sem("dve_delta")
        dve_dtu = sem("dve_dtu")
        pe_bc = sem("pe_bc")
        act_dA = sem("act_dA")
        act_C = sem("act_C")
        dve_dBu = sem("dve_dBu")
        dve_scan = sem("dve_scan")
        pool_hC = sem("pool_hC")
        pe_y = sem("pe_y")
        dve_yT = sem("dve_yT")
        pe_yT = sem("pe_yT")
        dve_h2 = sem("dve_h2")
        late_in = sem("late_in")
        w_in = sem("w_in")
        b12_in = sem("b12_in")
        b_out = sem("b_out")
        brow_in = sem("brow_in")
        ln_chain = sem("ln_chain")
        ln_stats = sem("ln_stats")
        ln_std = sem("ln_std")
        ln_done = sem("ln_done")
        dve_bparts = sem("dve_bparts")
        zero_out = sem("zero_out")
        pe_xaT = sem("pe_xaT")
        act_xaT = sem("act_xaT")
        pe_lg = sem("pe_lg")
        dve_lg = sem("dve_lg")
        c3 = sem("c3")
        dve_hot = sem("dve_hot")
        pe_rank = sem("pe_rank")
        dve_slots = sem("dve_slots")
        dve_te = sem("dve_te")
        dve_ex = sem("dve_ex")
        act_ex = sem("act_ex")
        dve_gate = sem("dve_gate")
        rows_out = sem("rows_out")
        tile_in0 = sem("tile_in0")
        tile_in1 = sem("tile_in1")
        pe_xg = sem("pe_xg")
        act_xg = sem("act_xg")
        pe_up = sem("pe_up")
        act_gelu = sem("act_gelu")
        pe_hidT = sem("pe_hidT")
        dve_hidT = sem("dve_hidT")
        pe_down = sem("pe_down")
        dve_yo = sem("dve_yo")
        yo_out = [sem("yo_out0"), sem("yo_out1")]
        yg_in = [sem(f"yg_in{k}") for k in range(YG)]
        best_chain = sem("best_chain")
        act_xab = sem("act_xab")
        pool_xa = sem("pool_xa")
        dve_h3 = sem("dve_h3")
        last_in = sem("last_in")
        act_xn4 = sem("act_xn4")
        pe_xT4 = sem("pe_xT4")
        act_xT4 = sem("act_xT4")
        pe_qk4 = sem("pe_qk4")
        pe_v4 = sem("pe_v4")
        dve_qk4 = sem("dve_qk4")
        dve_v4 = sem("dve_v4")
        pe_s4 = sem("pe_s4")
        dve_mask4 = sem("dve_mask4")
        dve_nm4 = sem("dve_nm4")
        act_p4 = sem("act_p4")
        pe_pt4 = sem("pe_pt4")
        dve_pt4 = sem("dve_pt4")
        pe_pv4 = sem("pe_pv4")
        dve_rs4 = sem("dve_rs4")
        dve_h4 = sem("dve_h4")
        ring_in = [sem(f"ring_in{k}") for k in range(RING // LOAD)]
        dve_hot5 = sem("dve_hot5")
        pe_rank5 = sem("pe_rank5")
        dve_rank5 = sem("dve_rank5")
        pe_count5 = sem("pe_count5")
        c5 = sem("c5")
        dve_ex5 = sem("dve_ex5")
        act_ex5 = sem("act_ex5")
        dve_to5 = sem("dve_to5")
        rows5_out = sem("rows5_out")
        tile5_in = [sem("tile5_in0"), sem("tile5_in1")]
        pe_xg5 = sem("pe_xg5")
        act_xg5 = sem("act_xg5")
        pe_y5 = sem("pe_y5")
        dve_y5 = sem("dve_y5")
        y5_out = [sem("y5_out0"), sem("y5_out1")]
        dve_h5 = sem("dve_h5")
        N_CONSTS = 15
        N_LAST = 9
        N_LATE = 10

        def bias_rows(name):
            return A[name].rearrange("(o d) -> o d", o=1).to_broadcast([P, D])

        def two_banks(lo, rows=P):
            return ps[0:rows, lo:lo + 2, 0:HC]

        def vhead(hd):
            return v32[:, :, :].rearrange("p j (g s d) -> p (j g) s d", s=2, d=HD)[:, :, hd, :]

        def vpart(hd, part):
            lo = (P // 2) * hd + VW * part
            return Vst[:, :, :, :].rearrange("p j (g s) c -> p (j g) s c", s=2)[:, :, hd, lo:lo + HD]

        def halves(ap):
            return ap.rearrange("p (c t) -> p c t", c=2)

        A = {n: a.bitcast(BF16) if n in ("sel", "ones3", "tri", "onesm", "tri5", "ones3p") else a for n, a in A.items()}
        block = ctx.enter_context(nc.Block())

        @block.sync
        def _(q):
            q.dma_start(xT[:, :, :], A["xT"][0]).then_inc(x_in, 16)
            q.dma_start(wqkv[:, :, :], A["wqkvT"]).then_inc(consts_in, 16)
            q.dma_start(bqk[:, :], A["bqk"]).then_inc(consts_in, 16)
            q.dma_start(bv[:, :], bias_rows("bv")).then_inc(consts_in, 16)
            q.dma_start(bo[:, :], bias_rows("bo")).then_inc(consts_in, 16)
            q.dma_start(wo[:, :, :], A["woT"]).then_inc(consts_in, 16)
            q.dma_start(ident[:, :], A["ident"]).then_inc(consts_in, 16)
            q.dma_start(xpw[:, :, :], A["xpwT"]).then_inc(consts_in, 16)
            q.dma_start(xpbc[:, :, :], A["xpbcT"]).then_inc(consts_in, 16)
            q.dma_start(dtw[:, :], A["dtwT"]).then_inc(consts_in, 16)
            q.dma_start(dtb[:, :], A["dtb"]).then_inc(consts_in, 16)
            q.dma_start(dsk[:, :], A["dsk"]).then_inc(consts_in, 16)
            q.dma_start(alog[:, :], A["alog"]).then_inc(consts_in, 16)
            q.dma_start(sel[:, :, :], A["sel"]).then_inc(consts_in, 16)
            q.dma_start(Kst[PART:KR, :, :], A["ones3"]).then_inc(consts_in, 16)
            q.dma_start(sel3[:, :], A["sel3"]).then_inc(consts_in, 16)
            q.wait_ge(pool_init, 2)
            for b in range(NB):
                q.dma_start(Hs[0:TXT, b * NT + QT, :], A["txt"][b]).then_inc(txt_in, 16)
            def load_x(b):
                q.wait_ge(pe_v, b)
                q.dma_start(xT[:, :, :], A["xT"][b]).then_inc(x_in, 16)

            def restack(b):
                q.wait_ge(dve_p3, 4 * (b + 1))
                for part in range(3):
                    q.dma_start(qk_dram[b, part].rearrange("a (m p) s -> p (a m) s", p=P),
                                parts[:, part, :, :]).then_inc(parts_out, 16)
                q.wait_ge(parts_out, 48 * (b + 1))
                for stack, a, order in ((Qst, 0, QPARTS), (Kst, 1, KPARTS)):
                    for g, part in enumerate(order):
                        q.dma_start(stack[HD * g:HD * (g + 1), :, :],
                                    qk_dram[b, part, a].rearrange("(h d) s -> d h s", d=HD)).then_inc(stacks_in, 16)

            def maxima_rows(b):
                q.wait_ge(dve_mparts, b + 1)
                q.dma_start(m_dram[b].rearrange("a (r s) -> r a s", s=P), mparts[:, :, :]).then_inc(mrow_out, 16)
                q.wait_ge(mrow_out, 16 * (b + 1))
                q.dma_start(Qst[PART:KR, :, :].rearrange("p h s -> p (h s)"), m_dram[b]).then_inc(mrow_in, 16)
            restack(0)
            if STAGE >= 3:
                q.dma_start(xs_dram.rearrange("(j p) d -> p j d", p=P),
                            zeros[:, :].rearrange("p (o d) -> p o d", o=1).to_broadcast([P, MT, D])).then_inc(zero_out, 16)
                q.dma_start(xs5_dram.rearrange("(j p) d -> p j d", p=P),
                            zeros[:, :].rearrange("p (o d) -> p o d", o=1).to_broadcast([P, NP2, D])).then_inc(zero_out, 16)
            with q.Fori(0, NB - 1) as b:
                load_x(b + 1)
                maxima_rows(b)
                restack(b + 1)
            maxima_rows(NB - 1)
            q.wait_ge(dve_h2, NB + 1)
            if STAGE >= 3:
                q.dma_start(b12[:, :], A["b12"]).then_inc(b12_in, 16)
                for dst, name in ((rw[:, :, :], "rw"), (tri[:, :], "tri"), (onesm[:, :], "onesm"), (real[:, :], "real"),
                                  (iota1[:, :], "iota1"), (iota128[:, :], "iota128"), (ramp[:, :], "ramp"),
                                  (keep[:, :], "keep1"), (nottoken[:, :], "nottoken"), (ones3[:, :], "ones3p")):
                    q.dma_start(dst, A[name]).then_inc(late_in, 16)
                q.wait_ge(dve_bparts, 3)
                q.dma_start(b_dram.rearrange("k e f -> e k f"), b12p[:, :, :]).then_inc(b_out, 16)
                q.wait_ge(b_out, 16)
                q.dma_start(brow[:, :, :], b_dram).then_inc(brow_in, 16)
                for e in range(0, NE1, 2):
                    q.dma_start(W1[:, e:e + 2, :, :], A["w1"][:, e:e + 2]).then_inc(w_in, 16)
                    q.dma_start(W2[:, e:e + 2, :, :], A["w2"][:, e:e + 2]).then_inc(w_in, 16)
                q.wait_ge(rows_out, 16 * G)
                q.wait_ge(zero_out, 32)

                def tile_load(j, u, tile_in):
                    q.wait_ge(pe_xg, j - 1)
                    q.dma_start(xg[:, u, :], xs_dram[bass.ds(j * P, P), :]).then_inc(tile_in, 16)

                def tile_store(j, u):
                    q.wait_ge(dve_yo, j + 1)
                    q.dma_start(ys_dram[bass.ds(j * P, P), :], yo[:, u, :]).then_inc(yo_out[u], 16)
                q.dma_start(xg[:, 0, :], xs_dram[0:P, :]).then_inc(tile_in0, 16)
                q.dma_start(xg[:, 1, :], xs_dram[P:2 * P, :]).then_inc(tile_in1, 16)
                with q.Fori(1, MT // 2) as i:
                    tile_load(2 * i, 0, tile_in0)
                    tile_store(2 * i - 2, 0)
                    tile_load(2 * i + 1, 1, tile_in1)
                    tile_store(2 * i - 1, 1)
                tile_store(MT - 2, 0)
                tile_store(MT - 1, 1)
                q.wait_ge(dve_h3, G)
            if STAGE >= 4:
                for dst, name in ((w4[:, :, :], "w4T"), (bqk4[:, :], "bqk4"), (mask4[:, :], "mask4"), (wg[:, :, :], "wg"),
                                  (tri5[:, :, :], "tri5"), (real5[:, :], "real"), (nottoken5[:, :], "nottoken"),
                                  (iota5[:, :], "iota5")):
                    q.dma_start(dst, A[name]).then_inc(last_in, 16)
                q.dma_start(bv4[:, :], bias_rows("bv4")).then_inc(last_in, 16)
                if STAGE >= 5:
                    for k in range(RING // LOAD):
                        q.dma_start(ring[:, LOAD * k:LOAD * (k + 1), :, :], A["we"][:, LOAD * k:LOAD * (k + 1)]).then_inc(ring_in[k], 16)
                q.wait_ge(dve_h4, G + 1)
            if STAGE >= 5:
                q.wait_ge(zero_out, 32)
                q.wait_ge(rows5_out, 32 * G)

                def pair_load(j, u, first):
                    if not first:
                        q.wait_ge(pe_xg5, j - 1)
                    q.dma_start(xg5[:, u, :], xs5_dram[bass.ds(j * P, P), :]).then_inc(tile5_in[u], 16)

                def pair_store(j, u):
                    q.wait_ge(dve_y5, 2 * j + 2)
                    q.dma_start(ys5_dram[bass.ds(j * P, P), :], yo5[:, u, :]).then_inc(y5_out[u], 16)

                def turn_of_ring(lap, last_lap):
                    for k in range(RING // LOAD):
                        for m in range(LOAD // 2):
                            j = lap * (RING // 2) + k * (LOAD // 2) + m
                            u = m % 2
                            if not (last_lap and k == RING // LOAD - 1):
                                pair_load(j + 2, u, False)
                            pair_store(j, u)
                        if not last_lap:
                            q.dma_start(ring[:, LOAD * k:LOAD * (k + 1), :, :],
                                        A["we"][:, bass.ds((lap + 1) * RING + LOAD * k, LOAD)]).then_inc(ring_in[k], 16)
                pair_load(0, 0, True)
                pair_load(1, 1, True)
                with q.Fori(0, NE2 // RING - 1) as lap:
                    turn_of_ring(lap, False)
                turn_of_ring(NE2 // RING - 1, True)
                q.wait_ge(dve_h5, 2 * G)
            for b in range(NB):
                q.dma_start(out[b, 0:S].rearrange("(i p) d -> p i d", p=P), Hs[:, b * NT:b * NT + QT, :]).then_inc(out_done, 16)
                q.dma_start(out[b, S:L], Hs[0:TXT, b * NT + QT, :]).then_inc(out_done, 16)
            q.wait_ge(out_done, 32 * NB)

        @block.tensor
        def _(pe):
            def project(b, first):
                pe.wait_ge(x_in, 16 * (b + 1))
                if not first:
                    pe.wait_ge(dve_h1, b)
                for t in range(4):
                    for c in range(KC):
                        m = nc.tensor.matmul(ps[:, t, :], wqkv[:, c, P * t:P * (t + 1)], xT[:, c, :],
                                             start=(c == 0), stop=(c == KC - 1))
                    m.then_inc(pe_qk, 1)
                for i in range(QT):
                    for c in range(KC):
                        m = nc.tensor.matmul(ps[:, 4 + i // 2, D * (i % 2):D * (i % 2 + 1)],
                                             xT[:, c, P * i:P * (i + 1)], wqkv[:, c, 2 * D:3 * D],
                                             start=(c == 0), stop=(c == KC - 1))
                m.then_inc(pe_v, 1)

            def attention(b):
                pe.wait_ge(stacks_in, 192 * (b + 1))
                pe.wait_ge(dve_v, b + 1)
                pe.wait_ge(dve_h2, b + 1)

                def scores(h, group, first):
                    if not first:
                        pe.wait_ge(dve_max, H * b + h - 1)
                    for i in range(QT):
                        m = nc.tensor.matmul(ps[:, 4 * group + i, :], Qst[0:PART, h, P * i:P * (i + 1)],
                                             Kst[0:PART, h, :], start=True, stop=True)
                    m.then_inc(pe_s, 1)
                scores(0, 0, True)
                scores(1, 1, True)
                with pe.Fori(1, H // 2) as i:
                    scores(2 * i, 0, False)
                    scores(2 * i + 1, 1, False)
                pe.wait_ge(dve_max, H * (b + 1))
                nc.tensor.transpose(ps[:, 0, 0:P], mx[:, :, :].rearrange("p h i -> p (h i)"),
                                    ident[:, :]).then_inc(pe_mT, 1)
                pe.wait_ge(dve_mneg, b + 1)
                pe.wait_ge(mrow_in, 16 * (b + 1))

                def tscores(n, h, k):
                    pe.wait_ge(act_exp, NU * b + n + 1)
                    for j in range(2):
                        m = nc.tensor.matmul(ps[:, 2 * (k % 2) + j, :], Kst[:, h, P * (2 * (k % 2) + j):P * (2 * (k % 2) + j + 1)],
                                             Qst[:, h, :], start=True, stop=True)
                    m.then_inc(pe_st, 1)

                def combine(pair, u):
                    pe.wait_ge(act_OT, (H // 2) * b + pair + 3)
                    pe.wait_ge(dve_vals, (H // 2) * b + pair + 1)
                    for i in range(QT):
                        m = nc.tensor.matmul(ps[:, 6 + u, 2 * VW * i:2 * VW * (i + 1)], OT[:, u, P * i:P * (i + 1)],
                                             sel3[:, :], start=True, stop=True)
                    m.then_inc(pe_cmb, 1)

                def two_pairs(i, first, last):
                    for k in range(8):
                        if not (last and k >= 5):
                            tscores(8 * i + k + 3, 4 * i + (k + 3) // 2, (k + 3) % 8)
                        weighted(8 * i + k, 4 * i + k // 2, k, 2 * i + k // 4)
                        if k % 4 == 1 and not (first and k == 1):
                            combine(2 * i + k // 4 - 1, 1 - k // 4)

                def weighted(n, h, k, pair):
                    pe.wait_ge(dve_lo, NU * b + n + 1 + 4)
                    if k % 4 == 0:
                        pe.wait_ge(act_OT, (H // 2) * b + pair + 1)
                    for j in range(2):
                        for part in range(2):
                            m = nc.tensor.matmul(ps[:, 4 + k // 4, :], Vst[:, 2 * (k % 2) + j, h, :], Phl[:, k % 4, part, j, :],
                                                 start=(k % 4 == 0 and j == 0 and part == 0),
                                                 stop=(k % 4 == 3 and j == 1 and part == 1))
                    m.then_inc(pe_pv, 1)
                for k in range(3):
                    tscores(k, k // 2, k)
                two_pairs(0, True, False)
                with pe.Fori(1, H // 4 - 1) as i:
                    two_pairs(i, False, False)
                two_pairs(H // 4 - 1, False, True)
                combine(H // 2 - 1, 1)
                pe.wait_ge(dve_vals, (H // 2) * (b + 1) + 2)
                for c in range(KC):
                    for i in range(QT):
                        m = nc.tensor.transpose(ps[:, c, P * i:P * (i + 1)], vals[:, i, P * c:P * (c + 1)], ident[:, :])
                m.then_inc(pe_vT, 1)
                pe.wait_ge(dve_vT, b + 1)
                for i in range(QT):
                    for c in range(KC):
                        m = nc.tensor.matmul(ps[:, 2 + i // 2, D * (i % 2):D * (i % 2 + 1)],
                                             valsT[:, c, P * i:P * (i + 1)], wo[:, c, :],
                                             start=(c == 0), stop=(c == KC - 1))
                m.then_inc(pe_o, 1)

            def scan(b, last):
                pe.wait_ge(dve_xn, b + 1)
                pe.wait_ge(dve_h1, b + 1)
                if not last:
                    pe.wait_ge(dve_qk32, 4 * (b + 2))
                    pe.wait_ge(dve_v32, b + 2)
                for c in range(KC):
                    for i in range(NT):
                        dst = ps[:, 4 + c, P * i:P * (i + 1)] if i < QT else ps[:, 6, P * c:P * (c + 1)]
                        m = nc.tensor.transpose(dst, xn[:, i, P * c:P * (c + 1)], ident[:, :])
                m.then_inc(pe_uT, 1)
                pe.wait_ge(act_uT, b + 1)
                for half in range(2):
                    for c in range(KC):
                        nc.tensor.matmul(ps[0:RANK, half, 0:HC], xpw[:, c, :], uT[:, c, HC * half:HC * (half + 1)],
                                         start=(c == 0), stop=(c == KC - 1))
                for half in range(2):
                    for c in range(KC):
                        m = nc.tensor.matmul(ps[0:96, 2 + half, 0:HC], xpbc[:, c, :], uT[:, c, HC * half:HC * (half + 1)],
                                             start=(c == 0), stop=(c == KC - 1))
                m.then_inc(pe_xp, 1)
                pe.wait_ge(act_dlow, b + 1)
                for c in range(KC):
                    for half in range(2):
                        m = nc.tensor.matmul(ps[:, 4 + 2 * c + half, 0:HC], dtw[:, P * c:P * (c + 1)],
                                             dlow[:, HC * half:HC * (half + 1)], start=True, stop=True)
                m.then_inc(pe_dt, 1)

                def spread(n, first):
                    if not first:
                        pe.wait_ge(dve_dBu, NS * b + n)
                        pe.wait_ge(act_C, NS * b + n)
                    for which in range(2):
                        for half in range(2):
                            m = nc.tensor.matmul(ps[:, 2 * which + half, 0:HC], sel[:, NS * which + n, :],
                                                 bcs[:, HC * half:HC * (half + 1)], start=True, stop=True)
                    m.then_inc(pe_bc, 1)

                def add_state(n, u, start, stop):
                    for c in range(KC):
                        pe.wait_ge(pool_hC, 2 * (NS * b + n) + 1 + c)
                        for half in range(2):
                            m = nc.tensor.matmul(ps[:, 4 + 2 * c + half, 0:HC], ident[:, :],
                                                 hC[:, u, c, HC * half:HC * (half + 1)], start=start, stop=stop,
                                                 skip_group_check=True)
                    m.then_inc(pe_y, 1)
                pe.wait_ge(dve_bcs, b + 1)
                spread(0, True)
                pe.wait_ge(dve_xb, b + 1)
                spread(1, False)
                add_state(0, 0, True, False)
                spread(2, False)
                add_state(1, 1, False, False)
                with pe.Fori(1, NS // 2 - 1) as i:
                    spread(2 * i + 1, False)
                    add_state(2 * i, 0, False, False)
                    spread(2 * i + 2, False)
                    add_state(2 * i + 1, 1, False, False)
                spread(NS - 1, False)
                add_state(NS - 2, 0, False, False)
                add_state(NS - 1, 1, False, True)
                pe.wait_ge(dve_yT, b + 1)
                pe.wait_ge(dve_dBu, NS * (b + 1))
                pe.wait_ge(act_C, NS * (b + 1))
                for i in range(NT):
                    rows = P if i < QT else TXT
                    for c in range(KC):
                        m = nc.tensor.transpose(ps[0:rows, i // 2, D * (i % 2) + P * c:D * (i % 2) + P * (c + 1)],
                                                xb[:, c, P * i:P * i + rows], ident[:, :])
                m.then_inc(pe_yT, 1)

            def route(r, weights, n_experts, rank=None):
                def turn(t, u, first):
                    pe.wait_ge(act_xab, r * G + t + 1)
                    if not first:
                        pe.wait_ge(act_xaT, r * G + t - 1)
                    for c in range(KC):
                        m = nc.tensor.transpose(ps[:, u, P * c:P * (c + 1)], xab[:, u, P * c:P * (c + 1)], ident[:, :])
                    m.then_inc(pe_xaT, 1)

                def logits(t, u, first):
                    pe.wait_ge(act_xaT, r * G + t + 1)
                    if not first:
                        pe.wait_ge(dve_lg, r * G + t - 1)
                    for c in range(KC):
                        m = nc.tensor.matmul(ps[:, 2 + u, 0:n_experts], xaT[:, u, c, :], weights[:, c, :],
                                             start=(c == 0), stop=(c == KC - 1))
                    m.then_inc(pe_lg, 1)
                    if rank:
                        rank(t, u, isinstance(t, int) and t == 0)
                turn(0, 0, True)
                turn(1, 1, True)
                logits(0, 0, True)
                turn(2, 0, False)
                logits(1, 1, True)
                with pe.Fori(1, G // 2 - 1) as i:
                    turn(2 * i + 1, 1, False)
                    logits(2 * i, 0, False)
                    turn(2 * i + 2, 0, False)
                    logits(2 * i + 1, 1, False)
                turn(G - 1, 1, False)
                logits(G - 2, 0, False)
                logits(G - 1, 1, False)

            def one_expert():
                pe.wait_ge(late_in, 16 * N_LATE)
                route(0, rw, NE1)
                pe.wait_ge(dve_hot, 1)
                nc.tensor.matmul(ps[:, 4, 0:G * NE1], tri[:, :], hot[:, :, :].rearrange("p g e -> p (g e)"), start=True, stop=True)
                nc.tensor.matmul(ps[:, 5, 0:G * NE1], onesm[:, :], hot[:, :, :].rearrange("p g e -> p (g e)"),
                                 start=True, stop=True).then_inc(pe_rank, 1)
                pe.wait_ge(dve_te, 1)
                pe.wait_ge(w_in, 16 * NE1)
                pe.wait_ge(brow_in, 16)

                def turn(j, u, tile_in, first):
                    pe.wait_ge(tile_in, 16 * (j // 2 + 1) if isinstance(j, int) else 8 * (j - u) + 16)
                    if not first:
                        pe.wait_ge(act_xg, j - 1)
                    for c in range(KC):
                        m = nc.tensor.transpose(ps[:, u, P * c:P * (c + 1)], xg[:, u, P * c:P * (c + 1)], ident[:, :])
                    m.then_inc(pe_xg, 1)

                def up(j, u, first):
                    e = pe.value_load(tei[0:1, bass.ds(j, 1)], min_val=0, max_val=NE1 - 1)
                    pe.wait_ge(act_xg, j + 1)
                    if not first:
                        pe.wait_ge(act_gelu, j - 1)
                    for c in range(KC):
                        nc.tensor.matmul(ps[:, 2 + u, :], xgT[:, u, c, :], W1[:, e, c, :], start=(c == 0), stop=False)
                    nc.tensor.matmul(ps[:, 2 + u, :], ones3[:, :], brow[:, e, 0:FF], start=False, stop=True).then_inc(pe_up, 1)

                def down(j, u, first):
                    e = pe.value_load(tei[0:1, bass.ds(j, 1)], min_val=0, max_val=NE1 - 1)
                    pe.wait_ge(act_gelu, j + 1)
                    if not first:
                        pe.wait_ge(dve_hidT, j - 1)
                    for f in range(FC):
                        m = nc.tensor.transpose(ps[:, 4 + u, P * f:P * (f + 1)], hid[:, u, P * f:P * (f + 1)], ident[:, :])
                    m.then_inc(pe_hidT, 1)
                    pe.wait_ge(dve_hidT, j + 1)
                    if not first:
                        pe.wait_ge(dve_yo, j - 1)
                    for f in range(FC):
                        nc.tensor.matmul(ps[:, 6 + u, 0:D], hidT[:, u, f, :], W2[:, e, f, :], start=(f == 0), stop=False)
                    nc.tensor.matmul(ps[:, 6 + u, 0:D], ones3[:, :], brow[:, e, FF:FF + D], start=False, stop=True).then_inc(pe_down, 1)
                turn(0, 0, tile_in0, True)
                up(0, 0, True)
                turn(1, 1, tile_in1, True)
                up(1, 1, True)
                down(0, 0, True)
                turn(2, 0, tile_in0, False)
                up(2, 0, False)
                down(1, 1, True)
                with pe.Fori(1, MT // 2 - 1) as i:
                    turn(2 * i + 1, 1, tile_in1, False)
                    up(2 * i + 1, 1, False)
                    down(2 * i, 0, False)
                    turn(2 * i + 2, 0, tile_in0, False)
                    up(2 * i + 2, 0, False)
                    down(2 * i + 1, 1, False)
                turn(MT - 1, 1, tile_in1, False)
                up(MT - 1, 1, False)
                down(MT - 2, 0, False)
                down(MT - 1, 1, False)

            def causal_batch(b):
                for i in range(NT):
                    pe.wait_ge(act_xn4, NT * b + i + 1)
                    if i == 0:
                        pe.wait_ge(dve_h4, NT * b + 1)
                    for c in range(KC):
                        dst = ps[:, c, P * i:P * (i + 1)] if i < QT else ps[:, 2, P * c:P * (c + 1)]
                        m = nc.tensor.transpose(dst, xn4[:, i, P * c:P * (c + 1)], ident[:, :])
                m.then_inc(pe_xT4, 1)
                pe.wait_ge(act_xT4, b + 1)
                for t in range(4):
                    for lo, n, dst in ((0, S, ps[:, t, :]), (S, P, ps[:, 4, P * t:P * (t + 1)])):
                        for c in range(KC):
                            m = nc.tensor.matmul(dst, w4[:, c, P * t:P * (t + 1)], xT4[:, c, lo:lo + n],
                                                 start=(c == 0), stop=(c == KC - 1))
                m.then_inc(pe_qk4, 1)
                for i in range(NT):
                    for c in range(KC):
                        m = nc.tensor.matmul(ps[:, 5 + i // 2, D * (i % 2):D * (i % 2 + 1)], xT4[:, c, P * i:P * (i + 1)],
                                             w4[:, c, 2 * D:3 * D], start=(c == 0), stop=(c == KC - 1))
                m.then_inc(pe_v4, 1)

                def scores(i):
                    if i >= 2:
                        pe.wait_ge(act_p4, NT * b + i - 1)
                    for lo, hi in ((0, min(P * (i + 1), S)), (S, P * (i + 1))):
                        for c in range(KC):
                            if hi > lo:
                                m = nc.tensor.matmul(ps[:, 2 * (i % 2) + lo // S, 0:hi - lo], QK4[:, c, P * i:P * (i + 1)],
                                                     QK4[:, 2 + c, lo:hi], start=(c == 0), stop=(c == KC - 1))
                    m.then_inc(pe_s4, 1)

                def weighted(i):
                    pe.wait_ge(act_p4, NT * b + i + 1)
                    if i >= 1:
                        pe.wait_ge(dve_pt4, NT * b + i)
                    for j in range(i + 1):
                        m = nc.tensor.transpose(ps[:, 4 + j // QT, P * (j % QT):P * (j % QT + 1)],
                                                P4[:, i % 2, P * j:P * (j + 1)], ident[:, :])
                    m.then_inc(pe_pt4, 1)
                    pe.wait_ge(dve_pt4, NT * b + i + 1)
                    if i >= 2:
                        pe.wait_ge(dve_h4, NT * b + i)
                    for j in range(i + 1):
                        m = nc.tensor.matmul(ps[:, 6 + i % 2, 0:D], PT4[:, i % 2, j, :], V4[:, j, :],
                                             start=(j == 0), stop=(j == i))
                    m.then_inc(pe_pv4, 1)
                pe.wait_ge(dve_qk4, b + 1)
                pe.wait_ge(dve_v4, b + 1)
                scores(0)
                for i in range(1, NT):
                    scores(i)
                    weighted(i - 1)
                weighted(NT - 1)

            def causal():
                pe.wait_ge(last_in, 16 * N_LAST)
                with pe.Fori(0, NB) as b:
                    causal_batch(b)

            def rank(t, u, first):
                for k in range(2):
                    pe.wait_ge(dve_hot5, 2 * t + k + 1)
                    nc.tensor.matmul(ps[:, 4 + k, 0:NE2], tri5[:, 0, :], hotb[:, u, k, :], start=first, stop=False,
                                     skip_group_check=True).then_inc(pe_rank5, 1)
                for k in range(2):
                    pe.wait_ge(dve_rank5, 2 * t + k + 1)
                    nc.tensor.matmul(ps[:, 4 + k, 0:NE2], tri5[:, 1, :], hotb[:, u, k, :], start=False, stop=False,
                                     skip_group_check=True).then_inc(pe_count5, 1)

            def two_experts():
                route(1, wg, NE2, rank)

                def turn(j, u, first):
                    pe.wait_ge(tile5_in[u], 8 * (j - u) + 16)
                    if not first:
                        pe.wait_ge(act_xg5, j - 1)
                    for c in range(KC):
                        m = nc.tensor.transpose(ps[:, u, P * c:P * (c + 1)], xg5[:, u, P * c:P * (c + 1)], ident[:, :])
                    m.then_inc(pe_xg5, 1)

                def multiply(j, u, place, first):
                    pe.wait_ge(act_xg5, j + 1)
                    if not first:
                        pe.wait_ge(dve_y5, 2 * (j - 1))
                    for k in range(2):
                        for c in range(KC):
                            m = nc.tensor.matmul(ps[:, 2 + u, D * k:D * (k + 1)], xgT5[:, u, c, :], ring[:, place + k, c, :],
                                                 start=(c == 0), stop=(c == KC - 1))
                    m.then_inc(pe_y5, 1)

                def lap_of_ring(lap, first_lap, last_lap):
                    for k in range(RING // LOAD):
                        pe.wait_ge(ring_in[k], 16 * lap + 16)
                        for m in range(LOAD // 2):
                            j = lap * (RING // 2) + k * (LOAD // 2) + m
                            u = m % 2
                            if not (last_lap and k == RING // LOAD - 1 and m == LOAD // 2 - 1):
                                turn(j + 1, 1 - u, first_lap and k == 0 and m == 0)
                            multiply(j, u, LOAD * k + 2 * m, first_lap and k == 0)
                turn(0, 0, True)
                lap_of_ring(0, True, False)
                with pe.Fori(1, NE2 // RING - 1) as lap:
                    lap_of_ring(lap, False, False)
                lap_of_ring(NE2 // RING - 1, False, True)

            pe.wait_ge(consts_in, 16 * N_CONSTS)
            for _ in range(4):
                pe.nop().then_inc(pe_pv, 1)
            for _ in range(2):
                pe.nop().then_inc(pe_cmb, 1)
            project(0, True)
            with pe.Fori(0, NB - 1) as b:
                attention(b)
                project(b + 1, False)
                scan(b, False)
            attention(NB - 1)
            scan(NB - 1, True)
            if STAGE >= 3:
                one_expert()
            if STAGE >= 4:
                causal()
            if STAGE >= 5:
                two_experts()

        @block.scalar
        def _(act):
            def split(b):
                for t in range(4):
                    act.wait_ge(dve_qk32, 4 * b + t + 1)
                    if t == 0 and not isinstance(b, int):
                        act.wait_ge(parts_out, 48 * b)
                    nc.scalar.activation(parts[:, 0, t, :], qk32[:, t, :], ACT.Copy).then_inc(act_p1, 1)
                act.wait_ge(dve_v32, b + 1)
                for hd in range(2):
                    v = nc.scalar.activation(vpart(hd, 0), vhead(hd), ACT.Copy)
                v.then_inc(act_v1, 1)
                for t in range(4):
                    act.wait_ge(dve_res, 4 * b + t + 1)
                    nc.scalar.activation(parts[:, 1, t, :], qk32[:, t, :], ACT.Copy).then_inc(act_p2, 1)
                act.wait_ge(dve_vr, b + 1)
                for hd in range(2):
                    v = nc.scalar.activation(vpart(hd, 1), vhead(hd), ACT.Copy)
                v.then_inc(act_v2, 1)

            def attention(b):
                def exps(n, k):
                    act.wait_ge(pe_st, NU * b + n + 1)
                    act.wait_ge(dve_lo, NU * b + n + 1)
                    e = nc.scalar.activation(P32[:, k % 4, :, :], ps[:, 2 * (k % 2):2 * (k % 2) + 2, :],
                                             ACT.Exp, scale=float(HD) ** -0.5)
                    if k % 2 == 0:
                        act.wait_ge(pe_pv, NU * b + n + 1)
                        e = nc.scalar.activation(Phl[:, k % 4, 0, :, :], ps[:, 2 * (k % 2):2 * (k % 2) + 2, :],
                                                 ACT.Exp, scale=float(HD) ** -0.5)
                    e.then_inc(act_exp, 1)

                def evacuate(pair, u):
                    act.wait_ge(pe_pv, NU * b + 4 * pair + 4 + 4)
                    act.wait_ge(pe_cmb, (H // 2) * b + pair + 1)
                    nc.scalar.activation(OT[:, u, :], ps[:, 4 + u, :], ACT.Copy).then_inc(act_OT, 1)

                def two_pairs(i, first):
                    for k in range(8):
                        exps(8 * i + k, k)
                        if k % 4 == 3 and not (first and k == 3):
                            evacuate(2 * i + k // 4 - 1, 1 - k // 4)
                two_pairs(0, True)
                with act.Fori(1, H // 4) as i:
                    two_pairs(i, False)
                evacuate(H // 2 - 1, 1)

            def standard_deviations(b):
                act.wait_ge(dve_stats, b + 1)
                nc.scalar.activation(rstd[:, :], mv[:, :, 1], ACT.Sqrt).then_inc(act_std, 1)

            def scan(b):
                act.wait_ge(pe_uT, b + 1)
                for c in range(KC):
                    nc.scalar.activation(uT[:, c, 0:S], ps[:, 4 + c, :], ACT.Copy)
                nc.scalar.activation(uT[:, :, S:LP], ps[:, 6, 0:2 * P].rearrange("p (c t) -> p c t", c=KC)[:, :, 0:LP - S],
                                     ACT.Copy).then_inc(act_uT, 1)
                act.wait_ge(pe_xp, b + 1)
                nc.scalar.activation(halves(dlow[:, :]), two_banks(0, RANK), ACT.Copy).then_inc(act_dlow, 1)
                act.wait_ge(dve_sp, b + 1)
                nc.scalar.activation(sp[:, :, :], sp[:, :, :], ACT.Exp, scale=-1.0).then_inc(act_sp, 1)
                act.wait_ge(act_sp, 2 * b + 1)
                nc.scalar.activation(sp[:, :, :], sp[:, :, :], ACT.Ln, bias=1.0).then_inc(act_sp, 1)
                act.wait_ge(dve_delta, b + 1)

                def decay(n, u, first):
                    for c in range(KC):
                        if not first:
                            act.wait_ge(dve_scan, 2 * (NS * b + n - 2) + c + 1)
                        nc.scalar.activation(dA[:, u, c, :], delta[:, c, :], ACT.Exp,
                                             scale=acol[:, bass.ds(n + NS * c, 1)]).then_inc(act_dA, 1)
                    act.wait_ge(pe_bc, NS * b + n + 1)
                    if not first:
                        act.wait_ge(pool_hC, 2 * (NS * b + n - 1))
                    nc.scalar.activation(halves(Cb[:, u, :]), two_banks(2), ACT.Copy).then_inc(act_C, 1)
                decay(0, 0, True)
                decay(1, 1, True)
                with act.Fori(1, NS // 2) as i:
                    decay(2 * i, 0, False)
                    decay(2 * i + 1, 1, False)

            def normalise_rows(r, norm):
                def rows(t, u, first):
                    if not first:
                        act.wait_ge(pe_xaT, r * G + t - 1)
                        act.wait_ge(pool_xa, r * G + t - 1)
                    nc.scalar.activation(xab[:, u, :], Hs[:, t, :], ACT.Identity, bias=lbias[:, bass.ds(t, 1)],
                                         scale=lrstd[:, bass.ds(t, 1)]).then_inc(act_xab, 1)

                def turned(t, u, first):
                    act.wait_ge(pe_xaT, r * G + t + 1)
                    if not first:
                        act.wait_ge(pe_lg, r * G + t - 1)
                    nc.scalar.activation(xaT[:, u, :, :], ps[:, u, 0:D].rearrange("p (c t) -> p c t", c=KC), ACT.Copy).then_inc(act_xaT, 1)
                act.wait_ge(ln_stats, norm)
                nc.scalar.activation(lrstd[:, :], lrstd[:, :], ACT.Sqrt).then_inc(ln_std, 1)
                act.wait_ge(ln_done, norm)
                rows(0, 0, True)
                rows(1, 1, True)
                turned(0, 0, True)
                rows(2, 0, False)
                turned(1, 1, True)
                with act.Fori(1, G // 2 - 1) as i:
                    rows(2 * i + 1, 1, False)
                    turned(2 * i, 0, False)
                    rows(2 * i + 2, 0, False)
                    turned(2 * i + 1, 1, False)
                rows(G - 1, 1, False)
                turned(G - 2, 0, False)
                turned(G - 1, 1, False)

            def one_expert():
                act.wait_ge(late_in, 16 * N_LATE)
                normalise_rows(0, 1)
                act.wait_ge(dve_ex, 1)
                nc.scalar.activation(lg[:, :, :], lg[:, :, :], ACT.Exp).then_inc(act_ex, 1)

                def turned(j, u, first):
                    act.wait_ge(pe_xg, j + 1)
                    if not first:
                        act.wait_ge(pe_up, j - 1)
                    nc.scalar.activation(xgT[:, u, :, :], ps[:, u, 0:D].rearrange("p (c t) -> p c t", c=KC), ACT.Copy).then_inc(act_xg, 1)

                def gelu(j, u, first):
                    act.wait_ge(pe_up, j + 1)
                    if not first:
                        act.wait_ge(pe_hidT, j - 1)
                    nc.scalar.activation(hid[:, u, :], ps[:, 2 + u, :], ACT.Gelu).then_inc(act_gelu, 1)
                turned(0, 0, True)
                gelu(0, 0, True)
                turned(1, 1, True)
                gelu(1, 1, True)
                with act.Fori(1, MT // 2) as i:
                    turned(2 * i, 0, False)
                    gelu(2 * i, 0, False)
                    turned(2 * i + 1, 1, False)
                    gelu(2 * i + 1, 1, False)

            def causal():
                act.wait_ge(ln_stats, 2)
                nc.scalar.activation(lrstd[:, :], lrstd[:, :], ACT.Sqrt).then_inc(ln_std, 1)
                act.wait_ge(ln_done, 2)
                with act.Fori(0, NB) as b:
                    for i in range(NT):
                        nc.scalar.activation(xn4[:, i, :], Hs[:, NT * b + i, :], ACT.Identity, bias=lbias[:, bass.ds(NT * b + i, 1)],
                                             scale=lrstd[:, bass.ds(NT * b + i, 1)]).then_inc(act_xn4, 1)
                    act.wait_ge(pe_xT4, b + 1)
                    for c in range(KC):
                        nc.scalar.activation(xT4[:, c, 0:S], ps[:, c, :], ACT.Copy)
                    nc.scalar.activation(xT4[:, :, S:LT], ps[:, 2, 0:D].rearrange("p (c t) -> p c t", c=KC), ACT.Copy).then_inc(act_xT4, 1)
                    for i in range(NT):
                        act.wait_ge(dve_nm4, NT * b + i + 1)
                        if i >= 2:
                            act.wait_ge(pe_pt4, NT * b + i - 1)
                        n = P * (i + 1)
                        nc.scalar.activation(P4[:, i % 2, 0:n], ps[:, 2 * (i % 2):2 * (i % 2) + 2, :].rearrange("p b s -> p (b s)")[:, 0:n],
                                             ACT.Exp, bias=nm4[:, i:i + 1], scale=float(D) ** -0.5,
                                             accum_out=rs4[:, i:i + 1]).then_inc(act_p4, 1)

            def two_experts():
                normalise_rows(1, 3)
                act.wait_ge(dve_ex5, 1)
                nc.scalar.activation(lg5[:, :, :], lg5[:, :, :], ACT.Exp)
                nc.scalar.activation(w5[:, :, :], w5[:, :, :], ACT.Exp).then_inc(act_ex5, 1)

                def turned(j, u, first):
                    act.wait_ge(pe_xg5, j + 1)
                    if not first:
                        act.wait_ge(pe_y5, j - 1)
                    nc.scalar.activation(xgT5[:, u, :, :], ps[:, u, 0:D].rearrange("p (c t) -> p c t", c=KC), ACT.Copy).then_inc(act_xg5, 1)
                turned(0, 0, True)
                turned(1, 1, True)
                with act.Fori(1, NP2 // 2) as i:
                    turned(2 * i, 0, False)
                    turned(2 * i + 1, 1, False)

            act.wait_ge(consts_in, 16 * N_CONSTS)
            nc.scalar.activation(acol[:, :], alog[:, :], ACT.Exp).then_inc(act_acol, 1)
            act.wait_ge(dve_init, 1)
            for _ in range(2):
                act.nop().then_inc(act_exp, 1)
                act.nop().then_inc(act_OT, 1)
            split(0)
            with act.Fori(0, NB - 1) as b:
                attention(b)
                standard_deviations(b)
                split(b + 1)
                scan(b)
            attention(NB - 1)
            standard_deviations(NB - 1)
            scan(NB - 1)
            if STAGE >= 3:
                one_expert()
            if STAGE >= 4:
                causal()
            if STAGE >= 5:
                two_experts()

        @block.gpsimd
        def _(pool):
            nc.gpsimd.memset(Hs[:, :, :].rearrange("p (b i) d -> p b i d", i=NT)[:, :, QT, :], 0.0).then_inc(pool_init, 1)
            nc.gpsimd.memset(zeros[:, :], 0.0).then_inc(pool_init, 1)
            nc.gpsimd.memset(mx[:, :, :], 0.0).then_inc(pool_init, 1)
            nc.gpsimd.memset(Vst[:, :, :, :].rearrange("p j h c -> p (j h c)").bitcast(F32), 0.0).then_inc(pool_init, 1)
            pool.wait_ge(pool_init, 4)
            for hd in range(2):
                vs = Vst[:, :, :, :].rearrange("p j (g s) c -> p (j g) s c", s=2)
                nc.gpsimd.memset(vs[:, :, hd, 64 * hd + HD:64 * hd + HD + 1], 1.0).then_inc(pool_init, 1)

            def output_gate(b, n, u, first):
                for c in range(KC):
                    if c == 0:
                        pool.wait_ge(act_C, NS * b + n + 1)
                        if not first:
                            pool.wait_ge(pe_y, NS * b + n - 1)
                    pool.wait_ge(dve_scan, 2 * (NS * b + n) + c + 1)
                    nc.gpsimd.tensor_tensor(hC[:, u, c, :], hst[:, u, c, :], Cb[:, u, :], ALU.mult).then_inc(pool_hC, 1)
            with pool.Fori(0, NB) as b:
                output_gate(b, 0, 0, True)
                output_gate(b, 1, 1, True)
                with pool.Fori(1, NS // 2) as i:
                    output_gate(b, 2 * i, 0, False)
                    output_gate(b, 2 * i + 1, 1, False)

            def keep_rows(r, xa):
                def rows(t, u):
                    pool.wait_ge(act_xab, r * G + t + 1)
                    nc.gpsimd.tensor_copy(xa[:, t, :], xab[:, u, :]).then_inc(pool_xa, 1)
                with pool.Fori(0, G // 2) as i:
                    rows(2 * i, 0)
                    rows(2 * i + 1, 1)
            if STAGE >= 3:
                keep_rows(0, xa)
                pool.wait_ge(dve_slots, 1)
                pool.wait_ge(zero_out, 32)
                pool.wait_ge(pool_xa, G)
                for t in range(G):
                    nc.gpsimd.indirect_dma_start(xs_dram, bass.IndirectOffsetOnAxis(slots[:, t:t + 1], 0), xa[:, t, :], None,
                                                 bounds_check=MT * P - 1, oob_is_err=False).then_inc(rows_out, 16)
                pool.wait_ge(yo_out[0], 8 * MT)
                pool.wait_ge(yo_out[1], 8 * MT)
                for t in range(G):
                    if t >= YG:
                        pool.wait_ge(dve_h3, t - YG + 1)
                    nc.gpsimd.indirect_dma_start(yg[:, t % YG, :], None, ys_dram, bass.IndirectOffsetOnAxis(slotg[:, t:t + 1], 0),
                                                 bounds_check=MT * P - 1, oob_is_err=False).then_inc(yg_in[t % YG], 16)
            if STAGE >= 5:
                keep_rows(1, xa5)
                pool.wait_ge(dve_to5, 1)
                pool.wait_ge(zero_out, 32)
                pool.wait_ge(pool_xa, 2 * G)
                for t in range(G):
                    for k in range(2):
                        nc.gpsimd.indirect_dma_start(xs5_dram, bass.IndirectOffsetOnAxis(to5[:, t, k:k + 1], 0), xa5[:, t, :], None,
                                                     bounds_check=NE2 * CAP - 1, oob_is_err=False).then_inc(rows5_out, 16)
                pool.wait_ge(y5_out[0], 8 * NP2)
                pool.wait_ge(y5_out[1], 8 * NP2)
                for n in range(2 * G):
                    if n >= YG:
                        pool.wait_ge(dve_h5, n - YG + 1)
                    nc.gpsimd.indirect_dma_start(yg5[:, n % YG, :], None, ys5_dram,
                                                 bass.IndirectOffsetOnAxis(from5[:, n // 2, n % 2:n % 2 + 1], 0),
                                                 bounds_check=NE2 * CAP - 1, oob_is_err=False).then_inc(yg_in[n % YG], 16)

        @block.vector
        def _(dve):
            def split(b):
                for t in range(4):
                    dve.wait_ge(pe_qk, 4 * b + t + 1)
                    nc.vector.tensor_scalar(qk32[:, t, :], ps[:, t, :], bqk[:, t:t + 1], None, ALU.add).then_inc(dve_qk32, 1)
                dve.wait_ge(pe_v, b + 1)
                for i in range(QT):
                    v = nc.vector.tensor_tensor(v32[:, i, :], ps[:, 4 + i // 2, D * (i % 2):D * (i % 2 + 1)], bv[:, :], ALU.add)
                v.then_inc(dve_v32, 1)
                for t in range(4):
                    dve.wait_ge(act_p1, 4 * b + t + 1)
                    nc.vector.tensor_tensor(qk32[:, t, :], qk32[:, t, :], parts[:, 0, t, :], ALU.subtract).then_inc(dve_res, 1)
                dve.wait_ge(act_v1, b + 1)
                for hd in range(2):
                    v = nc.vector.tensor_tensor(vhead(hd), vhead(hd), vpart(hd, 0), ALU.subtract)
                v.then_inc(dve_vr, 1)
                for t in range(4):
                    dve.wait_ge(act_p2, 4 * b + t + 1)
                    nc.vector.tensor_tensor(parts[:, 2, t, :], qk32[:, t, :], parts[:, 1, t, :], ALU.subtract).then_inc(dve_p3, 1)
                dve.wait_ge(act_v2, b + 1)
                for hd in range(2):
                    v = nc.vector.tensor_tensor(vpart(hd, 2), vhead(hd), vpart(hd, 1), ALU.subtract)
                v.then_inc(dve_v, 1)

            def attention(b):
                def maxima(h, group):
                    dve.wait_ge(pe_s, H * b + h + 1)
                    nc.vector.tensor_reduce(mx[:, h, :], ps[:, 4 * group:4 * group + 4, :], AX.X, ALU.max).then_inc(dve_max, 1)
                with dve.Fori(0, H // 2) as i:
                    maxima(2 * i, 0)
                    maxima(2 * i + 1, 1)
                dve.wait_ge(pe_mT, b + 1)
                nc.vector.tensor_scalar(mneg[:, :], ps[0:H * QT, 0, 0:P], -1.0, None, ALU.mult).then_inc(dve_mneg, 1)
                dve.wait_ge(dve_mneg, b + 1)
                nc.vector.tensor_copy(mparts[:, 0, :], mneg[:, :]).then_inc(dve_mchain, 1)
                dve.wait_ge(dve_mchain, 3 * b + 1)
                nc.vector.tensor_tensor(mneg[:, :], mneg[:, :], mparts[:, 0, :], ALU.subtract).then_inc(dve_mchain, 1)
                dve.wait_ge(dve_mchain, 3 * b + 2)
                nc.vector.tensor_copy(mparts[:, 1, :], mneg[:, :]).then_inc(dve_mchain, 1)
                dve.wait_ge(dve_mchain, 3 * b + 3)
                nc.vector.tensor_tensor(mparts[:, 2, :], mneg[:, :], mparts[:, 1, :], ALU.subtract).then_inc(dve_mparts, 1)

                def low(n, k, odd):
                    dve.wait_ge(act_exp, NU * b + n + 3)
                    if k % 2:
                        dve.wait_ge(pe_pv, NU * b + n + 1)
                        nc.vector.tensor_copy(Phl[:, k % 4, 0, :, :], P32[:, k % 4, :, :]).then_inc(dve_hi, 1)
                        dve.wait_ge(dve_hi, (NU // 2) * b + odd + 1)
                    nc.vector.tensor_tensor(Phl[:, k % 4, 1, :, :], P32[:, k % 4, :, :], Phl[:, k % 4, 0, :, :],
                                            ALU.subtract).then_inc(dve_lo, 1)

                def normalise(pair, u):
                    dve.wait_ge(pe_cmb, (H // 2) * b + pair + 1 + 2)
                    acc = ps[:, 6 + u, 0:2 * VW * QT].rearrange("p (i s d) -> p i s d", i=QT, s=2)
                    nc.vector.reciprocal(rsum[:, u, :, :, :], acc[:, :, :, HD:VW]).then_inc(dve_rsum, 1)
                    dve.wait_ge(dve_rsum, (H // 2) * b + pair + 1)
                    nc.vector.tensor_tensor(vals[:, :, bass.ds(pair * 2 * HD, 2 * HD)].rearrange("p i (s d) -> p i s d", s=2),
                                            acc[:, :, :, 0:HD], rsum[:, u, :, :, :].to_broadcast([P, QT, 2, HD]),
                                            ALU.mult).then_inc(dve_vals, 1)

                def two_pairs(i, first):
                    for k in range(8):
                        low(8 * i + k, k, 4 * i + k // 2)
                        if k % 4 == 3 and not (first and k == 3):
                            normalise(2 * i + k // 4 - 1, 1 - k // 4)
                two_pairs(0, True)
                with dve.Fori(1, H // 4) as i:
                    two_pairs(i, False)
                normalise(H // 2 - 1, 1)
                dve.wait_ge(pe_vT, b + 1)
                nc.vector.tensor_copy(valsT[:, :, :], ps[:, 0:KC, :]).then_inc(dve_vT, 1)
                dve.wait_ge(pe_o, b + 1)
                for i in range(QT):
                    v = nc.vector.tensor_tensor(Hs[:, b * NT + i, :], ps[:, 2 + i // 2, D * (i % 2):D * (i % 2 + 1)],
                                                bo[:, :], ALU.add)
                v.then_inc(dve_h1, 1)

            def normalised(b):
                dve.wait_ge(dve_h1, b + 1)
                nc.vector.memset(tick[:, :], 0.0)
                for i in range(NT):
                    v = nc.vector.bn_stats(st6[:, i, :], Hs[:, b * NT + i, :])
                v.then_inc(dve_bcchain, 1)
                dve.wait_ge(dve_bcchain, 7 * b + 1)
                nc.vector.memset(tick[:, :], 0.0)
                for i in range(NT):
                    v = nc.vector.bn_aggr(mv[:, i, :], st6[:, i, :])
                v.then_inc(dve_bcchain, 1)
                dve.wait_ge(dve_bcchain, 7 * b + 2)
                nc.vector.tensor_scalar(mv[:, :, 1], mv[:, :, 1], EPS, None, ALU.add).then_inc(dve_stats, 1)
                dve.wait_ge(act_std, b + 1)
                nc.vector.reciprocal(rstd[:, :], rstd[:, :]).then_inc(dve_rstd, 1)
                dve.wait_ge(dve_rstd, b + 1)
                for i in range(NT):
                    v = nc.vector.tensor_scalar(xn[:, i, :], Hs[:, b * NT + i, :], mv[:, i, 0:1], rstd[:, i:i + 1],
                                                ALU.subtract, ALU.mult)
                v.then_inc(dve_xn, 1)

            def scan(b):
                dve.wait_ge(pe_xp, b + 1)
                base = 7 * b + 2
                nc.vector.tensor_copy(halves(bc32[:, :]), two_banks(2, 96)).then_inc(dve_bcchain, 1)
                dve.wait_ge(dve_bcchain, base + 1)
                nc.vector.tensor_copy(bcp[:, 0, :], bc32[:, :]).then_inc(dve_bcchain, 1)
                dve.wait_ge(dve_bcchain, base + 2)
                nc.vector.tensor_tensor(bc32[:, :], bc32[:, :], bcp[:, 0, :], ALU.subtract).then_inc(dve_bcchain, 1)
                dve.wait_ge(dve_bcchain, base + 3)
                nc.vector.tensor_copy(bcp[:, 1, :], bc32[:, :]).then_inc(dve_bcchain, 1)
                dve.wait_ge(dve_bcchain, base + 4)
                nc.vector.tensor_tensor(bc32[:, :], bc32[:, :], bcp[:, 1, :], ALU.subtract).then_inc(dve_bcchain, 1)
                dve.wait_ge(dve_bcchain, base + 5)
                nc.vector.tensor_copy(bcs[0:32, :], bcp[0:32, 0, :])
                nc.vector.tensor_copy(bcs[32:64, :], bcp[32:64, 1, :])
                nc.vector.tensor_copy(bcs[64:96, :], bc32[64:96, :]).then_inc(dve_bcs, 1)
                dve.wait_ge(pe_dt, b + 1)
                for c in range(KC):
                    v = nc.vector.tensor_scalar(halves(xb[:, c, :]), two_banks(4 + 2 * c), dtb[:, c:c + 1], None, ALU.add)
                v.then_inc(dve_xb, 1)
                dve.wait_ge(dve_xb, b + 1)
                nc.vector.scalar_tensor_tensor(out=sp[:, :, :], in0=xb[:, :, :], scalar=-1.0, in1=xb[:, :, :],
                                               op0=ALU.mult, op1=ALU.max).then_inc(dve_sp, 1)
                dve.wait_ge(act_sp, 2 * b + 2)
                nc.vector.scalar_tensor_tensor(out=delta[:, :, :], in0=xb[:, :, :], scalar=0.0, in1=sp[:, :, :],
                                               op0=ALU.max, op1=ALU.add).then_inc(dve_delta, 1)
                dve.wait_ge(dve_delta, b + 1)
                dve.wait_ge(act_uT, b + 1)
                nc.vector.tensor_tensor(dtu[:, :, :], delta[:, :, :], uT[:, :, :], ALU.mult).then_inc(dve_dtu, 1)
                dve.wait_ge(dve_dtu, b + 1)

                def recurrence(n, u, first):
                    dve.wait_ge(pe_bc, NS * b + n + 1)
                    for c in range(KC):
                        v = nc.vector.tensor_tensor(halves(dBu[:, u, c, :]), halves(dtu[:, c, :]), two_banks(0), ALU.mult)
                    v.then_inc(dve_dBu, 1)
                    dve.wait_ge(dve_dBu, NS * b + n + 1)
                    if not first:
                        dve.wait_ge(pool_hC, 2 * (NS * b + n - 1))
                    for c in range(KC):
                        dve.wait_ge(act_dA, 2 * (NS * b + n) + c + 1)
                        nc.vector.tensor_tensor_scan(hst[:, u, c, :], dA[:, u, c, :], dBu[:, u, c, :], 0.0,
                                                     ALU.mult, ALU.add).then_inc(dve_scan, 1)
                recurrence(0, 0, True)
                recurrence(1, 1, True)
                with dve.Fori(1, NS // 2) as i:
                    recurrence(2 * i, 0, False)
                    recurrence(2 * i + 1, 1, False)
                dve.wait_ge(pe_y, NS * (b + 1))
                for c in range(KC):
                    v = nc.vector.scalar_tensor_tensor(out=halves(xb[:, c, :]), in0=halves(uT[:, c, :]), scalar=dsk[:, c:c + 1],
                                                       in1=two_banks(4 + 2 * c), op0=ALU.mult, op1=ALU.add)
                v.then_inc(dve_yT, 1)
                dve.wait_ge(pe_yT, b + 1)
                for i in range(NT):
                    rows = P if i < QT else TXT
                    v = nc.vector.tensor_tensor(Hs[0:rows, b * NT + i, :], Hs[0:rows, b * NT + i, :],
                                                ps[0:rows, i // 2, D * (i % 2):D * (i % 2 + 1)], ALU.add)
                v.then_inc(dve_h2, 1)

            def layer_norm(r):
                with dve.Fori(0, G) as t:
                    v = nc.vector.bn_stats(lst[:, t, :], Hs[:, t, :])
                    v.then_inc(ln_chain, 1)
                n = [(r + 1) * G + 6 * r]
                dve.wait_ge(ln_chain, n[0])

                def link(ins):
                    n[0] += 1
                    ins.then_inc(ln_chain, 1)
                    dve.wait_ge(ln_chain, n[0])
                m0, m1, q0, q1 = (lst[:, :, k] for k in (1, 4, 2, 5))
                link(nc.vector.tensor_tensor(lmean[:, :], m0, m1, ALU.add))
                link(nc.vector.tensor_tensor(ltmp[:, :], m0, m1, ALU.subtract))
                link(nc.vector.scalar_tensor_tensor(out=ltmp[:, :], in0=ltmp[:, :], scalar=0.25, in1=ltmp[:, :],
                                                    op0=ALU.mult, op1=ALU.mult))
                link(nc.vector.tensor_tensor(lrstd[:, :], q0, q1, ALU.add))
                link(nc.vector.scalar_tensor_tensor(out=lrstd[:, :], in0=lrstd[:, :], scalar=1.0 / D, in1=ltmp[:, :],
                                                    op0=ALU.mult, op1=ALU.add))
                nc.vector.tensor_scalar(lrstd[:, :], lrstd[:, :], EPS, None, ALU.add).then_inc(ln_stats, 1)
                dve.wait_ge(ln_std, r + 1)
                link(nc.vector.reciprocal(lrstd[:, :], lrstd[:, :]))
                nc.vector.scalar_tensor_tensor(out=lbias[:, :], in0=lmean[:, :], scalar=-0.5, in1=lrstd[:, :],
                                               op0=ALU.mult, op1=ALU.mult).then_inc(ln_done, 1)

            def choose(r, n_experts, lgb, lg, then=None):
                def tile(t, u):
                    dve.wait_ge(pe_lg, r * G + t + 1)
                    nc.vector.tensor_copy(lgb[:, u, :], ps[:, 2 + u, 0:n_experts]).then_inc(dve_lg, 1)
                    dve.wait_ge(dve_lg, r * G + t + 1)
                    nc.vector.tensor_copy(lg[:, t, :], lgb[:, u, :])
                    nc.vector.max(m8b[:, u, :], lgb[:, u, :]).then_inc(best_chain, 1)
                    dve.wait_ge(best_chain, 3 * (r * G + t) + 1)
                    nc.vector.tensor_copy(best[:, t, :], m8b[:, u, 0:2])
                    nc.vector.max_index(i8b[:, u, :], m8b[:, u, :], lgb[:, u, :]).then_inc(best_chain, 1)
                    dve.wait_ge(best_chain, 3 * (r * G + t) + 2)
                    nc.vector.tensor_copy(besti[:, t, :], i8b[:, u, 0:2]).then_inc(best_chain, 1)
                    if then:
                        dve.wait_ge(best_chain, 3 * (r * G + t) + 3)
                        then(t, u)
                with dve.Fori(0, G // 2) as i:
                    tile(2 * i, 0)
                    tile(2 * i + 1, 1)
                dve.wait_ge(best_chain, 3 * (r + 1) * G)

            def one_expert():
                n = [0]

                def link(ins):
                    n[0] += 1
                    ins.then_inc(c3, 1)
                    dve.wait_ge(c3, n[0])
                dve.wait_ge(dve_h2, NB + 1)
                layer_norm(0)
                dve.wait_ge(b12_in, 16)
                nc.vector.tensor_copy(b12p[:, 0, :], b12[:, :]).then_inc(dve_bparts, 1)
                dve.wait_ge(dve_bparts, 1)
                link(nc.vector.tensor_tensor(b12[:, :], b12[:, :], b12p[:, 0, :], ALU.subtract))
                nc.vector.tensor_copy(b12p[:, 1, :], b12[:, :]).then_inc(dve_bparts, 1)
                dve.wait_ge(dve_bparts, 2)
                nc.vector.tensor_tensor(b12p[:, 2, :], b12[:, :], b12p[:, 1, :], ALU.subtract).then_inc(dve_bparts, 1)
                dve.wait_ge(late_in, 16 * N_LATE)
                choose(0, NE1, lgb, lg)
                flat = [P, G, NE1]
                link(nc.vector.tensor_tensor(hot[:, :, :], iota1[:, :].rearrange("p (o e) -> p o e", o=1).to_broadcast(flat),
                                             besti[:, :, 0:1].to_broadcast(flat), ALU.is_equal))
                nc.vector.tensor_tensor(hot[:, :, :], hot[:, :, :], real[:, :].rearrange("p (g o) -> p g o", o=1).to_broadcast(flat),
                                        ALU.mult).then_inc(dve_hot, 1)
                nc.vector.tensor_tensor(lg[:, :, :], lg[:, :, :], best[:, :, 0:1].to_broadcast(flat), ALU.subtract).then_inc(dve_ex, 1)
                dve.wait_ge(pe_rank, 1)
                link(nc.vector.tensor_copy(cnt[:, :, :], ps[:, 5, 0:G * NE1].rearrange("p (g e) -> p e g", e=NE1)))
                link(nc.vector.tensor_tensor_scan(cum[:, :, :].rearrange("p e g -> p (e g)"), keep[:, :],
                                                  cnt[:, :, :].rearrange("p e g -> p (e g)"), 0.0, ALU.mult, ALU.add))
                steps = [P, NE1, G]
                link(nc.vector.tensor_tensor(big[:, :, 0:G], cum[:, :, G - 1:G].to_broadcast(steps),
                                             iota128[:, :].rearrange("p (o g) -> p o g", o=1).to_broadcast(steps), ALU.is_gt))
                link(nc.vector.tensor_reduce(ntile[:, :], big[:, :, 0:G], AX.X, ALU.add))
                link(nc.vector.memset(toff[:, :], 1.0))
                link(nc.vector.tensor_tensor_scan(tend[:, :], toff[:, :], ntile[:, :], 0.0, ALU.mult, ALU.add))
                link(nc.vector.tensor_tensor(toff[:, :], tend[:, :], ntile[:, :], ALU.subtract))
                link(nc.vector.tensor_scalar(toff[:, :], toff[:, :], float(P), None, ALU.mult))
                link(nc.vector.tensor_tensor(cum[:, :, :], cum[:, :, :], cnt[:, :, :], ALU.subtract))
                link(nc.vector.tensor_tensor(cum[:, :, :], cum[:, :, :], toff[:, :].rearrange("p (e o) -> p e o", o=1).to_broadcast(steps), ALU.add))
                link(nc.vector.tensor_tensor(pos[:, :, :], cum[:, :, :].rearrange("p e g -> p g e"),
                                             ps[:, 4, 0:G * NE1].rearrange("p (g e) -> p g e", e=NE1), ALU.add))
                link(nc.vector.tensor_tensor(pos[:, :, :], pos[:, :, :], hot[:, :, :], ALU.mult))
                link(nc.vector.tensor_reduce(slotf[:, :], pos[:, :, :], AX.X, ALU.add))
                link(nc.vector.tensor_copy(slotg[:, :], slotf[:, :]))
                nc.vector.tensor_tensor(slots[:, :], slotf[:, :], nottoken[:, :], ALU.add).then_inc(dve_slots, 1)
                pairs = [P, MT, NE1]
                which = big[:, :, :].rearrange("p a b -> p (a b)").rearrange("p (m e) -> p m e", e=NE1)
                link(nc.vector.tensor_tensor(which, tend[:, :].rearrange("p (o e) -> p o e", o=1).to_broadcast(pairs),
                                             ramp[:, :].rearrange("p (m o) -> p m o", o=1).to_broadcast(pairs), ALU.is_le))
                link(nc.vector.tensor_reduce(te[:, :], which, AX.X, ALU.add))
                nc.vector.tensor_scalar(tei[:, :], te[:, :], float(NE1 - 1), None, ALU.min).then_inc(dve_te, 1)
                dve.wait_ge(act_ex, 1)
                link(nc.vector.tensor_reduce(gate[:, :], lg[:, :, :], AX.X, ALU.add))
                link(nc.vector.reciprocal(gate[:, :], gate[:, :]))
                link(nc.vector.tensor_tensor(gate[:, :], gate[:, :], real[:, :], ALU.mult))

                def step(j, u, first):
                    dve.wait_ge(pe_hidT, j + 1)
                    if not first:
                        dve.wait_ge(pe_down, j - 1)
                    nc.vector.tensor_copy(hidT[:, u, :, :], ps[:, 4 + u, :].rearrange("p (f t) -> p f t", f=FC)).then_inc(dve_hidT, 1)
                    dve.wait_ge(pe_down, j + 1)
                    if not first:
                        dve.wait_ge(yo_out[u], 8 * (j - u))
                    nc.vector.tensor_copy(yo[:, u, :], ps[:, 6 + u, 0:D]).then_inc(dve_yo, 1)
                step(0, 0, True)
                step(1, 1, True)
                with dve.Fori(1, MT // 2) as i:
                    step(2 * i, 0, False)
                    step(2 * i + 1, 1, False)
                for t in range(G):
                    dve.wait_ge(yg_in[t % YG], 16 * (t // YG + 1))
                    nc.vector.scalar_tensor_tensor(out=Hs[:, t, :], in0=yg[:, t % YG, :], scalar=gate[:, t:t + 1], in1=Hs[:, t, :],
                                                   op0=ALU.mult, op1=ALU.add).then_inc(dve_h3, 1)

            def causal():
                dve.wait_ge(dve_h3, G)
                layer_norm(1)
                dve.nop().then_inc(dve_h4, 1)
                dve.wait_ge(last_in, 16 * N_LAST)
                with dve.Fori(0, NB) as b:
                    dve.wait_ge(pe_qk4, b + 1)
                    for t in range(4):
                        nc.vector.tensor_scalar(QK4[:, t, 0:S], ps[:, t, :], bqk4[:, t:t + 1], None, ALU.add)
                        v = nc.vector.tensor_scalar(QK4[:, t, S:LT], ps[:, 4, P * t:P * (t + 1)], bqk4[:, t:t + 1], None, ALU.add)
                    v.then_inc(dve_qk4, 1)
                    dve.wait_ge(pe_v4, b + 1)
                    for i in range(NT):
                        v = nc.vector.tensor_tensor(V4[:, i, :], ps[:, 5 + i // 2, D * (i % 2):D * (i % 2 + 1)], bv4[:, :], ALU.add)
                    v.then_inc(dve_v4, 1)

                    def maxima(i):
                        dve.wait_ge(pe_s4, NT * b + i + 1)
                        row = ps[:, 2 * (i % 2):2 * (i % 2) + 2, :].rearrange("p b s -> p (b s)")
                        nc.vector.tensor_tensor(row[:, P * i:P * (i + 1)], row[:, P * i:P * (i + 1)], mask4[:, :],
                                                ALU.add).then_inc(dve_mask4, 1)
                        dve.wait_ge(dve_mask4, 2 * (NT * b + i) + 1)
                        nc.vector.tensor_reduce(nm4[:, i:i + 1], row[:, 0:P * (i + 1)], AX.X, ALU.max).then_inc(dve_mask4, 1)
                        dve.wait_ge(dve_mask4, 2 * (NT * b + i) + 2)
                        nc.vector.tensor_scalar(nm4[:, i:i + 1], nm4[:, i:i + 1], -float(D) ** -0.5, None, ALU.mult).then_inc(dve_nm4, 1)

                    def weighted(i):
                        dve.wait_ge(pe_pt4, NT * b + i + 1)
                        n = P * (i + 1)
                        nc.vector.tensor_copy(PT4[:, i % 2, 0:i + 1, :].rearrange("p j q -> p (j q)"),
                                              ps[:, 4:6, :].rearrange("p b s -> p (b s)")[:, 0:n]).then_inc(dve_pt4, 1)
                        dve.wait_ge(pe_pv4, NT * b + i + 1)
                        nc.vector.reciprocal(rs4[:, i:i + 1], rs4[:, i:i + 1]).then_inc(dve_rs4, 1)
                        dve.wait_ge(dve_rs4, NT * b + i + 1)
                        nc.vector.scalar_tensor_tensor(out=Hs[:, NT * b + i, :], in0=ps[:, 6 + i % 2, 0:D], scalar=rs4[:, i:i + 1],
                                                       in1=Hs[:, NT * b + i, :], op0=ALU.mult, op1=ALU.add).then_inc(dve_h4, 1)
                    maxima(0)
                    for i in range(1, NT):
                        maxima(i)
                        weighted(i - 1)
                    weighted(NT - 1)

            def two_experts():
                n = [0]

                def link(ins):
                    n[0] += 1
                    ins.then_inc(c5, 1)
                    dve.wait_ge(c5, n[0])
                dve.wait_ge(dve_h4, G + 1)
                layer_norm(2)

                def rank(t, u):
                    for k in range(2):
                        nc.vector.tensor_scalar(hotb[:, u, k, :], iota5[:, :], besti[:, t, k:k + 1], real5[:, bass.ds(t, 1)],
                                                ALU.is_equal, ALU.mult).then_inc(dve_hot5, 1)
                    for k in range(2):
                        dve.wait_ge(pe_rank5, 2 * t + k + 1)
                        nc.vector.tensor_tensor_reduce(out=junk[:, :], in0=hotb[:, u, k, :], in1=ps[:, 4 + k, 0:NE2], scale=1.0, scalar=0.0,
                                                       op0=ALU.mult, op1=ALU.add, accum_out=locb[:, u, k:k + 1]).then_inc(dve_rank5, 1)
                        dve.wait_ge(dve_rank5, 2 * t + k + 1)
                    nc.vector.tensor_copy(hot2[:, t, :], hotb[:, u, 1, :])
                    nc.vector.tensor_copy(loc[:, t, :], locb[:, u, :])
                    dve.wait_ge(pe_count5, 2 * t + 2)
                choose(1, NE2, lgb5, lg5, rank)
                flat = [P, G, NE2]
                link(nc.vector.tensor_copy(c1[:, :], ps[:, 4, 0:NE2]))
                link(nc.vector.tensor_tensor(lg5[:, :, :], lg5[:, :, :], best[:, :, 0:1].to_broadcast(flat), ALU.subtract))
                nc.vector.tensor_tensor(w5[:, :, :], best[:, :, :], best[:, :, 0:1].to_broadcast([P, G, 2]), ALU.subtract).then_inc(dve_ex5, 1)
                link(nc.vector.tensor_tensor(hot2f[:, :, :], hot2[:, :, :], c1[:, :].rearrange("p (o e) -> p o e", o=1).to_broadcast(flat), ALU.mult))
                link(nc.vector.tensor_reduce(den[:, :], hot2f[:, :, :], AX.X, ALU.add))
                link(nc.vector.tensor_tensor(loc[:, :, 1], loc[:, :, 1], den[:, :], ALU.add))
                link(nc.vector.tensor_scalar(v5[:, :, :], loc[:, :, :], float(CAP), None, ALU.is_lt))
                link(nc.vector.tensor_scalar(loc[:, :, :], loc[:, :, :], float(CAP - 1), None, ALU.min))
                link(nc.vector.scalar_tensor_tensor(out=rowf[:, :, :], in0=besti[:, :, :], scalar=float(CAP), in1=loc[:, :, :],
                                                    op0=ALU.mult, op1=ALU.add))
                link(nc.vector.tensor_copy(from5[:, :, :], rowf[:, :, :]))
                link(nc.vector.tensor_tensor(rowf[:, :, :], rowf[:, :, :],
                                             nottoken5[:, :].rearrange("p (g o) -> p g o", o=1).to_broadcast([P, G, 2]), ALU.add))
                link(nc.vector.scalar_tensor_tensor(out=rowf[:, :, :], in0=v5[:, :, :], scalar=-1e6, in1=rowf[:, :, :],
                                                    op0=ALU.mult, op1=ALU.add))
                nc.vector.tensor_scalar(to5[:, :, :], rowf[:, :, :], 1e6, None, ALU.add).then_inc(dve_to5, 1)
                dve.wait_ge(act_ex5, 1)
                link(nc.vector.tensor_reduce(den[:, :], lg5[:, :, :], AX.X, ALU.add))
                link(nc.vector.reciprocal(den[:, :], den[:, :]))
                link(nc.vector.tensor_tensor(w5[:, :, :], w5[:, :, :], den[:, :].rearrange("p (g o) -> p g o", o=1).to_broadcast([P, G, 2]), ALU.mult))
                link(nc.vector.tensor_reduce(den[:, :], w5[:, :, :], AX.X, ALU.add))
                link(nc.vector.tensor_scalar(den[:, :], den[:, :], FEPS, None, ALU.max))
                link(nc.vector.reciprocal(den[:, :], den[:, :]))
                link(nc.vector.tensor_tensor(w5[:, :, :], w5[:, :, :], den[:, :].rearrange("p (g o) -> p g o", o=1).to_broadcast([P, G, 2]), ALU.mult))
                link(nc.vector.tensor_tensor(w5[:, :, :], w5[:, :, :], v5[:, :, :], ALU.mult))

                def step(j, u, first):
                    dve.wait_ge(pe_y5, j + 1)
                    if not first:
                        dve.wait_ge(y5_out[u], 8 * (j - u))
                    for k in range(2):
                        nc.vector.tensor_copy(yo5[CAP * k:CAP * (k + 1), u, :], ps[CAP * k:CAP * (k + 1), 2 + u, D * k:D * (k + 1)]).then_inc(dve_y5, 1)
                step(0, 0, True)
                step(1, 1, True)
                with dve.Fori(1, NP2 // 2) as i:
                    step(2 * i, 0, False)
                    step(2 * i + 1, 1, False)
                for m in range(2 * G):
                    dve.wait_ge(yg_in[m % YG], 16 * (G // YG + m // YG + 1))
                    if m % 2:
                        dve.wait_ge(dve_h5, m)
                    nc.vector.scalar_tensor_tensor(out=Hs[:, m // 2, :], in0=yg5[:, m % YG, :], scalar=w5[:, m // 2, m % 2:m % 2 + 1],
                                                   in1=Hs[:, m // 2, :], op0=ALU.mult, op1=ALU.add).then_inc(dve_h5, 1)

            dve.wait_ge(act_acol, 1)
            nc.vector.tensor_scalar(acol[:, :], acol[:, :], -1.0, None, ALU.mult).then_inc(dve_init, 1)
            dve.wait_ge(consts_in, 16 * N_CONSTS)
            dve.wait_ge(txt_in, 16 * NB)
            dve.wait_ge(pool_init, 6)
            dve.nop().then_inc(dve_h2, 1)
            for _ in range(4):
                dve.nop().then_inc(dve_lo, 1)
            for _ in range(2):
                dve.nop().then_inc(dve_vals, 1)
            split(0)
            with dve.Fori(0, NB - 1) as b:
                attention(b)
                normalised(b)
                split(b + 1)
                scan(b)
            attention(NB - 1)
            normalised(NB - 1)
            scan(NB - 1)
            if STAGE >= 3:
                one_expert()
            if STAGE >= 4:
                causal()
            if STAGE >= 5:
                two_experts()


def layouts(x, txt, L0_tok_w_qkv, L0_tok_b_qkv, L0_tok_w_out, L0_tok_b_out, L0_attn_A_log, L0_attn_D_skip,
            L0_attn_dt_proj_w, L0_attn_dt_proj_b, L0_attn_x_proj_w, L0_ffn_router_w, L0_ffn_w1, L0_ffn_b1, L0_ffn_w2,
            L0_ffn_b2, L1_attn_Wq, L1_attn_bq, L1_attn_Wk, L1_attn_bk, L1_attn_Wv, L1_attn_bv, L1_ffn_wg, L1_ffn_we):
    import numpy as np

    def c(a):
        return np.ascontiguousarray(np.asarray(a))

    def ones_bf16(a):
        return (np.asarray(a) * 0x3F80).astype(np.uint16)

    def chunked(a):
        return c(np.asarray(a).reshape(-1, 128, a.shape[1]).transpose(1, 0, 2))

    def columns(v):
        return c(np.asarray(v).reshape(-1, 128).T)

    w = np.asarray(L0_tok_w_qkv).reshape(16, 3, 16, 256)
    bq = np.asarray(L0_tok_b_qkv).reshape(16, 3, 16)
    xp = np.asarray(L0_attn_x_proj_w)
    sel = np.zeros((96, 32, 128))
    for n in range(32):
        sel[n::32, n] = 1
    token = (np.arange(20) % 5 * 128 + np.arange(128)[:, None] < 589) * 1.0

    def rows(v):
        return np.tile(np.asarray(v, np.float32), (128, 1))
    sel3 = np.zeros((2, 64, 2, 17), np.float32)
    for head in range(2):
        for part in range(3):
            sel3[head, 17 * part:17 * (part + 1), head] = np.eye(17)
    sel3 = sel3.reshape(128, 34)
    return {
        "xT": c(np.asarray(x)[:, 0].transpose(0, 2, 1).reshape(4, 2, 128, 512).transpose(0, 2, 1, 3)),
        "txt": c(txt),
        "wqkvT": chunked(w.transpose(1, 0, 2, 3).reshape(768, 256).T),
        "bqk": columns(bq[:, 0:2].transpose(1, 0, 2).reshape(512)),
        "bv": c(bq[:, 2].reshape(256)),
        "woT": chunked(np.asarray(L0_tok_w_out).T),
        "bo": c(L0_tok_b_out),
        "ident": np.eye(128, dtype=np.float32),
        "ones3": ones_bf16(np.ones((3, 16, 512))),
        "xpwT": chunked(xp[:64].T),
        "xpbcT": chunked(np.concatenate([xp[64:]] * 3).T),
        "dtwT": c(np.asarray(L0_attn_dt_proj_w).T),
        "dtb": columns(L0_attn_dt_proj_b),
        "dsk": columns(L0_attn_D_skip),
        "alog": c(np.asarray(L0_attn_A_log).reshape(2, 128, 16).transpose(1, 0, 2).reshape(128, 32)),
        "sel3": sel3,
        "sel": ones_bf16(sel),
        "w1": c(np.asarray(L0_ffn_w1).reshape(14, 2, 128, 512).transpose(2, 0, 1, 3)),
        "w2": c(np.asarray(L0_ffn_w2).reshape(14, 4, 128, 256).transpose(2, 0, 1, 3)),
        "b12": c(np.concatenate([np.asarray(L0_ffn_b1), np.asarray(L0_ffn_b2)], 1)),
        "rw": chunked(np.asarray(L0_ffn_router_w)),
        "tri": ones_bf16(np.triu(np.ones((128, 128)), 1)),
        "onesm": ones_bf16(np.ones((128, 128))),
        "real": token.astype(np.float32),
        "nottoken": ((1 - token) * 1e6).astype(np.float32),
        "iota1": rows(np.arange(14)),
        "iota128": rows(np.arange(20) * 128),
        "ramp": rows(np.arange((4 * 589 + 14 * 127) // 128)),
        "keep1": rows(np.arange(14 * 20) % 20 != 0),
        "w4T": chunked(np.concatenate([np.asarray(L1_attn_Wq), np.asarray(L1_attn_Wk), np.asarray(L1_attn_Wv)]).T),
        "bqk4": columns(np.concatenate([np.asarray(L1_attn_bq), np.asarray(L1_attn_bk)])),
        "bv4": c(L1_attn_bv),
        "mask4": np.triu(np.full((128, 128), -3e38, np.float32), 1),
        "wg": chunked(np.asarray(L1_ffn_wg)),
        "we": c(np.asarray(L1_ffn_we).reshape(128, 2, 128, 256).transpose(2, 0, 1, 3)),
        "tri5": ones_bf16(np.stack([np.triu(np.ones((128, 128)), 1), np.tril(np.ones((128, 128)))], 1)),
        "iota5": rows(np.arange(128)),
        "ones3p": ones_bf16(np.ones((3, 128))),
    }


def kernel(**inputs):
    import numpy as _np
    import concourse.bacc as _bacc
    from concourse import mybir as _mybir
    from concourse.bass_utils import run_bass_kernel_spmd as _run

    nc = _bacc.Bacc("TRN2", target_bir_lowering=False, num_devices=1)
    arrays = layouts(**inputs)
    args = {n: nc.dram_tensor(f"in_{n}", a.shape, _mybir.dt.from_np(a.dtype), kind="ExternalInput").ap() for n, a in arrays.items()}
    out = nc.dram_tensor("out", (4, 589, 256), _mybir.dt.float32, kind="ExternalOutput").ap()
    fusion_kernel(nc, args, out)
    r = _run(nc, [{f"in_{n}": a for n, a in arrays.items()}], core_ids=[0])
    return r.results[0]["out"]
```

```python
import concourse.bass as bass
from concourse import mybir
from contextlib import ExitStack



def fusion_kernel(nc, A, out):
    F32, BF16, FP16, U32 = mybir.dt.float32, mybir.dt.bfloat16, mybir.dt.float16, mybir.dt.uint32
    ALU, ACT, AX = mybir.AluOpType, mybir.ActivationFunctionType, mybir.AxisListType

    P = 128
    NB, S, D = 4, 512, 256
    TXT = 77
    L = S + TXT
    LP = L + 1
    HC = LP // 2
    KC = D // P
    QT = S // P
    NT = QT + 1
    H, HD = 16, D // 16
    VBANKS = (7, 3)
    HH = H // 2
    PART = 6 * HD
    KR = PART + 3
    VW = HD + 1
    NU = 2 * H
    NS = 16
    RANK = 64
    EPS = 1e-5
    LT = NT * P
    NE2, CAP = 128, 64
    NP2 = NE2 // 2
    RING, LOAD = 32, 8
    GP = LOAD // 2
    DW = D + 1
    NOWHERE = 1 << 20
    TG = 4
    FEPS = 1.1920928955078125e-07
    NE1, FF = 14, 512
    FC = FF // P
    MT = (NB * L + NE1 * (P - 1)) // P
    QPARTS = [0, 0, 1, 1, 0, 2]
    KPARTS = [0, 1, 0, 1, 2, 0]

    ctx = ExitStack()
    with ctx:
        def sb(name, shape, dt=F32):
            return ctx.enter_context(nc.sbuf_tensor(name, shape, dt))

        def sem(name):
            return ctx.enter_context(nc.semaphore(name))

        def dram(name, shape, dt=F32):
            return nc.dram_tensor(name, shape, dt).ap()

        ps = ctx.enter_context(nc.psum_tensor("ps", [P, 8, 512], F32))

        Hs = sb("Hs", [P, NB * NT, D])
        ident = sb("ident", [P, P])
        zeros = sb("zeros", [P, DW])
        pooltick = sb("pooltick", [P, 1])
        tick2 = sb("tick2", [P, 1])
        G = NB * NT
        GG = G // TG
        lst = sb("lst", [P, G, 6])
        lmean = sb("lmean", [P, G])
        lrstd = sb("lrstd", [P, G])
        ltmp = sb("ltmp", [P, G])
        lbias = sb("lbias", [P, G])
        m8b = sb("m8b", [P, TG, 8])
        i8b = sb("i8b", [P, TG, 8], U32)
        best = sb("best", [P, G, 2])
        besti = sb("besti", [P, G, 2])
        early = ExitStack()

        def eb(name, shape, dt=F32):
            return early.enter_context(nc.sbuf_tensor(name, shape, dt))
        xT = eb("xT", [P, KC, S])
        wqkv = eb("wqkv", [P, KC, 3 * D])
        wo = eb("wo", [P, KC, D])
        bqk = eb("bqk", [P, 4])
        bv = eb("bv", [P, D])
        bo = eb("bo", [P, D])
        Qst = eb("Qst", [KR, H, S], BF16)
        Kst = eb("Kst", [KR, H, S], BF16)
        v32 = eb("v32", [P, QT, D])
        Vst = eb("Vst", [P, QT, H, P], BF16)
        sel3 = eb("sel3", [P, 2 * VW])
        OT = eb("OT", [P, 2, S])
        qk32 = eb("qk32", [P, 4, S])
        parts = eb("parts", [P, 3, 4, S], BF16)
        mx = eb("mx", [P, 2, P // QT, QT])
        mneg = eb("mneg", [HH * QT, 2, P])
        mparts = eb("mparts", [HH * QT, 2, 3, P], BF16)
        rsum = eb("rsum", [P, 2, QT, 2, 1])
        vals = eb("vals", [P, QT, D])
        valsT = eb("valsT", [P, KC, S])
        xpw = eb("xpw", [P, KC, RANK])
        xpbc = eb("xpbc", [P, KC, 96])
        dtw = eb("dtw", [RANK, D])
        dtb = eb("dtb", [P, KC])
        dsk = eb("dsk", [P, KC])
        alog = eb("alog", [P, KC * NS])
        acol = eb("acol", [P, KC * NS])
        sel = eb("sel", [96, 2 * NS, P], BF16)
        tick = eb("tick", [P, 1])
        st6 = eb("st6", [P, NT, 6])
        mv = eb("mv", [P, NT, 2])
        rstd = eb("rstd", [P, NT])
        xn = eb("xn", [P, NT, D])
        uT = eb("uT", [P, KC, LP])
        dlow = eb("dlow", [RANK, LP])
        bcs = eb("bcs", [96, LP], BF16)
        xb = eb("xb", [P, KC, LP])
        delta = eb("delta", [P, KC, LP])
        dtu = eb("dtu", [P, KC, LP])
        Cb = eb("Cb", [P, 2, LP])

        turn1, turn2 = ExitStack(), ExitStack()
        P32 = turn1.enter_context(nc.sbuf_tensor("P32", [P, 4, 2, S], F32))
        Phl = turn1.enter_context(nc.sbuf_tensor("Phl", [P, 4, 2, 2, S], FP16))
        turn1.close()
        dA = turn2.enter_context(nc.sbuf_tensor("dA", [P, 2, KC, LP], F32))
        dBu = turn2.enter_context(nc.sbuf_tensor("dBu", [P, 2, KC, LP], F32))
        hst = turn2.enter_context(nc.sbuf_tensor("hst", [P, 2, KC, LP], F32))
        hC = turn2.enter_context(nc.sbuf_tensor("hC", [P, 2, KC, LP], F32))
        turn2.close()
        turn2 = ExitStack()
        turn2.enter_context(nc.sbuf_tensor("skip_dA", [P, 4, KC, LP], F32))
        bc32 = turn2.enter_context(nc.sbuf_tensor("bc32", [96, LP], F32))
        bcp = turn2.enter_context(nc.sbuf_tensor("bcp", [96, 2, LP], BF16))
        sp = turn2.enter_context(nc.sbuf_tensor("sp", [P, KC, LP], F32))
        turn2.close()
        early.close()
        xab = sb("xab", [P, TG, D])
        xaT = sb("xaT", [P, TG, KC, P])
        late = ExitStack()

        def lb(name, shape, dt=F32):
            return late.enter_context(nc.sbuf_tensor(name, shape, dt))
        yg_place3 = ExitStack()
        yg = yg_place3.enter_context(nc.sbuf_tensor("yg", [P, G, D], F32))
        yg_place3.close()
        W1 = lb("W1", [P, NE1, KC, FF])
        W2 = lb("W2", [P, NE1, FC, D])
        b12 = lb("b12", [NE1, FF + D])
        b12p = lb("b12p", [NE1, 3, FF + D], BF16)
        brow = lb("brow", [3, NE1, FF + D], BF16)
        ones3 = lb("ones3", [3, P], BF16)
        rw = lb("rw", [P, KC, NE1])
        tri = lb("tri", [P, P], BF16)
        onesm = lb("onesm", [P, P], BF16)
        real = lb("real", [P, G])
        iota1 = lb("iota1", [P, NE1])
        iota128 = lb("iota128", [P, G])
        ramp = lb("ramp", [P, MT])
        keep = lb("keep", [P, NE1 * G])
        lg = lb("lg", [P, G, NE1])
        home = lb("home", [P, G])
        dest = lb("dest", [P, 2], U32)
        lgb = lb("lgb", [P, TG, NE1])
        nottoken = lb("nottoken", [P, G])
        hot = lb("hot", [P, G, NE1], BF16)
        cnt = lb("cnt", [P, NE1, G])
        cum = lb("cum", [P, NE1, G])
        big = lb("big", [P, NE1, MT])
        ntile = lb("ntile", [P, NE1])
        tend = lb("tend", [P, NE1])
        toff = lb("toff", [P, NE1])
        pos = lb("pos", [P, G, NE1])
        slotf = lb("slotf", [P, G])
        slots = lb("slots", [P, G], U32)
        te = lb("te", [P, MT])
        tei = lb("tei", [P, MT], U32)
        gate = lb("gate", [P, G])
        turn3 = ExitStack()
        xa = turn3.enter_context(nc.sbuf_tensor("xa", [P, G, DW], F32))
        turn3.close()
        xg = lb("xg", [P, 2, DW])
        xgT = lb("xgT", [P, 2, KC, P])
        hid = lb("hid", [P, 2, FF])
        hidT = lb("hidT", [P, 2, FC, P])
        yo = lb("yo", [P, 2, D])
        late.close()
        last = ExitStack()

        def tb(name, shape, dt=F32):
            return last.enter_context(nc.sbuf_tensor(name, shape, dt))
        yg_place = ExitStack()
        yg5 = yg_place.enter_context(nc.sbuf_tensor("yg5", [P, 2, G, D], F32))
        yg_place.close()
        ring = tb("ring", [P, RING, KC, D])
        wg = tb("wg", [P, KC, NE2])
        tri5 = tb("tri5", [P, 2, P], BF16)
        nottoken5 = tb("nottoken5", [P, G])
        home5 = tb("home5", [P, 2, G])
        iota5 = tb("iota5", [P, NE2])
        turn4 = ExitStack()

        def qb(name, shape, dt=F32):
            return turn4.enter_context(nc.sbuf_tensor(name, shape, dt))
        w4 = qb("w4", [P, KC, 3 * D])
        bqk4 = qb("bqk4", [P, 4])
        bv4 = qb("bv4", [P, D])
        mask4 = qb("mask4", [P, P])
        xn4 = qb("xn4", [P, NT, D])
        xT4 = qb("xT4", [P, KC, LT])
        QK4 = qb("QK4", [P, 4, LT])
        V4 = qb("V4", [P, NT, D])
        P4 = qb("P4", [P, 2, LT])
        PT4 = qb("PT4", [P, 2, NT, P])
        nm4 = qb("nm4", [P, NT])
        rs4 = qb("rs4", [P, NT])
        turn4.close()
        lgb5 = tb("lgb5", [P, TG, NE2])
        lg5 = tb("lg5", [P, G, NE2])
        bm5 = tb("bm5", [P, TG, 2])
        hotb = tb("hotb", [P, TG, 2, NE2], BF16)
        hred = tb("hred", [P, 2, NE2])
        hsum = tb("hsum", [P, 2, NE2], BF16)
        hot2 = tb("hot2", [P, G, NE2], BF16)
        hot2f = tb("hot2f", [P, G, NE2])
        junk = tb("junk", [P, TG, 2, NE2])
        locb = tb("locb", [P, TG, 2])
        over5 = tb("over5", [P, TG])
        row5 = tb("row5", [P, TG])
        loc = tb("loc", [P, G, 2])
        c1 = tb("c1", [P, NE2])
        w5 = tb("w5", [P, G, 2])
        v5 = tb("v5", [P, G, 2])
        den = tb("den", [P, G])
        rowf = tb("rowf", [P, G])
        to5 = tb("to5", [P, 2, G], U32)
        dest5 = tb("dest5", [P, 2, GP], U32)
        turn5 = ExitStack()
        xa5 = turn5.enter_context(nc.sbuf_tensor("xa5", [P, G, DW], F32))
        turn5.close()
        yo5 = tb("yo5", [P, 2, GP, D])
        xg5 = tb("xg5", [P, 2, GP, DW])
        xgT5 = tb("xgT5", [P, 2, KC, P])
        last.close()

        qk_dram = dram("qk_dram", [NB, 3, 2, D, S], BF16)
        xs_dram = dram("xs_dram", [MT * P, DW])
        ys_dram = dram("ys_dram", [G * P, D])
        b_dram = dram("b_dram", [3, NE1, FF + D], BF16)
        xs5_dram = dram("xs5_dram", [NE2 * CAP, DW])
        ys5_dram = dram("ys5_dram", [2 * G * P, D])
        m_dram = dram("m_dram", [NB, 2, 3, HH * QT * P], BF16)

        consts_in = sem("consts_in")
        txt_in = sem("txt_in")
        x_in = sem("x_in")
        parts_out = [sem(f"parts_out{k}") for k in range(3)]
        stacks_in = sem("stacks_in")
        mrow_out = sem("mrow_out")
        mrow_in = [sem("mrow_in0"), sem("mrow_in1")]
        out_done = sem("out_done")
        pool_init = sem("pool_init")
        pe_qk = sem("pe_qk")
        pe_v = sem("pe_v")
        pe_s = sem("pe_s")
        pe_mT = sem("pe_mT")
        pe_st = sem("pe_st")
        pe_pv = sem("pe_pv")
        pe_vT = sem("pe_vT")
        pe_o = sem("pe_o")
        dve_init = sem("dve_init")
        dve_v32 = sem("dve_v32")
        act_v1 = sem("act_v1")
        dve_vr = sem("dve_vr")
        act_v2 = sem("act_v2")
        dve_mchain = sem("dve_mchain")
        dve_hi = sem("dve_hi")
        dve_lo = sem("dve_lo")
        act_OT = sem("act_OT")
        pe_cmb = sem("pe_cmb")
        dve_qk32 = sem("dve_qk32")
        dve_res = sem("dve_res")
        dve_p3 = sem("dve_p3")
        dve_v = sem("dve_v")
        dve_max = sem("dve_max")
        dve_mneg = sem("dve_mneg")
        dve_mparts = sem("dve_mparts")
        dve_rsum = sem("dve_rsum")
        dve_vals = sem("dve_vals")
        dve_vT = sem("dve_vT")
        dve_h1 = sem("dve_h1")
        act_acol = sem("act_acol")
        act_p1 = sem("act_p1")
        act_p2 = sem("act_p2")
        act_exp = sem("act_exp")
        dve_stats = sem("dve_stats")
        act_std = sem("act_std")
        dve_rstd = sem("dve_rstd")
        dve_xn = sem("dve_xn")
        pe_uT = sem("pe_uT")
        act_uT = sem("act_uT")
        pe_xp = sem("pe_xp")
        act_dlow = sem("act_dlow")
        dve_bcs = sem("dve_bcs")
        dve_bcchain = sem("dve_bcchain")
        pe_dt = sem("pe_dt")
        dve_xb = sem("dve_xb")
        dve_sp = sem("dve_sp")
        act_sp = sem("act_sp")
        dve_delta = sem("dve_delta")
        dve_dtu = sem("dve_dtu")
        pe_bc = sem("pe_bc")
        act_dA = sem("act_dA")
        act_C = sem("act_C")
        dve_dBu = sem("dve_dBu")
        dve_scan = sem("dve_scan")
        pool_hC = sem("pool_hC")
        pe_y = sem("pe_y")
        dve_yT = sem("dve_yT")
        pe_yT = sem("pe_yT")
        dve_h2 = sem("dve_h2")
        late_in = sem("late_in")
        w_in = sem("w_in")
        b12_in = sem("b12_in")
        b_out = sem("b_out")
        brow_in = sem("brow_in")
        ln_chain = sem("ln_chain")
        ln_stats = sem("ln_stats")
        ln_std = sem("ln_std")
        ln_done = sem("ln_done")
        dve_bparts = sem("dve_bparts")
        zero_out = sem("zero_out")
        pe_xaT = sem("pe_xaT")
        act_xaT = sem("act_xaT")
        pe_lg = sem("pe_lg")
        dve_lg = sem("dve_lg")
        c3 = sem("c3")
        dve_hot = sem("dve_hot")
        pe_rank = sem("pe_rank")
        dve_slots = sem("dve_slots")
        dve_te = sem("dve_te")
        dve_ex = sem("dve_ex")
        act_ex = sem("act_ex")
        rows_out = sem("rows_out")
        tile_in0 = sem("tile_in0")
        tile_in1 = sem("tile_in1")
        pe_xg = sem("pe_xg")
        act_xg = sem("act_xg")
        pe_up = sem("pe_up")
        act_gelu = sem("act_gelu")
        pe_hidT = sem("pe_hidT")
        dve_hidT = sem("dve_hidT")
        pe_down = sem("pe_down")
        dve_yo = sem("dve_yo")
        yo_out = [sem("yo_out0"), sem("yo_out1")]
        yg_in = [sem(f"yg_in{b}") for b in range(NB)]
        best_chain = sem("best_chain")
        act_xab = sem("act_xab")
        act_xa = sem("act_xa")
        dve_xa = sem("dve_xa")
        dve_h3 = sem("dve_h3")
        last_in = sem("last_in")
        act_xn4 = sem("act_xn4")
        pe_xT4 = sem("pe_xT4")
        act_xT4 = sem("act_xT4")
        pe_qk4 = sem("pe_qk4")
        pe_v4 = sem("pe_v4")
        dve_qk4 = sem("dve_qk4")
        dve_v4 = sem("dve_v4")
        pe_s4 = sem("pe_s4")
        dve_mask4 = sem("dve_mask4")
        dve_nm4 = sem("dve_nm4")
        act_p4 = sem("act_p4")
        pe_pt4 = sem("pe_pt4")
        dve_pt4 = sem("dve_pt4")
        pe_pv4 = sem("pe_pv4")
        dve_rs4 = sem("dve_rs4")
        dve_h4 = sem("dve_h4")
        ring_in = [sem(f"ring_in{k}") for k in range(RING // LOAD)]
        dve_hot5 = sem("dve_hot5")
        pe_rank5 = sem("pe_rank5")
        dve_rank5 = sem("dve_rank5")
        pe_count5 = sem("pe_count5")
        c5 = sem("c5")
        dve_ex5 = sem("dve_ex5")
        dve_to5 = sem("dve_to5")
        rows5_out = sem("rows5_out")
        tile5_in = [sem("tile5_in0"), sem("tile5_in1")]
        dve_dest5 = sem("dve_dest5")
        dve_dest = sem("dve_dest")
        pool_home = sem("pool_home")
        pe_xg5 = sem("pe_xg5")
        act_xg5 = sem("act_xg5")
        pe_y5 = sem("pe_y5")
        dve_y5 = sem("dve_y5")
        y5_out = [sem("y5_out0"), sem("y5_out1")]
        dve_h5 = sem("dve_h5")
        N_CONSTS = 15
        N_LAST = 9
        N_LATE = 11

        def bias_rows(name):
            return A[name].rearrange("(o d) -> o d", o=1).to_broadcast([P, D])

        def two_banks(lo, rows=P):
            return ps[0:rows, lo:lo + 2, 0:HC]

        def vhead(hd):
            return v32[:, :, :].rearrange("p j (g s d) -> p (j g) s d", s=2, d=HD)[:, :, hd, :]

        def vpart(hd, part):
            lo = (P // 2) * hd + VW * part
            return Vst[:, :, :, :].rearrange("p j (g s) c -> p (j g) s c", s=2)[:, :, hd, lo:lo + HD]

        def halves(ap):
            return ap.rearrange("p (c t) -> p c t", c=2)

        A = {n: a.bitcast(BF16) if n in ("sel", "ones3", "tri", "onesm", "tri5", "ones3p") else a for n, a in A.items()}
        block = ctx.enter_context(nc.Block())

        @block.sync
        def _(q):
            q.dma_start(xT[:, :, :], A["xT"][0]).then_inc(x_in, 16)
            q.dma_start(wqkv[:, :, :], A["wqkvT"]).then_inc(consts_in, 16)
            q.dma_start(bqk[:, :], A["bqk"]).then_inc(consts_in, 16)
            q.dma_start(bv[:, :], bias_rows("bv")).then_inc(consts_in, 16)
            q.dma_start(bo[:, :], bias_rows("bo")).then_inc(consts_in, 16)
            q.dma_start(wo[:, :, :], A["woT"]).then_inc(consts_in, 16)
            q.dma_start(ident[:, :], A["ident"]).then_inc(consts_in, 16)
            q.dma_start(xpw[:, :, :], A["xpwT"]).then_inc(consts_in, 16)
            q.dma_start(xpbc[:, :, :], A["xpbcT"]).then_inc(consts_in, 16)
            q.dma_start(dtw[:, :], A["dtwT"]).then_inc(consts_in, 16)
            q.dma_start(dtb[:, :], A["dtb"]).then_inc(consts_in, 16)
            q.dma_start(dsk[:, :], A["dsk"]).then_inc(consts_in, 16)
            q.dma_start(alog[:, :], A["alog"]).then_inc(consts_in, 16)
            q.dma_start(sel[:, :, :], A["sel"]).then_inc(consts_in, 16)
            q.dma_start(Kst[PART:KR, :, :], A["ones3"]).then_inc(consts_in, 16)
            q.dma_start(sel3[:, :], A["sel3"]).then_inc(consts_in, 16)
            q.wait_ge(pool_init, 2)
            for b in range(NB):
                q.dma_start(Hs[0:TXT, b * NT + QT, :], A["txt"][b]).then_inc(txt_in, 16)
            def load_x(b):
                q.wait_ge(pe_v, b)
                q.dma_start(xT[:, :, :], A["xT"][b]).then_inc(x_in, 16)

            def restack(b):
                made = (act_p1, act_p2, dve_p3)

                def out_part(part):
                    q.wait_ge(made[part], 4 * (b + 1))
                    q.dma_start(qk_dram[b, part].rearrange("a (m p) s -> p (a m) s", p=P),
                                parts[:, part, :, :]).then_inc(parts_out[part], 16)

                def in_part(part):
                    q.wait_ge(parts_out[part], 16 * (b + 1))
                    for stack, a, order in ((Qst, 0, QPARTS), (Kst, 1, KPARTS)):
                        for g in range(len(order)):
                            if order[g] == part:
                                q.dma_start(stack[HD * g:HD * (g + 1), :, :],
                                            qk_dram[b, part, a].rearrange("(h d) s -> d h s", d=HD)).then_inc(stacks_in, 16)
                out_part(0)
                out_part(1)
                in_part(0)
                out_part(2)
                in_part(1)
                in_part(2)

            def maxima_rows(b):
                for half in range(2):
                    n = 2 * b + half + 1
                    q.wait_ge(dve_mparts, n)
                    q.dma_start(m_dram[b, half].rearrange("a (r s) -> r a s", s=P), mparts[:, half, :, :]).then_inc(mrow_out, 16)
                    q.wait_ge(mrow_out, 16 * n)
                    q.dma_start(Qst[PART:KR, HH * half:HH * (half + 1), :].rearrange("p h s -> p (h s)"), m_dram[b, half]).then_inc(mrow_in[half], 16)
            restack(0)
            load_x(1)
            maxima_rows(0)
            q.dma_start(xs_dram.rearrange("(j p) d -> p j d", p=P),
                        zeros[:, :].rearrange("p (o d) -> p o d", o=1).to_broadcast([P, MT, DW])).then_inc(zero_out, 16)
            q.dma_start(ys_dram.rearrange("(j p) d -> p j d", p=P),
                        zeros[:, 0:D].rearrange("p (o d) -> p o d", o=1).to_broadcast([P, G, D])).then_inc(zero_out, 16)
            q.dma_start(xs5_dram.rearrange("(j p) d -> p j d", p=P),
                        zeros[:, :].rearrange("p (o d) -> p o d", o=1).to_broadcast([P, NP2, DW])).then_inc(zero_out, 16)
            q.dma_start(ys5_dram.rearrange("(j p) d -> p j d", p=P),
                        zeros[:, 0:D].rearrange("p (o d) -> p o d", o=1).to_broadcast([P, 2 * G, D])).then_inc(zero_out, 16)
            restack(1)
            with q.Fori(1, NB - 1) as b:
                load_x(b + 1)
                maxima_rows(b)
                restack(b + 1)
            maxima_rows(NB - 1)
            q.wait_ge(dve_h2, NB + 1)
            q.dma_start(b12[:, :], A["b12"]).then_inc(b12_in, 16)
            for dst, name in ((rw[:, :, :], "rw"), (tri[:, :], "tri"), (onesm[:, :], "onesm"), (real[:, :], "real"),
                              (iota1[:, :], "iota1"), (iota128[:, :], "iota128"), (ramp[:, :], "ramp"),
                              (keep[:, :], "keep1"), (nottoken[:, :], "nottoken"), (ones3[:, :], "ones3p")):
                q.dma_start(dst, A[name]).then_inc(late_in, 16)
            q.dma_start(home[:, :], A["home5"][:, 0, :]).then_inc(late_in, 16)
            for e in range(0, NE1, 2):
                q.dma_start(W1[:, e:e + 2, :, :], A["w1"][:, e:e + 2]).then_inc(w_in, 16)
                q.dma_start(W2[:, e:e + 2, :, :], A["w2"][:, e:e + 2]).then_inc(w_in, 16)
            q.wait_ge(dve_bparts, 3)
            q.dma_start(b_dram.rearrange("k e f -> e k f"), b12p[:, :, :]).then_inc(b_out, 16)
            q.wait_ge(b_out, 16)
            q.dma_start(brow[:, :, :], b_dram).then_inc(brow_in, 16)
            q.wait_ge(rows_out, 16 * G)
            q.wait_ge(zero_out, 64)

            def tile_load(j, u, tile_in):
                q.wait_ge(pe_xg, j - 1)
                q.wait_ge(dve_dest, j - 1)
                q.dma_start(xg[:, u, :], xs_dram[bass.ds(j * P, P), :]).then_inc(tile_in, 16)
            q.dma_start(xg[:, 0, :], xs_dram[0:P, :]).then_inc(tile_in0, 16)
            q.dma_start(xg[:, 1, :], xs_dram[P:2 * P, :]).then_inc(tile_in1, 16)
            with q.Fori(1, MT // 2) as i:
                tile_load(2 * i, 0, tile_in0)
                tile_load(2 * i + 1, 1, tile_in1)
            q.wait_ge(pe_down, MT)
            q.wait_ge(yo_out[0], 8 * MT)
            q.wait_ge(yo_out[1], 8 * MT)
            for b in range(NB):
                q.dma_start(yg[:, NT * b:NT * (b + 1), :],
                            ys_dram.rearrange("(n p) d -> p n d", p=P)[:, NT * b:NT * (b + 1), :]).then_inc(yg_in[b], 16)
            q.wait_ge(dve_h3, G)
            for dst, name in ((w4[:, :, :], "w4T"), (bqk4[:, :], "bqk4"), (mask4[:, :], "mask4"), (wg[:, :, :], "wg"),
                              (tri5[:, :, :], "tri5"), (home5[:, :, :], "home5"), (nottoken5[:, :], "nottoken"),
                              (iota5[:, :], "iota5")):
                q.dma_start(dst, A[name]).then_inc(last_in, 16)
            q.dma_start(bv4[:, :], bias_rows("bv4")).then_inc(last_in, 16)
            for k in range(RING // LOAD):
                q.dma_start(ring[:, LOAD * k:LOAD * (k + 1), :, :], A["we"][:, LOAD * k:LOAD * (k + 1)]).then_inc(ring_in[k], 16)
            q.wait_ge(dve_h4, G + 1)
            q.wait_ge(zero_out, 64)
            q.wait_ge(rows5_out, 32 * G)

            def group_load(g, u):
                q.dma_start(xg5[:, u, :, :], xs5_dram[bass.ds(g * GP * P, GP * P), :].rearrange("(m p) d -> p m d", p=P)).then_inc(tile5_in[u], 16)

            def lap_of_ring(lap, last_lap):
                for k in range(RING // LOAD):
                    g = lap * (RING // LOAD) + k
                    if not (last_lap and k >= RING // LOAD - 2):
                        q.wait_ge(pe_xg5, GP * (g + 1))
                        q.wait_ge(dve_dest5, g + 1)
                        group_load(g + 2, k % 2)
                    if not last_lap:
                        q.wait_ge(pe_y5, GP * (g + 1))
                        q.dma_start(ring[:, LOAD * k:LOAD * (k + 1), :, :],
                                    A["we"][:, bass.ds((lap + 1) * RING + LOAD * k, LOAD)]).then_inc(ring_in[k], 16)
            group_load(0, 0)
            group_load(1, 1)
            with q.Fori(0, NE2 // RING - 1) as lap:
                lap_of_ring(lap, False)
            lap_of_ring(NE2 // RING - 1, True)
            q.wait_ge(pe_y5, NP2)
            q.wait_ge(y5_out[0], 8 * NP2)
            q.wait_ge(y5_out[1], 8 * NP2)
            for b in range(NB):
                for k in range(2):
                    q.dma_start(yg5[:, k, NT * b:NT * (b + 1), :],
                                ys5_dram.rearrange("(n p) d -> p n d", p=P)[:, G * k + NT * b:G * k + NT * (b + 1), :]).then_inc(yg_in[b], 16)
            for b in range(NB):
                q.wait_ge(dve_h5, 2 * NT * (b + 1))
                q.dma_start(out[b, 0:S].rearrange("(i p) d -> p i d", p=P), Hs[:, b * NT:b * NT + QT, :]).then_inc(out_done, 16)
                q.dma_start(out[b, S:L], Hs[0:TXT, b * NT + QT, :]).then_inc(out_done, 16)
            q.wait_ge(out_done, 32 * NB)

        @block.tensor
        def _(pe):
            def project_qk(b, first):
                pe.wait_ge(x_in, 16 * (b + 1))
                if not first:
                    pe.wait_ge(dve_h1, b)
                for t in range(4):
                    for c in range(KC):
                        m = nc.tensor.matmul(ps[:, t, :], wqkv[:, c, P * t:P * (t + 1)], xT[:, c, :],
                                             start=(c == 0), stop=(c == KC - 1))
                    m.then_inc(pe_qk, 1)

            def project_v(b):
                pe.wait_ge(dve_qk32, 4 * (b + 1))
                for i in range(QT):
                    for c in range(KC):
                        m = nc.tensor.matmul(ps[:, VBANKS[i // 2], D * (i % 2):D * (i % 2 + 1)],
                                             xT[:, c, P * i:P * (i + 1)], wqkv[:, c, 2 * D:3 * D],
                                             start=(c == 0), stop=(c == KC - 1))
                m.then_inc(pe_v, 1)

            def attention(b):
                pe.wait_ge(stacks_in, 192 * (b + 1))
                pe.wait_ge(dve_v, b + 1)
                pe.wait_ge(dve_h2, b + 1)

                def scores(h, group, first):
                    if not first:
                        pe.wait_ge(dve_max, H * b + h - 1)
                    for i in range(QT):
                        m = nc.tensor.matmul(ps[:, 4 * group + i, :], Qst[0:PART, h, P * i:P * (i + 1)],
                                             Kst[0:PART, h, :], start=True, stop=True)
                    m.then_inc(pe_s, 1)
                def turned(half, bank):
                    pe.wait_ge(dve_max, H * b + HH * (half + 1))
                    nc.tensor.transpose(ps[:, bank, 0:P], mx[:, half, :, :].rearrange("p h i -> p (h i)"),
                                        ident[:, :]).then_inc(pe_mT, 1)
                scores(0, 0, True)
                scores(1, 1, True)
                with pe.Fori(1, HH // 2) as i:
                    scores(2 * i, 0, False)
                    scores(2 * i + 1, 1, False)
                scores(HH, 0, False)
                turned(0, 4)
                pe.wait_ge(dve_mneg, 2 * b + 1)
                scores(HH + 1, 1, False)
                with pe.Fori(HH // 2 + 1, H // 2) as i:
                    scores(2 * i, 0, False)
                    scores(2 * i + 1, 1, False)
                turned(1, 7)
                pe.wait_ge(mrow_in[0], 16 * (b + 1))

                def tscores(n, h, k):
                    pe.wait_ge(act_exp, NU * b + n + 1)
                    for j in range(2):
                        m = nc.tensor.matmul(ps[:, 2 * (k % 2) + j, :], Kst[:, h, P * (2 * (k % 2) + j):P * (2 * (k % 2) + j + 1)],
                                             Qst[:, h, :], start=True, stop=True)
                    m.then_inc(pe_st, 1)

                def combine(pair, u):
                    pe.wait_ge(act_OT, (H // 2) * b + pair + 3)
                    pe.wait_ge(dve_vals, (H // 2) * b + pair + 1)
                    for i in range(QT):
                        m = nc.tensor.matmul(ps[:, 6 + u, 2 * VW * i:2 * VW * (i + 1)], OT[:, u, P * i:P * (i + 1)],
                                             sel3[:, :], start=True, stop=True)
                    m.then_inc(pe_cmb, 1)

                def two_pairs(i, first, last):
                    for k in range(8):
                        if k == 5 and not first:
                            pe.wait_ge(mrow_in[1], 16 * (b + 1))
                        if not (last and k >= 5):
                            tscores(8 * i + k + 3, 4 * i + (k + 3) // 2, (k + 3) % 8)
                        weighted(8 * i + k, 4 * i + k // 2, k, 2 * i + k // 4)
                        if k % 4 == 1 and not (first and k == 1):
                            combine(2 * i + k // 4 - 1, 1 - k // 4)

                def weighted(n, h, k, pair):
                    pe.wait_ge(dve_lo, NU * b + n + 1 + 4)
                    if k % 4 == 0:
                        pe.wait_ge(act_OT, (H // 2) * b + pair + 1)
                    for j in range(2):
                        for part in range(2):
                            m = nc.tensor.matmul(ps[:, 4 + k // 4, :], Vst[:, 2 * (k % 2) + j, h, :], Phl[:, k % 4, part, j, :],
                                                 start=(k % 4 == 0 and j == 0 and part == 0),
                                                 stop=(k % 4 == 3 and j == 1 and part == 1))
                    m.then_inc(pe_pv, 1)
                for k in range(3):
                    tscores(k, k // 2, k)
                two_pairs(0, True, False)
                with pe.Fori(1, H // 4 - 1) as i:
                    two_pairs(i, False, False)
                two_pairs(H // 4 - 1, False, True)
                combine(H // 2 - 1, 1)
                pe.wait_ge(dve_vals, (H // 2) * (b + 1) + 2)
                for c in range(KC):
                    for i in range(QT):
                        m = nc.tensor.transpose(ps[:, c, P * i:P * (i + 1)], vals[:, i, P * c:P * (c + 1)], ident[:, :])
                m.then_inc(pe_vT, 1)
                pe.wait_ge(dve_vT, b + 1)
                for i in range(QT):
                    for c in range(KC):
                        m = nc.tensor.matmul(ps[:, 2 + i // 2, D * (i % 2):D * (i % 2 + 1)],
                                             valsT[:, c, P * i:P * (i + 1)], wo[:, c, :],
                                             start=(c == 0), stop=(c == KC - 1))
                    if i % 2:
                        m.then_inc(pe_o, 1)

            def scan(b, last):
                pe.wait_ge(dve_xn, b + 1)
                pe.wait_ge(dve_h1, b + 1)
                for c in range(KC):
                    for i in range(NT):
                        dst = ps[:, 4 + c, P * i:P * (i + 1)] if i < QT else ps[:, 6, P * c:P * (c + 1)]
                        m = nc.tensor.transpose(dst, xn[:, i, P * c:P * (c + 1)], ident[:, :])
                m.then_inc(pe_uT, 1)
                if not last:
                    project_v(b + 1)
                    pe.wait_ge(dve_qk32, 4 * (b + 2))
                    pe.wait_ge(dve_v32, b + 2)
                pe.wait_ge(act_uT, b + 1)
                for half in range(2):
                    for c in range(KC):
                        nc.tensor.matmul(ps[0:RANK, half, 0:HC], xpw[:, c, :], uT[:, c, HC * half:HC * (half + 1)],
                                         start=(c == 0), stop=(c == KC - 1))
                for half in range(2):
                    for c in range(KC):
                        m = nc.tensor.matmul(ps[0:96, 2 + half, 0:HC], xpbc[:, c, :], uT[:, c, HC * half:HC * (half + 1)],
                                             start=(c == 0), stop=(c == KC - 1))
                m.then_inc(pe_xp, 1)
                pe.wait_ge(act_dlow, b + 1)
                for c in range(KC):
                    for half in range(2):
                        m = nc.tensor.matmul(ps[:, 4 + 2 * c + half, 0:HC], dtw[:, P * c:P * (c + 1)],
                                             dlow[:, HC * half:HC * (half + 1)], start=True, stop=True)
                m.then_inc(pe_dt, 1)

                def spread(n, first):
                    if not first:
                        pe.wait_ge(dve_dBu, NS * b + n)
                        pe.wait_ge(act_C, NS * b + n)
                    for which in range(2):
                        for half in range(2):
                            m = nc.tensor.matmul(ps[:, 2 * which + half, 0:HC], sel[:, NS * which + n, :],
                                                 bcs[:, HC * half:HC * (half + 1)], start=True, stop=True)
                    m.then_inc(pe_bc, 1)

                def add_state(n, u, start, stop):
                    for c in range(KC):
                        pe.wait_ge(pool_hC, 2 * (NS * b + n) + 1 + c)
                        for half in range(2):
                            m = nc.tensor.matmul(ps[:, 4 + 2 * c + half, 0:HC], ident[:, :],
                                                 hC[:, u, c, HC * half:HC * (half + 1)], start=start, stop=stop,
                                                 skip_group_check=True)
                    m.then_inc(pe_y, 1)
                pe.wait_ge(dve_bcs, b + 1)
                spread(0, True)
                pe.wait_ge(dve_xb, b + 1)
                spread(1, False)
                add_state(0, 0, True, False)
                spread(2, False)
                add_state(1, 1, False, False)
                with pe.Fori(1, NS // 2 - 1) as i:
                    spread(2 * i + 1, False)
                    add_state(2 * i, 0, False, False)
                    spread(2 * i + 2, False)
                    add_state(2 * i + 1, 1, False, False)
                spread(NS - 1, False)
                add_state(NS - 2, 0, False, False)
                add_state(NS - 1, 1, False, True)
                pe.wait_ge(dve_yT, b + 1)
                pe.wait_ge(dve_dBu, NS * (b + 1))
                pe.wait_ge(act_C, NS * (b + 1))
                for i in range(NT):
                    rows = P if i < QT else TXT
                    for c in range(KC):
                        m = nc.tensor.transpose(ps[0:rows, i // 2, D * (i % 2) + P * c:D * (i % 2) + P * (c + 1)],
                                                xb[:, c, P * i:P * i + rows], ident[:, :])
                m.then_inc(pe_yT, 1)

            def route(r, weights, n_experts, rank=None):
                def turn(g, first):
                    pe.wait_ge(act_xab, r * GG + g + 1)
                    for m in range(TG):
                        if m % 2 == 0 and not first:
                            pe.wait_ge(act_xaT, 2 * (r * GG + g) - 1 + m // 2)
                        for c in range(KC):
                            ins = nc.tensor.transpose(ps[:, m // 2, D * (m % 2) + P * c:D * (m % 2) + P * (c + 1)],
                                                      xab[:, m, P * c:P * (c + 1)], ident[:, :])
                        if m % 2:
                            ins.then_inc(pe_xaT, 1)

                def logits(g, first):
                    if not first:
                        pe.wait_ge(dve_lg, r * GG + g)
                    for m in range(TG):
                        if m % 2 == 0:
                            pe.wait_ge(act_xaT, 2 * (r * GG + g) + m // 2 + 1)
                        for c in range(KC):
                            ins = nc.tensor.matmul(ps[:, 2, n_experts * m:n_experts * (m + 1)], xaT[:, m, c, :], weights[:, c, :],
                                                   start=(c == 0), stop=(c == KC - 1))
                    ins.then_inc(pe_lg, 1)
                turn(0, r == 0)
                logits(0, r == 0)
                if rank is None:
                    with pe.Fori(1, GG) as g:
                        turn(g, False)
                        logits(g, False)
                else:
                    turn(1, False)
                    rank(0, True)
                    logits(1, False)
                    with pe.Fori(2, GG) as g:
                        turn(g, False)
                        rank(g - 1, False)
                        logits(g, False)
                    rank(GG - 1, False)

            def one_expert():
                pe.wait_ge(late_in, 16 * N_LATE)
                route(0, rw, NE1)
                pe.wait_ge(dve_hot, 1)
                nc.tensor.matmul(ps[:, 4, 0:G * NE1], tri[:, :], hot[:, :, :].rearrange("p g e -> p (g e)"), start=True, stop=True)
                nc.tensor.matmul(ps[:, 5, 0:G * NE1], onesm[:, :], hot[:, :, :].rearrange("p g e -> p (g e)"),
                                 start=True, stop=True).then_inc(pe_rank, 1)
                pe.wait_ge(dve_te, 1)
                pe.wait_ge(w_in, 16 * NE1)
                pe.wait_ge(brow_in, 16)

                def turn(j, u, tile_in, first):
                    pe.wait_ge(tile_in, 16 * (j // 2 + 1) if isinstance(j, int) else 8 * (j - u) + 16)
                    if not first:
                        pe.wait_ge(act_xg, j - 1)
                    for c in range(KC):
                        m = nc.tensor.transpose(ps[:, u, P * c:P * (c + 1)], xg[:, u, P * c:P * (c + 1)], ident[:, :])
                    m.then_inc(pe_xg, 1)

                def up(j, u, first):
                    e = pe.value_load(tei[0:1, bass.ds(j, 1)], min_val=0, max_val=NE1 - 1)
                    pe.wait_ge(act_xg, j + 1)
                    if not first:
                        pe.wait_ge(act_gelu, j - 1)
                    for c in range(KC):
                        nc.tensor.matmul(ps[:, 2 + u, :], xgT[:, u, c, :], W1[:, e, c, :], start=(c == 0), stop=False)
                    nc.tensor.matmul(ps[:, 2 + u, :], ones3[:, :], brow[:, e, 0:FF], start=False, stop=True).then_inc(pe_up, 1)

                def hidden(j, u, first):
                    pe.wait_ge(act_gelu, j + 1)
                    if not first:
                        pe.wait_ge(dve_hidT, j - 1)
                    for f in range(FC):
                        m = nc.tensor.transpose(ps[:, 4 + u, P * f:P * (f + 1)], hid[:, u, P * f:P * (f + 1)], ident[:, :])
                    m.then_inc(pe_hidT, 1)

                def down(j, u, first):
                    e = pe.value_load(tei[0:1, bass.ds(j, 1)], min_val=0, max_val=NE1 - 1)
                    pe.wait_ge(dve_hidT, j + 1)
                    if not first:
                        pe.wait_ge(dve_yo, j - 1)
                    for f in range(FC):
                        nc.tensor.matmul(ps[:, 6 + u, 0:D], hidT[:, u, f, :], W2[:, e, f, :], start=(f == 0), stop=False)
                    nc.tensor.matmul(ps[:, 6 + u, 0:D], ones3[:, :], brow[:, e, FF:FF + D], start=False, stop=True).then_inc(pe_down, 1)

                def step(j, u, first):
                    hidden(j, u, first)
                    up(j + 1, 1 - u, first and j == 0)
                    down(j, u, first)
                    turn(j + 2, u, (tile_in0, tile_in1)[u], False)
                turn(0, 0, tile_in0, True)
                up(0, 0, True)
                turn(1, 1, tile_in1, True)
                step(0, 0, True)
                step(1, 1, True)
                with pe.Fori(1, MT // 2 - 1) as i:
                    step(2 * i, 0, False)
                    step(2 * i + 1, 1, False)
                hidden(MT - 2, 0, False)
                up(MT - 1, 1, False)
                down(MT - 2, 0, False)
                hidden(MT - 1, 1, False)
                down(MT - 1, 1, False)

            def causal():
                def turned(b):
                    for i in range(NT):
                        pe.wait_ge(act_xn4, NT * b + i + 1)
                        for c in range(KC):
                            dst = ps[:, c, P * i:P * (i + 1)] if i < QT else ps[:, 2, P * c:P * (c + 1)]
                            m = nc.tensor.transpose(dst, xn4[:, i, P * c:P * (c + 1)], ident[:, :])
                    m.then_inc(pe_xT4, 1)

                def project(b):
                    pe.wait_ge(act_xT4, b + 1)
                    pe.wait_ge(dve_pt4, NT * b + 1)
                    for t in range(4):
                        for lo, n, dst in ((0, S, ps[:, t, :]), (S, P, ps[:, 4, P * t:P * (t + 1)])):
                            for c in range(KC):
                                m = nc.tensor.matmul(dst, w4[:, c, P * t:P * (t + 1)], xT4[:, c, lo:lo + n],
                                                     start=(c == 0), stop=(c == KC - 1))
                        m.then_inc(pe_qk4, 1)
                    pe.wait_ge(dve_h4, NT * b + 1)
                    for i in range(NT):
                        for c in range(KC):
                            m = nc.tensor.matmul(ps[:, 5 + i // 2, D * (i % 2):D * (i % 2 + 1)], xT4[:, c, P * i:P * (i + 1)],
                                                 w4[:, c, 2 * D:3 * D], start=(c == 0), stop=(c == KC - 1))
                    m.then_inc(pe_v4, 1)

                def attend(b, last):
                    def scores(i):
                        if i >= 2:
                            pe.wait_ge(act_p4, NT * b + i - 1)
                        for lo, hi in ((0, min(P * (i + 1), S)), (S, P * (i + 1))):
                            for c in range(KC):
                                if hi > lo:
                                    m = nc.tensor.matmul(ps[:, 2 * (i % 2) + lo // S, 0:hi - lo], QK4[:, c, P * i:P * (i + 1)],
                                                         QK4[:, 2 + c, lo:hi], start=(c == 0), stop=(c == KC - 1))
                        m.then_inc(pe_s4, 1)
                    pe.wait_ge(dve_qk4, b + 1)
                    scores(0)
                    scores(1)
                    for i in range(NT):
                        pe.wait_ge(act_p4, NT * b + i + 1)
                        if i == 0:
                            pe.wait_ge(dve_qk4, b + 1)
                        else:
                            pe.wait_ge(dve_pt4, NT * b + i + 1)
                        for j in range(i + 1):
                            m = nc.tensor.transpose(ps[:, 4 + j // QT, P * (j % QT):P * (j % QT + 1)],
                                                    P4[:, i % 2, P * j:P * (j + 1)], ident[:, :])
                        m.then_inc(pe_pt4, 1)
                        if i + 2 < NT:
                            scores(i + 2)
                        elif i == NT - 1 and not last:
                            turned(b + 1)
                        if i == 0:
                            pe.wait_ge(dve_v4, b + 1)
                        pe.wait_ge(dve_pt4, NT * b + i + 2)
                        if i >= 2:
                            pe.wait_ge(dve_h4, NT * b + i)
                        for j in range(i + 1):
                            m = nc.tensor.matmul(ps[:, 6 + i % 2, 0:D], PT4[:, i % 2, j, :], V4[:, j, :],
                                                 start=(j == 0), stop=(j == i))
                        m.then_inc(pe_pv4, 1)
                pe.wait_ge(last_in, 16 * N_LAST)
                turned(0)
                project(0)
                with pe.Fori(0, NB - 1) as b:
                    attend(b, False)
                    project(b + 1)
                attend(NB - 1, True)

            def rank(g, first):
                pe.wait_ge(dve_hot5, g + 1)
                if not first:
                    pe.wait_ge(dve_rank5, g)
                for m in range(TG):
                    dst = ps[:, 3 + m // 2, D * (m % 2):D * (m % 2 + 1)]
                    nc.tensor.matmul(dst, tri5[:, 0, :], hotb[:, m, :, :].rearrange("p k e -> p (k e)"), start=True, stop=False)
                    for before in range(m):
                        nc.tensor.matmul(dst, tri5[:, 1, :], hotb[:, before, :, :].rearrange("p k e -> p (k e)"), start=False, stop=False)
                    ins = nc.tensor.matmul(dst, tri5[:, 1, :], hsum[:, :, :].rearrange("p k e -> p (k e)"), start=False, stop=True)
                ins.then_inc(pe_rank5, 1)

            def two_experts():
                route(1, wg, NE2, rank)
                pe.wait_ge(dve_rank5, GG)
                nc.tensor.matmul(ps[:, 5, 0:NE2], tri5[:, 1, :], hsum[:, 0, :], start=True, stop=True).then_inc(pe_count5, 1)

                def turn(j, u, place, first):
                    if not first:
                        pe.wait_ge(act_xg5, j - 1)
                    for c in range(KC):
                        m = nc.tensor.transpose(ps[:, u, P * c:P * (c + 1)], xg5[:, place // GP, place % GP, P * c:P * (c + 1)], ident[:, :])
                    m.then_inc(pe_xg5, 1)

                def multiply(j, u, place, first):
                    pe.wait_ge(act_xg5, j + 1)
                    if not first:
                        pe.wait_ge(dve_y5, j - 1)
                    for k in range(2):
                        for c in range(KC):
                            m = nc.tensor.matmul(ps[:, 2 + u, D * k:D * (k + 1)], xgT5[:, u, c, :], ring[:, place + k, c, :],
                                                 start=(c == 0), stop=(c == KC - 1))
                    m.then_inc(pe_y5, 1)

                def lap_of_ring(lap, first_lap, last_lap):
                    for k in range(RING // LOAD):
                        pe.wait_ge(ring_in[k], 16 * lap + 16)
                        for m in range(GP):
                            j = lap * (RING // 2) + k * GP + m
                            if not (last_lap and k == RING // LOAD - 1 and m == GP - 1):
                                if m == GP - 1:
                                    pe.wait_ge(tile5_in[(k + 1) % 2], 32 * lap + 16 * ((k + 1) // 2) + 16)
                                turn(j + 1, (m + 1) % 2, (k * GP + m + 1) % (2 * GP), first_lap and k == 0 and m == 0)
                            multiply(j, m % 2, LOAD * k + 2 * m, first_lap and k == 0 and m < 2)
                pe.wait_ge(tile5_in[0], 16)
                turn(0, 0, 0, True)
                lap_of_ring(0, True, False)
                with pe.Fori(1, NE2 // RING - 1) as lap:
                    lap_of_ring(lap, False, False)
                lap_of_ring(NE2 // RING - 1, False, True)

            pe.wait_ge(consts_in, 16 * N_CONSTS)
            for _ in range(4):
                pe.nop().then_inc(pe_pv, 1)
            for _ in range(2):
                pe.nop().then_inc(pe_cmb, 1)
            project_qk(0, True)
            project_v(0)
            with pe.Fori(0, NB - 1) as b:
                attention(b)
                project_qk(b + 1, False)
                scan(b, False)
            attention(NB - 1)
            scan(NB - 1, True)
            one_expert()
            causal()
            two_experts()

        @block.scalar
        def _(act):
            def split_first(b):
                for t in range(4):
                    act.wait_ge(dve_qk32, 4 * b + t + 1)
                    if t == 0 and not isinstance(b, int):
                        act.wait_ge(parts_out[0], 16 * b)
                        act.wait_ge(parts_out[1], 16 * b)
                    nc.scalar.activation(parts[:, 0, t, :], qk32[:, t, :], ACT.Copy).then_inc(act_p1, 1)

            def split_rest(b):
                act.wait_ge(dve_v32, b + 1)
                for hd in range(2):
                    v = nc.scalar.activation(vpart(hd, 0), vhead(hd), ACT.Copy)
                v.then_inc(act_v1, 1)
                for t in range(4):
                    act.wait_ge(dve_res, 4 * b + t + 1)
                    nc.scalar.activation(parts[:, 1, t, :], qk32[:, t, :], ACT.Copy).then_inc(act_p2, 1)
                act.wait_ge(dve_vr, b + 1)
                for hd in range(2):
                    v = nc.scalar.activation(vpart(hd, 1), vhead(hd), ACT.Copy)
                v.then_inc(act_v2, 1)

            def attention(b):
                def exps(n, k):
                    act.wait_ge(pe_st, NU * b + n + 1)
                    act.wait_ge(dve_lo, NU * b + n + 1)
                    e = nc.scalar.activation(P32[:, k % 4, :, :], ps[:, 2 * (k % 2):2 * (k % 2) + 2, :],
                                             ACT.Exp, scale=float(HD) ** -0.5)
                    if k % 2 == 0:
                        act.wait_ge(pe_pv, NU * b + n + 1)
                        e = nc.scalar.activation(Phl[:, k % 4, 0, :, :], ps[:, 2 * (k % 2):2 * (k % 2) + 2, :],
                                                 ACT.Exp, scale=float(HD) ** -0.5)
                    e.then_inc(act_exp, 1)

                def evacuate(pair, u):
                    act.wait_ge(pe_pv, NU * b + 4 * pair + 4 + 4)
                    act.wait_ge(pe_cmb, (H // 2) * b + pair + 1)
                    nc.scalar.activation(OT[:, u, :], ps[:, 4 + u, :], ACT.Copy).then_inc(act_OT, 1)

                def two_pairs(i, first):
                    for k in range(8):
                        exps(8 * i + k, k)
                        if k % 4 == 3 and not (first and k == 3):
                            evacuate(2 * i + k // 4 - 1, 1 - k // 4)
                two_pairs(0, True)
                with act.Fori(1, H // 4) as i:
                    two_pairs(i, False)
                evacuate(H // 2 - 1, 1)

            def standard_deviations(b):
                act.wait_ge(dve_stats, b + 1)
                nc.scalar.activation(rstd[:, :], mv[:, :, 1], ACT.Sqrt).then_inc(act_std, 1)

            def transposed(b):
                act.wait_ge(pe_uT, b + 1)
                for c in range(KC):
                    nc.scalar.activation(uT[:, c, 0:S], ps[:, 4 + c, :], ACT.Copy)
                nc.scalar.activation(uT[:, :, S:LP], ps[:, 6, 0:2 * P].rearrange("p (c t) -> p c t", c=KC)[:, :, 0:LP - S],
                                     ACT.Copy).then_inc(act_uT, 1)

            def scan(b):
                act.wait_ge(pe_xp, b + 1)
                nc.scalar.activation(halves(dlow[:, :]), two_banks(0, RANK), ACT.Copy).then_inc(act_dlow, 1)
                act.wait_ge(dve_sp, b + 1)
                nc.scalar.activation(sp[:, :, :], sp[:, :, :], ACT.Exp, scale=-1.0).then_inc(act_sp, 1)
                act.wait_ge(act_sp, 2 * b + 1)
                nc.scalar.activation(sp[:, :, :], sp[:, :, :], ACT.Ln, bias=1.0).then_inc(act_sp, 1)
                act.wait_ge(dve_delta, b + 1)

                def decay(n, u, first):
                    for c in range(KC):
                        if not first:
                            act.wait_ge(dve_scan, 2 * (NS * b + n - 2) + c + 1)
                        nc.scalar.activation(dA[:, u, c, :], delta[:, c, :], ACT.Exp,
                                             scale=acol[:, bass.ds(n + NS * c, 1)]).then_inc(act_dA, 1)
                    act.wait_ge(pe_bc, NS * b + n + 1)
                    if not first:
                        act.wait_ge(pool_hC, 2 * (NS * b + n - 1))
                    nc.scalar.activation(halves(Cb[:, u, :]), two_banks(2), ACT.Copy).then_inc(act_C, 1)
                decay(0, 0, True)
                decay(1, 1, True)
                with act.Fori(1, NS // 2) as i:
                    decay(2 * i, 0, False)
                    decay(2 * i + 1, 1, False)

            def normalise_rows(r, norm, xa):
                def rows(g, first):
                    if not first:
                        act.wait_ge(pe_xaT, 2 * (r * GG + g))
                        if r == 0:
                            act.wait_ge(dve_xa, g)
                    for m in range(TG):
                        ins = nc.scalar.activation(xab[:, m, :], Hs[:, TG * g + m, :], ACT.Identity, bias=lbias[:, bass.ds(TG * g + m, 1)],
                                                   scale=lrstd[:, bass.ds(TG * g + m, 1)])
                    ins.then_inc(act_xab, 1)

                def keep(g):
                    for m in range(TG):
                        ins = nc.scalar.activation(xa[:, TG * g + m, 0:D], Hs[:, TG * g + m, :], ACT.Identity,
                                                   bias=lbias[:, bass.ds(TG * g + m, 1)], scale=lrstd[:, bass.ds(TG * g + m, 1)])
                    ins.then_inc(act_xa, 1)

                def turned(g, first):
                    if not first:
                        act.wait_ge(pe_lg, r * GG + g)
                    for h in range(TG // 2):
                        act.wait_ge(pe_xaT, 2 * (r * GG + g) + h + 1)
                        nc.scalar.activation(xaT[:, 2 * h:2 * h + 2, :, :].rearrange("p m c t -> p (m c t)"), ps[:, h, :], ACT.Copy).then_inc(act_xaT, 1)
                act.wait_ge(ln_stats, norm)
                nc.scalar.activation(lrstd[:, :], lrstd[:, :], ACT.Sqrt).then_inc(ln_std, 1)
                act.wait_ge(ln_done, norm)
                rows(0, r == 0)
                turned(0, r == 0)
                with act.Fori(1, GG) as g:
                    rows(g, False)
                    turned(g, False)
                    if r:
                        keep(g - 1)
                if r:
                    keep(GG - 1)

            def one_expert():
                act.wait_ge(late_in, 16 * N_LATE)
                normalise_rows(0, 1, xa)
                act.wait_ge(dve_ex, 1)
                nc.scalar.activation(lg[:, :, :], lg[:, :, :], ACT.Exp).then_inc(act_ex, 1)

                def turned(j, u, first):
                    act.wait_ge(pe_xg, j + 1)
                    if not first:
                        act.wait_ge(pe_up, j - 1)
                    nc.scalar.activation(xgT[:, u, :, :], ps[:, u, 0:D].rearrange("p (c t) -> p c t", c=KC), ACT.Copy).then_inc(act_xg, 1)

                def gelu(j, u, first):
                    act.wait_ge(pe_up, j + 1)
                    if not first:
                        act.wait_ge(pe_hidT, j - 1)
                    nc.scalar.activation(hid[:, u, :], ps[:, 2 + u, :], ACT.Gelu).then_inc(act_gelu, 1)
                turned(0, 0, True)
                gelu(0, 0, True)
                turned(1, 1, True)
                gelu(1, 1, True)
                with act.Fori(1, MT // 2) as i:
                    turned(2 * i, 0, False)
                    gelu(2 * i, 0, False)
                    turned(2 * i + 1, 1, False)
                    gelu(2 * i + 1, 1, False)

            def causal():
                act.wait_ge(ln_stats, 2)
                nc.scalar.activation(lrstd[:, :], lrstd[:, :], ACT.Sqrt).then_inc(ln_std, 1)
                act.wait_ge(ln_done, 2)

                def rows(b, i):
                    nc.scalar.activation(xn4[:, i, :], Hs[:, NT * b + i, :], ACT.Identity, bias=lbias[:, bass.ds(NT * b + i, 1)],
                                         scale=lrstd[:, bass.ds(NT * b + i, 1)]).then_inc(act_xn4, 1)

                def turned(b):
                    act.wait_ge(pe_xT4, b + 1)
                    for c in range(KC):
                        nc.scalar.activation(xT4[:, c, 0:S], ps[:, c, :], ACT.Copy)
                    nc.scalar.activation(xT4[:, :, S:LT], ps[:, 2, 0:D].rearrange("p (c t) -> p c t", c=KC), ACT.Copy).then_inc(act_xT4, 1)

                def attend(b, last):
                    for i in range(NT):
                        act.wait_ge(dve_nm4, NT * b + i + 1)
                        if i >= 2:
                            act.wait_ge(pe_pt4, NT * b + i - 1)
                        n = P * (i + 1)
                        nc.scalar.activation(P4[:, i % 2, 0:n], ps[:, 2 * (i % 2):2 * (i % 2) + 2, :].rearrange("p b s -> p (b s)")[:, 0:n],
                                             ACT.Exp, bias=nm4[:, i:i + 1], scale=float(D) ** -0.5,
                                             accum_out=rs4[:, i:i + 1]).then_inc(act_p4, 1)
                        if not last:
                            rows(b + 1, i)
                    if not last:
                        turned(b + 1)
                for i in range(NT):
                    rows(0, i)
                turned(0)
                with act.Fori(0, NB - 1) as b:
                    attend(b, False)
                attend(NB - 1, True)

            def two_experts():
                normalise_rows(1, 3, xa5)
                act.wait_ge(dve_ex5, 1)
                nc.scalar.activation(lg5[:, :, :], lg5[:, :, :], ACT.Exp)
                nc.scalar.activation(w5[:, :, :], w5[:, :, :], ACT.Exp).then_inc(act_ex, 1)

                def turned(j, u, first):
                    act.wait_ge(pe_xg5, j + 1)
                    if not first:
                        act.wait_ge(pe_y5, j - 1)
                    nc.scalar.activation(xgT5[:, u, :, :], ps[:, u, 0:D].rearrange("p (c t) -> p c t", c=KC), ACT.Copy).then_inc(act_xg5, 1)
                turned(0, 0, True)
                turned(1, 1, True)
                with act.Fori(1, NP2 // 2) as i:
                    turned(2 * i, 0, False)
                    turned(2 * i + 1, 1, False)

            act.wait_ge(consts_in, 16 * N_CONSTS)
            nc.scalar.activation(acol[:, :], alog[:, :], ACT.Exp).then_inc(act_acol, 1)
            act.wait_ge(dve_init, 1)
            for _ in range(2):
                act.nop().then_inc(act_exp, 1)
                act.nop().then_inc(act_OT, 1)
            split_first(0)
            split_rest(0)
            with act.Fori(0, NB - 1) as b:
                attention(b)
                standard_deviations(b)
                split_first(b + 1)
                transposed(b)
                split_rest(b + 1)
                scan(b)
            attention(NB - 1)
            standard_deviations(NB - 1)
            transposed(NB - 1)
            scan(NB - 1)
            one_expert()
            causal()
            two_experts()

        @block.gpsimd
        def _(pool):
            nc.gpsimd.memset(Hs[:, :, :].rearrange("p (b i) d -> p b i d", i=NT)[:, :, QT, :], 0.0).then_inc(pool_init, 1)
            nc.gpsimd.memset(zeros[:, :], 0.0).then_inc(pool_init, 1)
            nc.gpsimd.memset(mx[:, :, :, :], 0.0).then_inc(pool_init, 1)
            nc.gpsimd.memset(Vst[:, :, :, :].rearrange("p j h c -> p (j h c)").bitcast(F32), 0.0).then_inc(pool_init, 1)
            pool.wait_ge(pool_init, 4)
            for hd in range(2):
                vs = Vst[:, :, :, :].rearrange("p j (g s) c -> p (j g) s c", s=2)
                nc.gpsimd.memset(vs[:, :, hd, 64 * hd + HD:64 * hd + HD + 1], 1.0).then_inc(pool_init, 1)

            def output_gate(b, n, u, first):
                for c in range(KC):
                    if c == 0:
                        pool.wait_ge(act_C, NS * b + n + 1)
                        if not first:
                            pool.wait_ge(pe_y, NS * b + n - 1)
                    pool.wait_ge(dve_scan, 2 * (NS * b + n) + c + 1)
                    nc.gpsimd.tensor_tensor(hC[:, u, c, :], hst[:, u, c, :], Cb[:, u, :], ALU.mult).then_inc(pool_hC, 1)
            with pool.Fori(0, NB) as b:
                output_gate(b, 0, 0, True)
                output_gate(b, 1, 1, True)
                with pool.Fori(1, NS // 2) as i:
                    output_gate(b, 2 * i, 0, False)
                    output_gate(b, 2 * i + 1, 1, False)

            pool.wait_ge(late_in, 16 * N_LATE)
            pool.wait_ge(ln_stats, 1)
            nc.gpsimd.tensor_copy(xa[:, :, D:DW].rearrange("p g o -> p (g o)"), home[:, :]).then_inc(pool_home, 1)
            pool.wait_ge(dve_slots, 1)
            pool.wait_ge(zero_out, 64)
            pool.wait_ge(dve_xa, GG)
            pool.wait_ge(pool_home, 1)
            for t in range(G):
                nc.gpsimd.indirect_dma_start(xs_dram, bass.IndirectOffsetOnAxis(slots[:, t:t + 1], 0), xa[:, t, :], None,
                                             bounds_check=MT * P - 1, oob_is_err=False).then_inc(rows_out, 16)

            def result(j, u):
                pool.wait_ge(dve_yo, j + 1)
                pool.wait_ge(pool_home, j + 1)
                nc.gpsimd.tensor_tensor(pooltick[:, :], zeros[:, 0:1], zeros[:, 0:1], ALU.add).then_inc(pool_home, 1)
                nc.gpsimd.indirect_dma_start(ys_dram, bass.IndirectOffsetOnAxis(dest[:, u:u + 1], 0), yo[:, u, :], None,
                                             bounds_check=G * P - 1, oob_is_err=False).then_inc(yo_out[u], 16)
            with pool.Fori(0, MT // 2) as i:
                result(2 * i, 0)
                result(2 * i + 1, 1)
            pool.wait_ge(zero_out, 64)
            pool.wait_ge(last_in, 16 * N_LAST)
            pool.wait_ge(ln_stats, 3)
            nc.gpsimd.tensor_copy(xa5[:, :, D:DW].rearrange("p g o -> p (g o)"), home5[:, 0, :]).then_inc(pool_home, 1)
            pool.wait_ge(act_xa, GG)
            for k in range(2):
                for t in range(G):
                    if k == 0 and t % TG == 0:
                        pool.wait_ge(dve_to5, t // TG + 1)
                    if k == 1 and t == 0:
                        pool.wait_ge(rows5_out, 16 * G)
                        nc.gpsimd.tensor_copy(xa5[:, :, D:DW].rearrange("p g o -> p (g o)"), home5[:, 1, :]).then_inc(pool_home, 1)
                        pool.wait_ge(dve_to5, GG + 1)
                    if t == 0:
                        pool.wait_ge(pool_home, 1 + MT + k + 1)
                    nc.gpsimd.indirect_dma_start(xs5_dram, bass.IndirectOffsetOnAxis(to5[:, k, t:t + 1], 0), xa5[:, t, :], None,
                                                 bounds_check=NE2 * CAP - 1, oob_is_err=False).then_inc(rows5_out, 16)

            def results(g, u):
                pool.wait_ge(dve_dest5, g + 1)
                pool.wait_ge(dve_y5, GP * (g + 1))
                pool.wait_ge(pool_home, 1 + MT + g + 2)
                nc.gpsimd.tensor_tensor(pooltick[:, :], zeros[:, 0:1], zeros[:, 0:1], ALU.add).then_inc(pool_home, 1)
                for m in range(GP):
                    nc.gpsimd.indirect_dma_start(ys5_dram, bass.IndirectOffsetOnAxis(dest5[:, u, m:m + 1], 0), yo5[:, u, m, :], None,
                                                 bounds_check=2 * G * P - 1, oob_is_err=False).then_inc(y5_out[u], 16)
            with pool.Fori(0, NP2 // GP // 2) as i:
                results(2 * i, 0)
                results(2 * i + 1, 1)

        @block.vector
        def _(dve):
            def split(b):
                for t in range(4):
                    dve.wait_ge(pe_qk, 4 * b + t + 1)
                    nc.vector.tensor_scalar(qk32[:, t, :], ps[:, t, :], bqk[:, t:t + 1], None, ALU.add).then_inc(dve_qk32, 1)
                for t in range(4):
                    dve.wait_ge(act_p1, 4 * b + t + 1)
                    nc.vector.tensor_tensor(qk32[:, t, :], qk32[:, t, :], parts[:, 0, t, :], ALU.subtract).then_inc(dve_res, 1)
                dve.wait_ge(pe_v, b + 1)
                for i in range(QT):
                    v = nc.vector.tensor_tensor(v32[:, i, :], ps[:, VBANKS[i // 2], D * (i % 2):D * (i % 2 + 1)], bv[:, :], ALU.add)
                v.then_inc(dve_v32, 1)
                dve.wait_ge(act_v1, b + 1)
                for hd in range(2):
                    v = nc.vector.tensor_tensor(vhead(hd), vhead(hd), vpart(hd, 0), ALU.subtract)
                v.then_inc(dve_vr, 1)
                for t in range(4):
                    dve.wait_ge(act_p2, 4 * b + t + 1)
                    nc.vector.tensor_tensor(parts[:, 2, t, :], qk32[:, t, :], parts[:, 1, t, :], ALU.subtract).then_inc(dve_p3, 1)
                dve.wait_ge(act_v2, b + 1)
                for hd in range(2):
                    v = nc.vector.tensor_tensor(vpart(hd, 2), vhead(hd), vpart(hd, 1), ALU.subtract)
                v.then_inc(dve_v, 1)

            def attention(b):
                def maxima(h, group, half):
                    dve.wait_ge(pe_s, H * b + h + 1)
                    nc.vector.tensor_reduce(mx[:, half, h - HH * half, :], ps[:, 4 * group:4 * group + 4, :], AX.X, ALU.max).then_inc(dve_max, 1)

                def minus(half, bank):
                    n = 2 * b + half
                    dve.wait_ge(pe_mT, n + 1)
                    nc.vector.tensor_scalar(mneg[:, half, :], ps[0:HH * QT, bank, 0:P], -1.0, None, ALU.mult).then_inc(dve_mneg, 1)
                    dve.wait_ge(dve_mneg, n + 1)
                    nc.vector.tensor_copy(mparts[:, half, 0, :], mneg[:, half, :]).then_inc(dve_mchain, 1)
                    dve.wait_ge(dve_mchain, 3 * n + 1)
                    nc.vector.tensor_tensor(mneg[:, half, :], mneg[:, half, :], mparts[:, half, 0, :], ALU.subtract).then_inc(dve_mchain, 1)
                    dve.wait_ge(dve_mchain, 3 * n + 2)
                    nc.vector.tensor_copy(mparts[:, half, 1, :], mneg[:, half, :]).then_inc(dve_mchain, 1)
                    dve.wait_ge(dve_mchain, 3 * n + 3)
                    nc.vector.tensor_tensor(mparts[:, half, 2, :], mneg[:, half, :], mparts[:, half, 1, :], ALU.subtract).then_inc(dve_mparts, 1)

                with dve.Fori(0, HH // 2) as i:
                    maxima(2 * i, 0, 0)
                    maxima(2 * i + 1, 1, 0)
                maxima(HH, 0, 1)
                minus(0, 4)
                maxima(HH + 1, 1, 1)
                with dve.Fori(HH // 2 + 1, H // 2) as i:
                    maxima(2 * i, 0, 1)
                    maxima(2 * i + 1, 1, 1)
                minus(1, 7)

                def low(n, k, odd):
                    dve.wait_ge(act_exp, NU * b + n + 3)
                    if k % 2:
                        dve.wait_ge(pe_pv, NU * b + n + 1)
                        nc.vector.tensor_copy(Phl[:, k % 4, 0, :, :], P32[:, k % 4, :, :]).then_inc(dve_hi, 1)
                        dve.wait_ge(dve_hi, (NU // 2) * b + odd + 1)
                    nc.vector.tensor_tensor(Phl[:, k % 4, 1, :, :], P32[:, k % 4, :, :], Phl[:, k % 4, 0, :, :],
                                            ALU.subtract).then_inc(dve_lo, 1)

                def normalise(pair, u):
                    dve.wait_ge(pe_cmb, (H // 2) * b + pair + 1 + 2)
                    acc = ps[:, 6 + u, 0:2 * VW * QT].rearrange("p (i s d) -> p i s d", i=QT, s=2)
                    nc.vector.reciprocal(rsum[:, u, :, :, :], acc[:, :, :, HD:VW]).then_inc(dve_rsum, 1)
                    dve.wait_ge(dve_rsum, (H // 2) * b + pair + 1)
                    nc.vector.tensor_tensor(vals[:, :, bass.ds(pair * 2 * HD, 2 * HD)].rearrange("p i (s d) -> p i s d", s=2),
                                            acc[:, :, :, 0:HD], rsum[:, u, :, :, :].to_broadcast([P, QT, 2, HD]),
                                            ALU.mult).then_inc(dve_vals, 1)

                def two_pairs(i, first):
                    for k in range(8):
                        low(8 * i + k, k, 4 * i + k // 2)
                        if k % 4 == 3 and not (first and k == 3):
                            normalise(2 * i + k // 4 - 1, 1 - k // 4)
                two_pairs(0, True)
                with dve.Fori(1, H // 4) as i:
                    two_pairs(i, False)
                normalise(H // 2 - 1, 1)
                dve.wait_ge(pe_vT, b + 1)
                nc.vector.tensor_copy(valsT[:, :, :], ps[:, 0:KC, :]).then_inc(dve_vT, 1)
                for i in range(QT):
                    if i % 2 == 0:
                        dve.wait_ge(pe_o, QT // 2 * b + i // 2 + 1)
                    v = nc.vector.tensor_tensor(Hs[:, b * NT + i, :], ps[:, 2 + i // 2, D * (i % 2):D * (i % 2 + 1)],
                                                bo[:, :], ALU.add)
                v.then_inc(dve_h1, 1)

            def normalised(b):
                dve.wait_ge(dve_h1, b + 1)
                nc.vector.memset(tick[:, :], 0.0)
                for i in range(NT):
                    v = nc.vector.bn_stats(st6[:, i, :], Hs[:, b * NT + i, :])
                v.then_inc(dve_bcchain, 1)
                dve.wait_ge(dve_bcchain, 7 * b + 1)
                nc.vector.memset(tick[:, :], 0.0)
                for i in range(NT):
                    v = nc.vector.bn_aggr(mv[:, i, :], st6[:, i, :])
                v.then_inc(dve_bcchain, 1)
                dve.wait_ge(dve_bcchain, 7 * b + 2)
                nc.vector.tensor_scalar(mv[:, :, 1], mv[:, :, 1], EPS, None, ALU.add).then_inc(dve_stats, 1)
                dve.wait_ge(act_std, b + 1)
                nc.vector.reciprocal(rstd[:, :], rstd[:, :]).then_inc(dve_rstd, 1)
                dve.wait_ge(dve_rstd, b + 1)
                for i in range(NT):
                    v = nc.vector.tensor_scalar(xn[:, i, :], Hs[:, b * NT + i, :], mv[:, i, 0:1], rstd[:, i:i + 1],
                                                ALU.subtract, ALU.mult)
                v.then_inc(dve_xn, 1)

            def scan(b):
                dve.wait_ge(pe_dt, b + 1)
                for c in range(KC):
                    v = nc.vector.tensor_scalar(halves(xb[:, c, :]), two_banks(4 + 2 * c), dtb[:, c:c + 1], None, ALU.add)
                v.then_inc(dve_xb, 1)
                dve.wait_ge(dve_xb, b + 1)
                nc.vector.scalar_tensor_tensor(out=sp[:, :, :], in0=xb[:, :, :], scalar=-1.0, in1=xb[:, :, :],
                                               op0=ALU.mult, op1=ALU.max).then_inc(dve_sp, 1)
                dve.wait_ge(pe_xp, b + 1)
                base = 7 * b + 2
                nc.vector.tensor_copy(halves(bc32[:, :]), two_banks(2, 96)).then_inc(dve_bcchain, 1)
                dve.wait_ge(dve_bcchain, base + 1)
                nc.vector.tensor_copy(bcp[:, 0, :], bc32[:, :]).then_inc(dve_bcchain, 1)
                dve.wait_ge(dve_bcchain, base + 2)
                nc.vector.tensor_tensor(bc32[:, :], bc32[:, :], bcp[:, 0, :], ALU.subtract).then_inc(dve_bcchain, 1)
                dve.wait_ge(dve_bcchain, base + 3)
                nc.vector.tensor_copy(bcp[:, 1, :], bc32[:, :]).then_inc(dve_bcchain, 1)
                dve.wait_ge(dve_bcchain, base + 4)
                nc.vector.tensor_tensor(bc32[:, :], bc32[:, :], bcp[:, 1, :], ALU.subtract).then_inc(dve_bcchain, 1)
                dve.wait_ge(dve_bcchain, base + 5)
                nc.vector.tensor_copy(bcs[0:32, :], bcp[0:32, 0, :])
                nc.vector.tensor_copy(bcs[32:64, :], bcp[32:64, 1, :])
                nc.vector.tensor_copy(bcs[64:96, :], bc32[64:96, :]).then_inc(dve_bcs, 1)
                dve.wait_ge(act_sp, 2 * b + 2)
                nc.vector.scalar_tensor_tensor(out=delta[:, :, :], in0=xb[:, :, :], scalar=0.0, in1=sp[:, :, :],
                                               op0=ALU.max, op1=ALU.add).then_inc(dve_delta, 1)
                dve.wait_ge(dve_delta, b + 1)
                dve.wait_ge(act_uT, b + 1)
                nc.vector.tensor_tensor(dtu[:, :, :], delta[:, :, :], uT[:, :, :], ALU.mult).then_inc(dve_dtu, 1)
                dve.wait_ge(dve_dtu, b + 1)

                def recurrence(n, u, first):
                    dve.wait_ge(pe_bc, NS * b + n + 1)
                    for c in range(KC):
                        v = nc.vector.tensor_tensor(halves(dBu[:, u, c, :]), halves(dtu[:, c, :]), two_banks(0), ALU.mult)
                    v.then_inc(dve_dBu, 1)
                    dve.wait_ge(dve_dBu, NS * b + n + 1)
                    if not first:
                        dve.wait_ge(pool_hC, 2 * (NS * b + n - 1))
                    for c in range(KC):
                        dve.wait_ge(act_dA, 2 * (NS * b + n) + c + 1)
                        nc.vector.tensor_tensor_scan(hst[:, u, c, :], dA[:, u, c, :], dBu[:, u, c, :], 0.0,
                                                     ALU.mult, ALU.add).then_inc(dve_scan, 1)
                recurrence(0, 0, True)
                recurrence(1, 1, True)
                with dve.Fori(1, NS // 2) as i:
                    recurrence(2 * i, 0, False)
                    recurrence(2 * i + 1, 1, False)
                dve.wait_ge(pe_y, NS * (b + 1))
                for c in range(KC):
                    v = nc.vector.scalar_tensor_tensor(out=halves(xb[:, c, :]), in0=halves(uT[:, c, :]), scalar=dsk[:, c:c + 1],
                                                       in1=two_banks(4 + 2 * c), op0=ALU.mult, op1=ALU.add)
                v.then_inc(dve_yT, 1)
                dve.wait_ge(pe_yT, b + 1)
                for i in range(NT):
                    rows = P if i < QT else TXT
                    v = nc.vector.tensor_tensor(Hs[0:rows, b * NT + i, :], Hs[0:rows, b * NT + i, :],
                                                ps[0:rows, i // 2, D * (i % 2):D * (i % 2 + 1)], ALU.add)
                v.then_inc(dve_h2, 1)
                dve.wait_ge(dve_h2, b + 2)
                nc.vector.memset(tick2[:, :], 0.0)
                for i in range(NT):
                    nc.vector.bn_stats(lst[:, NT * b + i, :], Hs[:, NT * b + i, :]).then_inc(ln_chain, 1)

            def layer_norm(r):
                n = [(r + 1) * G + 6 * r]
                dve.wait_ge(ln_chain, n[0])

                def link(ins):
                    n[0] += 1
                    ins.then_inc(ln_chain, 1)
                    dve.wait_ge(ln_chain, n[0])
                m0, m1, q0, q1 = (lst[:, :, k] for k in (1, 4, 2, 5))
                link(nc.vector.tensor_tensor(lmean[:, :], m0, m1, ALU.add))
                link(nc.vector.tensor_tensor(ltmp[:, :], m0, m1, ALU.subtract))
                link(nc.vector.scalar_tensor_tensor(out=ltmp[:, :], in0=ltmp[:, :], scalar=0.25, in1=ltmp[:, :],
                                                    op0=ALU.mult, op1=ALU.mult))
                link(nc.vector.tensor_tensor(lrstd[:, :], q0, q1, ALU.add))
                link(nc.vector.scalar_tensor_tensor(out=lrstd[:, :], in0=lrstd[:, :], scalar=1.0 / D, in1=ltmp[:, :],
                                                    op0=ALU.mult, op1=ALU.add))
                nc.vector.tensor_scalar(lrstd[:, :], lrstd[:, :], EPS, None, ALU.add).then_inc(ln_stats, 1)
                dve.wait_ge(ln_std, r + 1)
                link(nc.vector.reciprocal(lrstd[:, :], lrstd[:, :]))
                nc.vector.scalar_tensor_tensor(out=lbias[:, :], in0=lmean[:, :], scalar=-0.5, in1=lrstd[:, :],
                                               op0=ALU.mult, op1=ALU.mult).then_inc(ln_done, 1)

            def choose(r, n_experts, lgb, lg, then=None):
                per = 3 if r == 0 else 4

                def group(g):
                    base = r * 3 * GG + per * g

                    def link(k):
                        dve.wait_ge(best_chain, base + k)
                    tiles = bass.ds(TG * g, TG)
                    if r == 0:
                        dve.wait_ge(act_xab, g + 1)
                        nc.vector.tensor_copy(xa[:, tiles, 0:D], xab[:, :, :]).then_inc(dve_xa, 1)
                    dve.wait_ge(pe_lg, r * GG + g + 1)
                    nc.vector.tensor_copy(lgb[:, :, :].rearrange("p m e -> p (m e)"), ps[:, 2, 0:TG * n_experts]).then_inc(dve_lg, 1)
                    dve.wait_ge(dve_lg, r * GG + g + 1)
                    nc.vector.tensor_copy(lg[:, tiles, :], lgb[:, :, :])
                    for m in range(TG):
                        ins = nc.vector.max(m8b[:, m, :], lgb[:, m, :])
                    ins.then_inc(best_chain, 1)
                    link(1)
                    nc.vector.tensor_copy(best[:, tiles, :], m8b[:, :, 0:2])
                    for m in range(TG):
                        ins = nc.vector.max_index(i8b[:, m, :], m8b[:, m, :], lgb[:, m, :])
                    ins.then_inc(best_chain, 1)
                    link(2)
                    nc.vector.tensor_copy(besti[:, tiles, :], i8b[:, :, 0:2]).then_inc(best_chain, 1)
                    if then:
                        then(g, link)
                    link(per)
                with dve.Fori(0, GG) as g:
                    group(g)

            def one_expert():
                n = [0]

                def link(ins):
                    n[0] += 1
                    ins.then_inc(c3, 1)
                    dve.wait_ge(c3, n[0])
                dve.wait_ge(dve_h2, NB + 1)
                layer_norm(0)
                dve.wait_ge(late_in, 16 * N_LATE)
                choose(0, NE1, lgb, lg)
                flat = [P, G, NE1]
                link(nc.vector.tensor_tensor(hot[:, :, :], iota1[:, :].rearrange("p (o e) -> p o e", o=1).to_broadcast(flat),
                                             besti[:, :, 0:1].to_broadcast(flat), ALU.is_equal))
                nc.vector.tensor_tensor(hot[:, :, :], hot[:, :, :], real[:, :].rearrange("p (g o) -> p g o", o=1).to_broadcast(flat),
                                        ALU.mult).then_inc(dve_hot, 1)
                nc.vector.tensor_tensor(lg[:, :, :], lg[:, :, :], best[:, :, 0:1].to_broadcast(flat), ALU.subtract).then_inc(dve_ex, 1)
                dve.wait_ge(pe_rank, 1)
                link(nc.vector.tensor_copy(cnt[:, :, :], ps[:, 5, 0:G * NE1].rearrange("p (g e) -> p e g", e=NE1)))
                link(nc.vector.tensor_tensor_scan(cum[:, :, :].rearrange("p e g -> p (e g)"), keep[:, :],
                                                  cnt[:, :, :].rearrange("p e g -> p (e g)"), 0.0, ALU.mult, ALU.add))
                steps = [P, NE1, G]
                link(nc.vector.tensor_tensor(big[:, :, 0:G], cum[:, :, G - 1:G].to_broadcast(steps),
                                             iota128[:, :].rearrange("p (o g) -> p o g", o=1).to_broadcast(steps), ALU.is_gt))
                link(nc.vector.tensor_reduce(ntile[:, :], big[:, :, 0:G], AX.X, ALU.add))
                link(nc.vector.memset(toff[:, :], 1.0))
                link(nc.vector.tensor_tensor_scan(tend[:, :], toff[:, :], ntile[:, :], 0.0, ALU.mult, ALU.add))
                link(nc.vector.tensor_tensor(toff[:, :], tend[:, :], ntile[:, :], ALU.subtract))
                link(nc.vector.tensor_scalar(toff[:, :], toff[:, :], float(P), None, ALU.mult))
                link(nc.vector.tensor_tensor(cum[:, :, :], cum[:, :, :], cnt[:, :, :], ALU.subtract))
                link(nc.vector.tensor_tensor(cum[:, :, :], cum[:, :, :], toff[:, :].rearrange("p (e o) -> p e o", o=1).to_broadcast(steps), ALU.add))
                link(nc.vector.tensor_tensor(pos[:, :, :], cum[:, :, :].rearrange("p e g -> p g e"),
                                             ps[:, 4, 0:G * NE1].rearrange("p (g e) -> p g e", e=NE1), ALU.add))
                link(nc.vector.tensor_tensor(pos[:, :, :], pos[:, :, :], hot[:, :, :], ALU.mult))
                link(nc.vector.tensor_reduce(slotf[:, :], pos[:, :, :], AX.X, ALU.add))
                nc.vector.tensor_tensor(slots[:, :], slotf[:, :], nottoken[:, :], ALU.add).then_inc(dve_slots, 1)
                dve.wait_ge(b12_in, 16)
                nc.vector.tensor_copy(b12p[:, 0, :], b12[:, :]).then_inc(dve_bparts, 1)
                dve.wait_ge(dve_bparts, 1)
                link(nc.vector.tensor_tensor(b12[:, :], b12[:, :], b12p[:, 0, :], ALU.subtract))
                nc.vector.tensor_copy(b12p[:, 1, :], b12[:, :]).then_inc(dve_bparts, 1)
                dve.wait_ge(dve_bparts, 2)
                nc.vector.tensor_tensor(b12p[:, 2, :], b12[:, :], b12p[:, 1, :], ALU.subtract).then_inc(dve_bparts, 1)
                pairs = [P, MT, NE1]
                which = big[:, :, :].rearrange("p a b -> p (a b)").rearrange("p (m e) -> p m e", e=NE1)
                link(nc.vector.tensor_tensor(which, tend[:, :].rearrange("p (o e) -> p o e", o=1).to_broadcast(pairs),
                                             ramp[:, :].rearrange("p (m o) -> p m o", o=1).to_broadcast(pairs), ALU.is_le))
                link(nc.vector.tensor_reduce(te[:, :], which, AX.X, ALU.add))
                nc.vector.tensor_scalar(tei[:, :], te[:, :], float(NE1 - 1), None, ALU.min).then_inc(dve_te, 1)
                dve.wait_ge(act_ex, 1)
                link(nc.vector.tensor_reduce(gate[:, :], lg[:, :, :], AX.X, ALU.add))
                link(nc.vector.reciprocal(gate[:, :], gate[:, :]))
                link(nc.vector.tensor_tensor(gate[:, :], gate[:, :], real[:, :], ALU.mult))

                def step(j, u, first):
                    dve.wait_ge(pe_hidT, j + 1)
                    if not first:
                        dve.wait_ge(pe_down, j - 1)
                    nc.vector.tensor_copy(hidT[:, u, :, :], ps[:, 4 + u, :].rearrange("p (f t) -> p f t", f=FC)).then_inc(dve_hidT, 1)
                    dve.wait_ge((tile_in0, tile_in1)[u], 8 * (j - u) + 16)
                    if not first:
                        dve.wait_ge(yo_out[u], 8 * (j - u))
                    nc.vector.tensor_scalar(dest[:, u:u + 1], xg[:, u, D:DW], -1.0, float(NOWHERE), ALU.mult, ALU.add).then_inc(dve_dest, 1)
                    dve.wait_ge(pe_down, j + 1)
                    nc.vector.tensor_copy(yo[:, u, :], ps[:, 6 + u, 0:D]).then_inc(dve_yo, 1)
                step(0, 0, True)
                step(1, 1, True)
                with dve.Fori(1, MT // 2) as i:
                    step(2 * i, 0, False)
                    step(2 * i + 1, 1, False)
                for t in range(G):
                    if t % NT == 0:
                        dve.wait_ge(yg_in[t // NT], 16)
                    nc.vector.scalar_tensor_tensor(out=Hs[:, t, :], in0=yg[:, t, :], scalar=gate[:, t:t + 1], in1=Hs[:, t, :],
                                                   op0=ALU.mult, op1=ALU.add).then_inc(dve_h3, 1)
                    if t:
                        dve.wait_ge(dve_h3, t)
                        nc.vector.bn_stats(lst[:, t - 1, :], Hs[:, t - 1, :]).then_inc(ln_chain, 1)
                dve.wait_ge(dve_h3, G)
                nc.vector.bn_stats(lst[:, G - 1, :], Hs[:, G - 1, :]).then_inc(ln_chain, 1)

            def causal():
                dve.wait_ge(dve_h3, G)
                layer_norm(1)
                dve.nop().then_inc(dve_h4, 1)
                dve.wait_ge(last_in, 16 * N_LAST)

                def project(b, first):
                    for t in range(4):
                        if t == 0 and not first:
                            dve.wait_ge(dve_h4, NT * b + 1)
                        dve.wait_ge(pe_qk4, 4 * b + t + 1)
                        nc.vector.tensor_scalar(QK4[:, t, 0:S], ps[:, t, :], bqk4[:, t:t + 1], None, ALU.add)
                        if t == 0 and not first:
                            nc.vector.bn_stats(lst[:, NT * b - 1, :], Hs[:, NT * b - 1, :]).then_inc(ln_chain, 1)
                    for t in range(4):
                        v = nc.vector.tensor_scalar(QK4[:, t, S:LT], ps[:, 4, P * t:P * (t + 1)], bqk4[:, t:t + 1], None, ALU.add)
                    v.then_inc(dve_qk4, 1)
                    dve.wait_ge(pe_v4, b + 1)
                    for i in range(NT):
                        v = nc.vector.tensor_tensor(V4[:, i, :], ps[:, 5 + i // 2, D * (i % 2):D * (i % 2 + 1)], bv4[:, :], ALU.add)
                    v.then_inc(dve_v4, 1)

                def attend(b):
                    def maxima(i):
                        dve.wait_ge(pe_s4, NT * b + i + 1)
                        row = ps[:, 2 * (i % 2):2 * (i % 2) + 2, :].rearrange("p b s -> p (b s)")
                        nc.vector.tensor_tensor(row[:, P * i:P * (i + 1)], row[:, P * i:P * (i + 1)], mask4[:, :],
                                                ALU.add).then_inc(dve_mask4, 1)
                        dve.wait_ge(dve_mask4, 2 * (NT * b + i) + 1)
                        nc.vector.tensor_reduce(nm4[:, i:i + 1], row[:, 0:P * (i + 1)], AX.X, ALU.max).then_inc(dve_mask4, 1)
                        dve.wait_ge(dve_mask4, 2 * (NT * b + i) + 2)
                        nc.vector.tensor_scalar(nm4[:, i:i + 1], nm4[:, i:i + 1], -float(D) ** -0.5, None, ALU.mult).then_inc(dve_nm4, 1)
                    maxima(0)
                    maxima(1)
                    for i in range(NT):
                        dve.wait_ge(pe_pt4, NT * b + i + 1)
                        if i >= 2:
                            dve.wait_ge(pe_pv4, NT * b + i - 1)
                        n = P * (i + 1)
                        nc.vector.tensor_copy(PT4[:, i % 2, 0:i + 1, :].rearrange("p j q -> p (j q)"),
                                              ps[:, 4:6, :].rearrange("p b s -> p (b s)")[:, 0:n]).then_inc(dve_pt4, 1)
                        if i + 2 < NT:
                            maxima(i + 2)
                        dve.wait_ge(pe_pv4, NT * b + i + 1)
                        if i:
                            dve.wait_ge(dve_h4, NT * b + i + 1)
                        nc.vector.reciprocal(rs4[:, i:i + 1], rs4[:, i:i + 1]).then_inc(dve_rs4, 1)
                        if i:
                            nc.vector.bn_stats(lst[:, NT * b + i - 1, :], Hs[:, NT * b + i - 1, :]).then_inc(ln_chain, 1)
                        dve.wait_ge(dve_rs4, NT * b + i + 1)
                        nc.vector.scalar_tensor_tensor(out=Hs[:, NT * b + i, :], in0=ps[:, 6 + i % 2, 0:D], scalar=rs4[:, i:i + 1],
                                                       in1=Hs[:, NT * b + i, :], op0=ALU.mult, op1=ALU.add).then_inc(dve_h4, 1)
                dve.nop().then_inc(dve_pt4, 1)
                project(0, True)
                with dve.Fori(0, NB - 1) as b:
                    attend(b)
                    project(b + 1, False)
                attend(NB - 1)
                dve.wait_ge(dve_h4, G + 1)
                nc.vector.bn_stats(lst[:, G - 1, :], Hs[:, G - 1, :]).then_inc(ln_chain, 1)

            def two_experts():
                n = [0]

                def link(ins):
                    n[0] += 1
                    ins.then_inc(c5, 1)
                    dve.wait_ge(c5, n[0])
                dve.wait_ge(dve_h4, G + 1)
                layer_norm(2)

                def rank(g, link):
                    tiles = bass.ds(TG * g, TG)
                    nc.vector.tensor_tensor(bm5[:, :, :], i8b[:, :, 0:2],
                                            nottoken5[:, tiles].rearrange("p (m o) -> p m o", o=1).to_broadcast([P, TG, 2]),
                                            ALU.add).then_inc(best_chain, 1)
                    link(4)
                    many = [P, 2 * TG, NE2]
                    nc.vector.tensor_tensor(hotb[:, :, :, :].rearrange("p m k e -> p (m k) e"),
                                            iota5[:, :].rearrange("p (o e) -> p o e", o=1).to_broadcast(many),
                                            bm5[:, :, :].rearrange("p m (k o) -> p (m k) o", o=1).to_broadcast(many),
                                            ALU.is_equal).then_inc(dve_hot5, 1)
                    dve.wait_ge(dve_hot5, g + 1)
                    nc.vector.tensor_reduce(hred[:, :, :].rearrange("p k e -> p (k e)"), hotb[:, :, :, :].rearrange("p m k e -> p (k e) m"),
                                            AX.X, ALU.add).then_inc(c5, 1)
                    nc.vector.tensor_copy(hot2[:, tiles, :], hotb[:, :, 1, :])
                    dve.wait_ge(pe_rank5, g + 1)
                    for m in range(TG):
                        for k in range(2):
                            ins = nc.vector.tensor_tensor_reduce(out=junk[:, m, k, :], in0=hotb[:, m, k, :],
                                                                 in1=ps[:, 3 + m // 2, D * (m % 2) + NE2 * k:D * (m % 2) + NE2 * (k + 1)],
                                                                 scale=1.0, scalar=0.0, op0=ALU.mult, op1=ALU.add,
                                                                 accum_out=locb[:, m, k:k + 1])
                    ins.then_inc(c5, 1)
                    dve.wait_ge(c5, 4 * g + 3)
                    nc.vector.tensor_tensor(hsum[:, :, :], hsum[:, :, :], hred[:, :, :], ALU.add).then_inc(c5, 1)
                    nc.vector.tensor_scalar(over5[:, :], locb[:, :, 0], float(CAP - 1), float(NOWHERE), ALU.is_gt, ALU.mult)
                    nc.vector.scalar_tensor_tensor(out=row5[:, :], in0=bm5[:, :, 0], scalar=float(CAP), in1=locb[:, :, 0],
                                                   op0=ALU.mult, op1=ALU.add).then_inc(c5, 1)
                    dve.wait_ge(c5, 4 * g + 5)
                    nc.vector.tensor_copy(loc[:, tiles, :], locb[:, :, :]).then_inc(dve_rank5, 1)
                    nc.vector.tensor_tensor(to5[:, 0, tiles], over5[:, :], row5[:, :], ALU.add).then_inc(dve_to5, 1)
                link(nc.vector.memset(hsum[:, :, :].rearrange("p k e -> p (k e)").bitcast(F32), 0.0))
                choose(1, NE2, lgb5, lg5, rank)
                n[0] += 4 * GG
                dve.wait_ge(dve_rank5, GG)
                dve.wait_ge(dve_to5, GG)
                flat = [P, G, NE2]
                dve.wait_ge(pe_count5, 1)
                link(nc.vector.tensor_copy(c1[:, :], ps[:, 5, 0:NE2]))
                link(nc.vector.tensor_tensor(hot2f[:, :, :], hot2[:, :, :], c1[:, :].rearrange("p (o e) -> p o e", o=1).to_broadcast(flat), ALU.mult))
                link(nc.vector.tensor_reduce(den[:, :], hot2f[:, :, :], AX.X, ALU.add))
                link(nc.vector.tensor_tensor(loc[:, :, 1], loc[:, :, 1], den[:, :], ALU.add))
                link(nc.vector.tensor_scalar(v5[:, :, :], loc[:, :, :], float(CAP), None, ALU.is_lt))
                link(nc.vector.scalar_tensor_tensor(out=rowf[:, :], in0=besti[:, :, 1], scalar=float(CAP), in1=loc[:, :, 1],
                                                    op0=ALU.mult, op1=ALU.add))
                link(nc.vector.tensor_tensor(rowf[:, :], rowf[:, :], nottoken5[:, :], ALU.add))
                link(nc.vector.scalar_tensor_tensor(out=rowf[:, :], in0=v5[:, :, 1], scalar=-float(NOWHERE), in1=rowf[:, :],
                                                    op0=ALU.mult, op1=ALU.add))
                nc.vector.tensor_scalar(to5[:, 1, :], rowf[:, :], float(NOWHERE), None, ALU.add).then_inc(dve_to5, 1)
                nc.vector.tensor_tensor(w5[:, :, :], best[:, :, :], best[:, :, 0:1].to_broadcast([P, G, 2]), ALU.subtract)
                link(nc.vector.tensor_tensor(lg5[:, :, :], lg5[:, :, :], best[:, :, 0:1].to_broadcast(flat), ALU.subtract))
                dve.nop().then_inc(dve_ex5, 1)
                dve.wait_ge(act_ex, 2)
                link(nc.vector.tensor_reduce(den[:, :], lg5[:, :, :], AX.X, ALU.add))
                link(nc.vector.reciprocal(den[:, :], den[:, :]))
                link(nc.vector.tensor_tensor(w5[:, :, :], w5[:, :, :], den[:, :].rearrange("p (g o) -> p g o", o=1).to_broadcast([P, G, 2]), ALU.mult))
                link(nc.vector.tensor_reduce(den[:, :], w5[:, :, :], AX.X, ALU.add))
                link(nc.vector.tensor_scalar(den[:, :], den[:, :], FEPS, None, ALU.max))
                link(nc.vector.reciprocal(den[:, :], den[:, :]))
                link(nc.vector.tensor_tensor(w5[:, :, :], w5[:, :, :], den[:, :].rearrange("p (g o) -> p g o", o=1).to_broadcast([P, G, 2]), ALU.mult))
                link(nc.vector.tensor_tensor(w5[:, :, :], w5[:, :, :], v5[:, :, :], ALU.mult))

                def step(j, u, place, first):
                    dve.wait_ge(pe_y5, j + 1)
                    for k in range(2):
                        ins = nc.vector.tensor_copy(yo5[CAP * k:CAP * (k + 1), place // GP, place % GP, :],
                                                    ps[CAP * k:CAP * (k + 1), 2 + u, D * k:D * (k + 1)])
                    ins.then_inc(dve_y5, 1)

                def group(g, u, first):
                    dve.wait_ge(tile5_in[u], 8 * (g - u) + 16)
                    if not first:
                        dve.wait_ge(y5_out[u], 8 * GP * (g - u))
                    nc.vector.tensor_scalar(dest5[:, u, :], xg5[:, u, :, D], -1.0, float(NOWHERE), ALU.mult, ALU.add).then_inc(dve_dest5, 1)
                    for m in range(GP):
                        step(GP * g + m, m % 2, GP * u + m, first)
                group(0, 0, True)
                group(1, 1, True)
                with dve.Fori(1, NP2 // GP // 2) as i:
                    group(2 * i, 0, False)
                    group(2 * i + 1, 1, False)
                for b in range(NB):
                    dve.wait_ge(yg_in[b], 16 + 32)
                    for k in range(2):
                        for t in range(NT * b, NT * (b + 1)):
                            if k:
                                dve.wait_ge(dve_h5, 2 * NT * b + t - NT * b + 1)
                            nc.vector.scalar_tensor_tensor(out=Hs[:, t, :], in0=yg5[:, k, t, :], scalar=w5[:, t, k:k + 1],
                                                           in1=Hs[:, t, :], op0=ALU.mult, op1=ALU.add).then_inc(dve_h5, 1)

            dve.wait_ge(act_acol, 1)
            nc.vector.tensor_scalar(acol[:, :], acol[:, :], -1.0, None, ALU.mult).then_inc(dve_init, 1)
            dve.wait_ge(consts_in, 16 * N_CONSTS)
            dve.wait_ge(txt_in, 16 * NB)
            dve.wait_ge(pool_init, 6)
            dve.nop().then_inc(dve_h2, 1)
            for _ in range(4):
                dve.nop().then_inc(dve_lo, 1)
            for _ in range(2):
                dve.nop().then_inc(dve_vals, 1)
            split(0)
            with dve.Fori(0, NB - 1) as b:
                attention(b)
                normalised(b)
                split(b + 1)
                scan(b)
            attention(NB - 1)
            normalised(NB - 1)
            scan(NB - 1)
            one_expert()
            causal()
            two_experts()


def layouts(x, txt, L0_tok_w_qkv, L0_tok_b_qkv, L0_tok_w_out, L0_tok_b_out, L0_attn_A_log, L0_attn_D_skip,
            L0_attn_dt_proj_w, L0_attn_dt_proj_b, L0_attn_x_proj_w, L0_ffn_router_w, L0_ffn_w1, L0_ffn_b1, L0_ffn_w2,
            L0_ffn_b2, L1_attn_Wq, L1_attn_bq, L1_attn_Wk, L1_attn_bk, L1_attn_Wv, L1_attn_bv, L1_ffn_wg, L1_ffn_we):
    import numpy as np

    def c(a):
        return np.ascontiguousarray(np.asarray(a))

    def ones_bf16(a):
        return (np.asarray(a) * 0x3F80).astype(np.uint16)

    def chunked(a):
        return c(np.asarray(a).reshape(-1, 128, a.shape[1]).transpose(1, 0, 2))

    def columns(v):
        return c(np.asarray(v).reshape(-1, 128).T)

    w = np.asarray(L0_tok_w_qkv).reshape(16, 3, 16, 256)
    bq = np.asarray(L0_tok_b_qkv).reshape(16, 3, 16)
    xp = np.asarray(L0_attn_x_proj_w)
    sel = np.zeros((96, 32, 128))
    for n in range(32):
        sel[n::32, n] = 1
    token = (np.arange(20) % 5 * 128 + np.arange(128)[:, None] < 589) * 1.0

    def rows(v):
        return np.tile(np.asarray(v, np.float32), (128, 1))
    sel3 = np.zeros((2, 64, 2, 17), np.float32)
    for head in range(2):
        for part in range(3):
            sel3[head, 17 * part:17 * (part + 1), head] = np.eye(17)
    sel3 = sel3.reshape(128, 34)
    return {
        "xT": c(np.asarray(x)[:, 0].transpose(0, 2, 1).reshape(4, 2, 128, 512).transpose(0, 2, 1, 3)),
        "txt": c(txt),
        "wqkvT": chunked(w.transpose(1, 0, 2, 3).reshape(768, 256).T),
        "bqk": columns(bq[:, 0:2].transpose(1, 0, 2).reshape(512)),
        "bv": c(bq[:, 2].reshape(256)),
        "woT": chunked(np.asarray(L0_tok_w_out).T),
        "bo": c(L0_tok_b_out),
        "ident": np.eye(128, dtype=np.float32),
        "ones3": ones_bf16(np.ones((3, 16, 512))),
        "xpwT": chunked(xp[:64].T),
        "xpbcT": chunked(np.concatenate([xp[64:]] * 3).T),
        "dtwT": c(np.asarray(L0_attn_dt_proj_w).T),
        "dtb": columns(L0_attn_dt_proj_b),
        "dsk": columns(L0_attn_D_skip),
        "alog": c(np.asarray(L0_attn_A_log).reshape(2, 128, 16).transpose(1, 0, 2).reshape(128, 32)),
        "sel3": sel3,
        "sel": ones_bf16(sel),
        "w1": c(np.asarray(L0_ffn_w1).reshape(14, 2, 128, 512).transpose(2, 0, 1, 3)),
        "w2": c(np.asarray(L0_ffn_w2).reshape(14, 4, 128, 256).transpose(2, 0, 1, 3)),
        "b12": c(np.concatenate([np.asarray(L0_ffn_b1), np.asarray(L0_ffn_b2)], 1)),
        "rw": chunked(np.asarray(L0_ffn_router_w)),
        "tri": ones_bf16(np.triu(np.ones((128, 128)), 1)),
        "onesm": ones_bf16(np.ones((128, 128))),
        "real": token.astype(np.float32),
        "nottoken": ((1 - token) * (1 << 20)).astype(np.float32),
        "iota1": rows(np.arange(14)),
        "iota128": rows(np.arange(20) * 128),
        "ramp": rows(np.arange((4 * 589 + 14 * 127) // 128)),
        "keep1": rows(np.arange(14 * 20) % 20 != 0),
        "w4T": chunked(np.concatenate([np.asarray(L1_attn_Wq), np.asarray(L1_attn_Wk), np.asarray(L1_attn_Wv)]).T),
        "bqk4": columns(np.concatenate([np.asarray(L1_attn_bq), np.asarray(L1_attn_bk)])),
        "bv4": c(L1_attn_bv),
        "mask4": np.triu(np.full((128, 128), -3e38, np.float32), 1),
        "wg": chunked(np.asarray(L1_ffn_wg)),
        "we": c(np.asarray(L1_ffn_we).reshape(128, 2, 128, 256).transpose(2, 0, 1, 3)),
        "tri5": ones_bf16(np.stack([np.triu(np.ones((128, 128)), 1), np.ones((128, 128))], 1)),
        "iota5": rows(np.arange(128)),
        "home5": c(((1 << 20) - (np.arange(2)[:, None] * 20 + np.arange(20)) * 128 - np.arange(128)[:, None, None]).astype(np.float32)),
        "ones3p": ones_bf16(np.ones((3, 128))),
    }


def kernel(**inputs):
    import numpy as _np
    import concourse.bacc as _bacc
    from concourse import mybir as _mybir
    from concourse.bass_utils import run_bass_kernel_spmd as _run

    nc = _bacc.Bacc("TRN2", target_bir_lowering=False, num_devices=1)
    arrays = layouts(**inputs)
    args = {n: nc.dram_tensor(f"in_{n}", a.shape, _mybir.dt.from_np(a.dtype), kind="ExternalInput").ap() for n, a in arrays.items()}
    out = nc.dram_tensor("out", (4, 589, 256), _mybir.dt.float32, kind="ExternalOutput").ap()
    fusion_kernel(nc, args, out)
    r = _run(nc, [{f"in_{n}": a for n, a in arrays.items()}], core_ids=[0])
    return r.results[0]["out"]
```
